# Optimizing a Trainium2 kernel written in Bass

```python
import numpy as np
import jax
import jax.numpy as jnp

def _softmax(x, axis=-1):
    return jax.nn.softmax(x, axis=axis)

def _gelu(x):
    return jax.nn.gelu(x, approximate=True)

def _silu(x):
    return jax.nn.silu(x)

def _sigmoid(x):
    return jax.nn.sigmoid(x)

def _layernorm(x, axis=-1, eps=1e-05):
    m = jnp.mean(x, axis=axis, keepdims=True)
    v = jnp.var(x, axis=axis, keepdims=True)
    return (x - m) / jnp.sqrt(v + eps)

def _scatter_add(tgt, idx, src, axis=0):
    return tgt.at[idx].add(src)

def _segment_sum(src, seg, n):
    return jax.ops.segment_sum(src, seg, n)
kernel_name = 'mk_decoder_preln_d2_seqx_r8_25a1ff'

def setup_inputs(seed: int=0):
    np.random.seed(seed)
    _w = jnp.asarray

    def _rec_inputs():
        import jax
        import jax.numpy as jnp
        _rk = jax.random.key(seed)
        x = -0.0005207 + 1.001 * jax.random.normal(jax.random.fold_in(_rk, 1), (16, 256, 128), jnp.float32)
        _lenS = 256 - jax.random.randint(jax.random.fold_in(_rk, 7), (16,), 0, max(1, 256 // 4) + 1, jnp.int32)
        _lenS2 = 64 - jax.random.randint(jax.random.fold_in(_rk, 8), (16,), 0, max(1, 64 // 4) + 1, jnp.int32)
        _ctx_1024P = jax.random.normal(jax.random.fold_in(_rk, 11), (16, 16, 128), jnp.float32)
        _ctx_1024c = jax.random.dirichlet(jax.random.fold_in(_rk, 511), 0.3 * jnp.ones((16,), jnp.float32), (16, 64))
        _ctx_1024t = jnp.einsum('bsk,bkd->bsd', _ctx_1024c, _ctx_1024P)
        _ctx_1024t = _ctx_1024t * jax.lax.rsqrt(jnp.mean(jnp.square(_ctx_1024t)) + 1e-12) * 0.953939
        ctx_1024 = -1.39393e-06 + 0.999914 * (_ctx_1024t + 0.3 * jax.random.normal(jax.random.fold_in(_rk, 611), (16, 64, 128), jnp.float32))
        itok_BxSx64_0_2047 = jax.random.randint(jax.random.fold_in(_rk, 12), (16, 256, 64), 0, 256, jnp.int32)
        _validS = jnp.arange(256)[None, :] < _lenS[:, None]
        _validS2 = jnp.arange(64)[None, :] < _lenS2[:, None]
        _causal = jnp.tril(jnp.ones((256, 256), dtype=bool))
        mask_Bx1xSxS2_fk1 = jnp.where(jnp.broadcast_to(_validS2[:, None, None, :], (16, 1, 256, 64)), 1.0, 0.0).astype(jnp.float32)
        return (x, ctx_1024, itok_BxSx64_0_2047, mask_Bx1xSxS2_fk1)
    x, ctx_1024, itok_BxSx64_0_2047, mask_Bx1xSxS2_fk1 = _rec_inputs()

    def _L0_attn_setup():
        import jax, jax.numpy as jnp
        import numpy as np
        S, B, D = (256, 2, 128)
        H, HD = (16, 64)
        SCALE = 1.0 / HD ** 0.5
        key = jax.random.key(seed)
        ks = jax.random.split(key, 7)
        std = 1.0 / np.sqrt(D)
        return {'inputs': jax.random.normal(ks[0], (S, B, D), dtype=jnp.float32), 'Wkv': jax.random.uniform(ks[1], (D, 2 * H * HD), jnp.float32, -std, std), 'bkv': jax.random.uniform(ks[2], (2 * H * HD,), jnp.float32, -std, std), 'Wq': jax.random.uniform(ks[3], (D, H * HD), jnp.float32, -std, std), 'bq': jax.random.uniform(ks[4], (H * HD,), jnp.float32, -std, std), 'Wp': jax.random.uniform(ks[5], (H * HD, D), jnp.float32, -std, std), 'bp': jax.random.uniform(ks[6], (D,), jnp.float32, -std, std)}
    _L0_attn_all = _L0_attn_setup()
    _L0_attn_in = {k: v for k, v in _L0_attn_all.items() if k in ('Wkv', 'bkv', 'Wq', 'bq', 'Wp', 'bp')}
    del _L0_attn_all

    def _L0_xattn_setup():
        import jax, jax.numpy as jnp
        import numpy as np
        B, NQ, NKV, K = (2, 128, 256, 64)
        D, H, LAT = (128, 16, 128)
        HD = D // H
        SCALE = 1.0 / np.sqrt(HD)
        key = jax.random.key(seed)
        ks = jax.random.split(key, 7)
        s = lambda fan_in: 1.0 / np.sqrt(fan_in)
        return {'x_q': jax.random.normal(ks[0], (B, NQ, D), jnp.float32), 'x_kv': jax.random.normal(ks[1], (B, NKV, D), jnp.float32), 'indices': jax.random.randint(ks[2], (B, NQ, K), 0, NKV), 'W_q': jax.random.normal(ks[3], (D, D), jnp.float32) * s(D), 'W_kv_down': jax.random.normal(ks[4], (LAT, D), jnp.float32) * s(D), 'W_kv_up': jax.random.normal(ks[5], (2 * D, LAT), jnp.float32) * s(LAT), 'W_out': jax.random.normal(ks[6], (D, D), jnp.float32) * s(D)}
    _L0_xattn_all = _L0_xattn_setup()
    _L0_xattn_in = {k: v for k, v in _L0_xattn_all.items() if k in ('W_q', 'W_kv_down', 'W_kv_up', 'W_out')}
    del _L0_xattn_all

    def _L0_ffn_setup():
        import jax, jax.numpy as jnp
        import numpy as np
        EPS = 1e-05
        LN_EPS = 1e-05
        NUM_EXPERTS = 8
        TOP_K = 2
        HIDDEN = 128
        INTER = 256

        def _swiglu(x, wg, wu, wd):
            return jax.nn.silu(x @ wg) * (x @ wu) @ wd
        key = jax.random.key(seed)
        ks = jax.random.split(key, 10)
        B, S, H, I, E = (8, 512, HIDDEN, INTER, NUM_EXPERTS)
        std_h = 1.0 / np.sqrt(H)
        std_i = 1.0 / np.sqrt(I)
        return {'x': jax.random.normal(ks[0], (B, S, H), dtype=jnp.float32), 'ln_scale': jnp.ones((H,), dtype=jnp.float32), 'ln_bias': jnp.zeros((H,), dtype=jnp.float32), 'gate_w': jax.random.normal(ks[1], (E, H), dtype=jnp.float32) * 0.01, 'Wg': jax.random.normal(ks[2], (E, H, I), dtype=jnp.float32) * std_h, 'Wu': jax.random.normal(ks[3], (E, H, I), dtype=jnp.float32) * std_h, 'Wd': jax.random.normal(ks[4], (E, I, H), dtype=jnp.float32) * std_i, 'sWg': jax.random.normal(ks[5], (H, I), dtype=jnp.float32) * std_h, 'sWu': jax.random.normal(ks[6], (H, I), dtype=jnp.float32) * std_h, 'sWd': jax.random.normal(ks[7], (I, H), dtype=jnp.float32) * std_i}
    _L0_ffn_all = _L0_ffn_setup()
    _L0_ffn_in = {k: v for k, v in _L0_ffn_all.items() if k in ('ln_scale', 'ln_bias', 'gate_w', 'Wg', 'Wu', 'Wd', 'sWg', 'sWu', 'sWd')}
    del _L0_ffn_all

    def _L1_attn_setup():
        import jax, jax.numpy as jnp
        import numpy as np
        D_MODEL = 128
        D_STATE = 64
        D_CONV = 4
        EXPAND = 2
        HEADDIM = 64
        D_INNER = EXPAND * D_MODEL
        NHEADS = D_INNER // HEADDIM
        CONV_DIM = D_INNER + 2 * D_STATE
        D_IN_PROJ = 2 * D_INNER + 2 * D_STATE + NHEADS
        BATCH, SEQLEN = (4, 256)
        DT_MIN, DT_MAX = (0.05, 1.0)
        EPS = 1e-05

        def _make_params(key, prefix):
            ks = jax.random.split(key, 5)
            p = {}
            p[prefix + 'in_w'] = jax.random.normal(ks[0], (D_IN_PROJ, D_MODEL), jnp.float32) * D_MODEL ** (-0.5)
            p[prefix + 'conv_w'] = jax.random.normal(ks[1], (CONV_DIM, D_CONV), jnp.float32) * D_CONV ** (-0.5)
            p[prefix + 'conv_b'] = jnp.zeros((CONV_DIM,), jnp.float32)
            u = jax.random.uniform(ks[2], (NHEADS,), jnp.float32)
            dt = jnp.exp(u * (np.log(DT_MAX) - np.log(DT_MIN)) + np.log(DT_MIN))
            p[prefix + 'dt_bias'] = dt + jnp.log(-jnp.expm1(-dt)) + 1.0
            p[prefix + 'A_log'] = jnp.log(jax.random.uniform(ks[3], (NHEADS,), jnp.float32, minval=1.0, maxval=16.0))
            p[prefix + 'Dp'] = jnp.ones((NHEADS,), jnp.float32)
            p[prefix + 'norm_w'] = jnp.ones((D_INNER,), jnp.float32)
            p[prefix + 'out_w'] = jax.random.normal(ks[4], (D_MODEL, D_INNER), jnp.float32) * D_INNER ** (-0.5)
            return p

        def _dconv(x, w, b):
            xt = x.transpose(0, 2, 1)
            out = jax.lax.conv_general_dilated(xt, w[:, None, :], (1,), [(D_CONV - 1, 0)], feature_group_count=CONV_DIM)
            return (out + b[:, None]).transpose(0, 2, 1)

        def _ssd(dt, A, xh, Bm, Cm):
            dA = jnp.exp(dt * A)

            def step(S, inp):
                dA_t, dt_t, x_t, B_t, C_t = inp
                S = S * dA_t[:, :, None, None] + (dt_t[:, :, None] * x_t)[..., None] * B_t[:, None, None, :]
                y = jnp.einsum('bhpn,bn->bhp', S, C_t)
                return (S, y)
            S0 = jnp.zeros((dt.shape[0], NHEADS, HEADDIM, D_STATE), dt.dtype)
            xs = (dA.swapaxes(0, 1), dt.swapaxes(0, 1), xh.swapaxes(0, 1), Bm.swapaxes(0, 1), Cm.swapaxes(0, 1))
            _, ys = jax.lax.scan(step, S0, xs)
            return ys.swapaxes(0, 1)

        def _mamba2(x, in_w, conv_w, conv_b, dt_bias, A_log, Dp, norm_w, out_w):
            Bsz, L, _ = x.shape
            zxbcdt = x @ in_w.T
            z = zxbcdt[..., :D_INNER]
            xBC = zxbcdt[..., D_INNER:D_INNER + CONV_DIM]
            dt = jax.nn.softplus(zxbcdt[..., D_INNER + CONV_DIM:] + dt_bias)
            xBC = jax.nn.silu(_dconv(xBC, conv_w, conv_b))
            xh = xBC[..., :D_INNER].reshape(Bsz, L, NHEADS, HEADDIM)
            Bm = xBC[..., D_INNER:D_INNER + D_STATE]
            Cm = xBC[..., D_INNER + D_STATE:]
            A = -jnp.exp(A_log)
            y = _ssd(dt, A, xh, Bm, Cm) + Dp[None, None, :, None] * xh
            y = y.reshape(Bsz, L, D_INNER) * jax.nn.silu(z)
            y = y * jax.lax.rsqrt(jnp.mean(y * y, -1, keepdims=True) + EPS) * norm_w
            return y @ out_w.T
        key = jax.random.key(seed)
        k1, k2, k3 = jax.random.split(key, 3)
        inp = {'x': jax.random.normal(k1, (BATCH, SEQLEN, D_MODEL), jnp.float32)}
        inp.update(_make_params(k2, 'f_'))
        inp.update(_make_params(k3, 'b_'))
        return inp
    _L1_attn_all = _L1_attn_setup()
    _L1_attn_in = {k: v for k, v in _L1_attn_all.items() if k in ('f_in_w', 'f_conv_w', 'f_conv_b', 'f_dt_bias', 'f_A_log', 'f_Dp', 'f_norm_w', 'f_out_w', 'b_in_w', 'b_conv_w', 'b_conv_b', 'b_dt_bias', 'b_A_log', 'b_Dp', 'b_norm_w', 'b_out_w')}
    del _L1_attn_all

    def _L1_xattn_setup():
        import jax, jax.numpy as jnp
        import numpy as np
        B, S, D = (2, 256, 128)
        H, DK = (16, 64)

        def _split_heads(t):
            b, s, _ = t.shape
            return t.reshape(b, s, H, DK).transpose(0, 2, 1, 3)
        key = jax.random.key(seed)
        ks = jax.random.split(key, 6)
        x = jax.random.normal(ks[0], (B, S, D), dtype=jnp.float32)
        y = jax.random.normal(ks[1], (B, S, D), dtype=jnp.float32)
        mask = jnp.triu(jnp.ones((S, S), jnp.float32), k=1)[None, None, :, :]
        mask = jnp.broadcast_to(mask, (B, 1, S, S))
        glorot = lambda k, shape: jax.random.uniform(k, shape, jnp.float32, -1.0, 1.0) * np.sqrt(6.0 / (shape[0] + shape[1]))
        W_q = glorot(ks[2], (D, H * DK))
        W_k = glorot(ks[3], (D, H * DK))
        W_v = glorot(ks[4], (D, H * DK))
        W_o = glorot(ks[5], (H * DK, D))
        return {'x': x, 'y': y, 'mask': mask, 'W_q': W_q, 'W_k': W_k, 'W_v': W_v, 'W_o': W_o}
    _L1_xattn_all = _L1_xattn_setup()
    _L1_xattn_in = {k: v for k, v in _L1_xattn_all.items() if k in ('W_q', 'W_k', 'W_v', 'W_o')}
    del _L1_xattn_all

    def _L1_ffn_setup():
        import jax, jax.numpy as jnp
        import numpy as np
        THRESHOLD = 0.1
        key = jax.random.key(seed)
        k1, k2, k3 = jax.random.split(key, 3)
        B, S, D, E = (4, 512, 128, 8)
        inputs = jax.random.normal(k1, (B, S, D), dtype=jnp.float32)
        gate_w = jax.random.normal(k2, (D, E), dtype=jnp.float32) * 0.02
        gate_b = jnp.zeros((E,), dtype=jnp.float32)
        expert_w = jax.random.normal(k3, (E, D, D), dtype=jnp.float32) * 0.02
        expert_b = jnp.zeros((E, D), dtype=jnp.float32)
        return {'inputs': inputs, 'gate_w': gate_w, 'gate_b': gate_b, 'expert_w': expert_w, 'expert_b': expert_b}
    _L1_ffn_all = _L1_ffn_setup()
    _L1_ffn_in = {k: v for k, v in _L1_ffn_all.items() if k in ('gate_w', 'gate_b', 'expert_w', 'expert_b')}
    del _L1_ffn_all
    return {'x': x, 'ctx_1024': ctx_1024, 'itok_BxSx64_0_2047': itok_BxSx64_0_2047, 'mask_Bx1xSxS2_fk1': mask_Bx1xSxS2_fk1, 'L0_attn_Wkv': _L0_attn_in['Wkv'], 'L0_attn_bkv': _L0_attn_in['bkv'], 'L0_attn_Wq': _L0_attn_in['Wq'], 'L0_attn_bq': _L0_attn_in['bq'], 'L0_attn_Wp': _L0_attn_in['Wp'], 'L0_attn_bp': _L0_attn_in['bp'], 'L0_xattn_W_q': _L0_xattn_in['W_q'], 'L0_xattn_W_kv_down': _L0_xattn_in['W_kv_down'], 'L0_xattn_W_kv_up': _L0_xattn_in['W_kv_up'], 'L0_xattn_W_out': _L0_xattn_in['W_out'], 'L0_ffn_ln_scale': _L0_ffn_in['ln_scale'], 'L0_ffn_ln_bias': _L0_ffn_in['ln_bias'], 'L0_ffn_gate_w': _L0_ffn_in['gate_w'], 'L0_ffn_Wg': _L0_ffn_in['Wg'], 'L0_ffn_Wu': _L0_ffn_in['Wu'], 'L0_ffn_Wd': _L0_ffn_in['Wd'], 'L0_ffn_sWg': _L0_ffn_in['sWg'], 'L0_ffn_sWu': _L0_ffn_in['sWu'], 'L0_ffn_sWd': _L0_ffn_in['sWd'], 'L1_attn_f_in_w': _L1_attn_in['f_in_w'], 'L1_attn_f_conv_w': _L1_attn_in['f_conv_w'], 'L1_attn_f_conv_b': _L1_attn_in['f_conv_b'], 'L1_attn_f_dt_bias': _L1_attn_in['f_dt_bias'], 'L1_attn_f_A_log': _L1_attn_in['f_A_log'], 'L1_attn_f_Dp': _L1_attn_in['f_Dp'], 'L1_attn_f_norm_w': _L1_attn_in['f_norm_w'], 'L1_attn_f_out_w': _L1_attn_in['f_out_w'], 'L1_attn_b_in_w': _L1_attn_in['b_in_w'], 'L1_attn_b_conv_w': _L1_attn_in['b_conv_w'], 'L1_attn_b_conv_b': _L1_attn_in['b_conv_b'], 'L1_attn_b_dt_bias': _L1_attn_in['b_dt_bias'], 'L1_attn_b_A_log': _L1_attn_in['b_A_log'], 'L1_attn_b_Dp': _L1_attn_in['b_Dp'], 'L1_attn_b_norm_w': _L1_attn_in['b_norm_w'], 'L1_attn_b_out_w': _L1_attn_in['b_out_w'], 'L1_xattn_W_q': _L1_xattn_in['W_q'], 'L1_xattn_W_k': _L1_xattn_in['W_k'], 'L1_xattn_W_v': _L1_xattn_in['W_v'], 'L1_xattn_W_o': _L1_xattn_in['W_o'], 'L1_ffn_gate_w': _L1_ffn_in['gate_w'], 'L1_ffn_gate_b': _L1_ffn_in['gate_b'], 'L1_ffn_expert_w': _L1_ffn_in['expert_w'], 'L1_ffn_expert_b': _L1_ffn_in['expert_b']}

def reference(x, ctx_1024, itok_BxSx64_0_2047, mask_Bx1xSxS2_fk1, L0_attn_Wkv, L0_attn_bkv, L0_attn_Wq, L0_attn_bq, L0_attn_Wp, L0_attn_bp, L0_xattn_W_q, L0_xattn_W_kv_down, L0_xattn_W_kv_up, L0_xattn_W_out, L0_ffn_ln_scale, L0_ffn_ln_bias, L0_ffn_gate_w, L0_ffn_Wg, L0_ffn_Wu, L0_ffn_Wd, L0_ffn_sWg, L0_ffn_sWu, L0_ffn_sWd, L1_attn_f_in_w, L1_attn_f_conv_w, L1_attn_f_conv_b, L1_attn_f_dt_bias, L1_attn_f_A_log, L1_attn_f_Dp, L1_attn_f_norm_w, L1_attn_f_out_w, L1_attn_b_in_w, L1_attn_b_conv_w, L1_attn_b_conv_b, L1_attn_b_dt_bias, L1_attn_b_A_log, L1_attn_b_Dp, L1_attn_b_norm_w, L1_attn_b_out_w, L1_xattn_W_q, L1_xattn_W_k, L1_xattn_W_v, L1_xattn_W_o, L1_ffn_gate_w, L1_ffn_gate_b, L1_ffn_expert_w, L1_ffn_expert_b):
    import jax
    import jax.numpy as jnp

    def _L0_attn_ref(inputs, Wkv, bkv, Wq, bq, Wp, bp):
        import jax, jax.numpy as jnp
        import numpy as np
        S, B, D = (256, 2, 128)
        H, HD = (16, 64)
        SCALE = 1.0 / HD ** 0.5
        s, b, _ = inputs.shape
        kv = inputs @ Wkv + bkv
        k, v = jnp.split(kv, 2, axis=-1)
        q = inputs @ Wq + bq
        k = k.reshape(s, b, H, HD)
        q = q.reshape(s, b, H, HD)
        v = v.reshape(s, b, H, HD)
        attn = jnp.einsum('sbhd,tbhd->bhst', q, k) * SCALE
        attn = jax.nn.softmax(attn, axis=-1)
        attn_vec = jnp.einsum('bhst,tbhd->sbhd', attn, v)
        attn_vec = attn_vec.reshape(s, b, H * HD)
        return attn_vec @ Wp + bp

    def _L0_xattn_ref(x_q, x_kv, indices, W_q, W_kv_down, W_kv_up, W_out):
        import jax, jax.numpy as jnp
        import numpy as np
        B, NQ, NKV, K = (2, 128, 256, 64)
        D, H, LAT = (128, 16, 128)
        HD = D // H
        SCALE = 1.0 / np.sqrt(HD)
        b, nq, d = x_q.shape
        q = (x_q @ W_q.T).reshape(b, nq, H, HD)
        c_kv = x_kv @ W_kv_down.T
        c_sel = c_kv[jnp.arange(b)[:, None, None], indices]
        kv = (c_sel @ W_kv_up.T).reshape(b, nq, K, 2, H, HD)
        k = kv[:, :, :, 0]
        v = kv[:, :, :, 1]
        scores = jnp.einsum('bqhd,bqkhd->bqkh', q, k) * SCALE
        attn = jax.nn.softmax(scores, axis=2)
        out = jnp.einsum('bqkh,bqkhd->bqhd', attn, v).reshape(b, nq, d)
        return out @ W_out.T

    def _L0_ffn_ref(x, ln_scale, ln_bias, gate_w, Wg, Wu, Wd, sWg, sWu, sWd):
        import jax, jax.numpy as jnp
        import numpy as np
        EPS = 1e-05
        LN_EPS = 1e-05
        NUM_EXPERTS = 8
        TOP_K = 2
        HIDDEN = 128
        INTER = 256

        def _swiglu(x, wg, wu, wd):
            return jax.nn.silu(x @ wg) * (x @ wu) @ wd
        B, S, H = x.shape
        xf = x.reshape(-1, H)
        mu = jnp.mean(xf, axis=-1, keepdims=True)
        var = jnp.var(xf, axis=-1, keepdims=True)
        xn = (xf - mu) * jax.lax.rsqrt(var + LN_EPS) * ln_scale + ln_bias
        logits = xn @ gate_w.T
        probs = jax.nn.softmax(logits, axis=-1)
        tk_probs, tk_idx = jax.lax.top_k(probs, TOP_K)
        tk_probs = tk_probs / (jnp.sum(tk_probs, axis=-1, keepdims=True) + EPS)
        onehot = tk_idx[..., None] == jnp.arange(NUM_EXPERTS)[None, None, :]
        w = jnp.sum(tk_probs[..., None] * onehot.astype(tk_probs.dtype), axis=1)
        out = _swiglu(xf, sWg, sWu, sWd)
        for e in range(NUM_EXPERTS):
            out = out + w[:, e:e + 1] * _swiglu(xf, Wg[e], Wu[e], Wd[e])
        return out.reshape(B, S, H)

    def _L1_attn_ref(x, f_in_w, f_conv_w, f_conv_b, f_dt_bias, f_A_log, f_Dp, f_norm_w, f_out_w, b_in_w, b_conv_w, b_conv_b, b_dt_bias, b_A_log, b_Dp, b_norm_w, b_out_w):
        import jax, jax.numpy as jnp
        import numpy as np
        D_MODEL = 128
        D_STATE = 64
        D_CONV = 4
        EXPAND = 2
        HEADDIM = 64
        D_INNER = EXPAND * D_MODEL
        NHEADS = D_INNER // HEADDIM
        CONV_DIM = D_INNER + 2 * D_STATE
        D_IN_PROJ = 2 * D_INNER + 2 * D_STATE + NHEADS
        BATCH, SEQLEN = (4, 256)
        DT_MIN, DT_MAX = (0.05, 1.0)
        EPS = 1e-05

        def _make_params(key, prefix):
            ks = jax.random.split(key, 5)
            p = {}
            p[prefix + 'in_w'] = jax.random.normal(ks[0], (D_IN_PROJ, D_MODEL), jnp.float32) * D_MODEL ** (-0.5)
            p[prefix + 'conv_w'] = jax.random.normal(ks[1], (CONV_DIM, D_CONV), jnp.float32) * D_CONV ** (-0.5)
            p[prefix + 'conv_b'] = jnp.zeros((CONV_DIM,), jnp.float32)
            u = jax.random.uniform(ks[2], (NHEADS,), jnp.float32)
            dt = jnp.exp(u * (np.log(DT_MAX) - np.log(DT_MIN)) + np.log(DT_MIN))
            p[prefix + 'dt_bias'] = dt + jnp.log(-jnp.expm1(-dt)) + 1.0
            p[prefix + 'A_log'] = jnp.log(jax.random.uniform(ks[3], (NHEADS,), jnp.float32, minval=1.0, maxval=16.0))
            p[prefix + 'Dp'] = jnp.ones((NHEADS,), jnp.float32)
            p[prefix + 'norm_w'] = jnp.ones((D_INNER,), jnp.float32)
            p[prefix + 'out_w'] = jax.random.normal(ks[4], (D_MODEL, D_INNER), jnp.float32) * D_INNER ** (-0.5)
            return p

        def _dconv(x, w, b):
            xt = x.transpose(0, 2, 1)
            out = jax.lax.conv_general_dilated(xt, w[:, None, :], (1,), [(D_CONV - 1, 0)], feature_group_count=CONV_DIM)
            return (out + b[:, None]).transpose(0, 2, 1)

        def _ssd(dt, A, xh, Bm, Cm):
            dA = jnp.exp(dt * A)

            def step(S, inp):
                dA_t, dt_t, x_t, B_t, C_t = inp
                S = S * dA_t[:, :, None, None] + (dt_t[:, :, None] * x_t)[..., None] * B_t[:, None, None, :]
                y = jnp.einsum('bhpn,bn->bhp', S, C_t)
                return (S, y)
            S0 = jnp.zeros((dt.shape[0], NHEADS, HEADDIM, D_STATE), dt.dtype)
            xs = (dA.swapaxes(0, 1), dt.swapaxes(0, 1), xh.swapaxes(0, 1), Bm.swapaxes(0, 1), Cm.swapaxes(0, 1))
            _, ys = jax.lax.scan(step, S0, xs)
            return ys.swapaxes(0, 1)

        def _mamba2(x, in_w, conv_w, conv_b, dt_bias, A_log, Dp, norm_w, out_w):
            Bsz, L, _ = x.shape
            zxbcdt = x @ in_w.T
            z = zxbcdt[..., :D_INNER]
            xBC = zxbcdt[..., D_INNER:D_INNER + CONV_DIM]
            dt = jax.nn.softplus(zxbcdt[..., D_INNER + CONV_DIM:] + dt_bias)
            xBC = jax.nn.silu(_dconv(xBC, conv_w, conv_b))
            xh = xBC[..., :D_INNER].reshape(Bsz, L, NHEADS, HEADDIM)
            Bm = xBC[..., D_INNER:D_INNER + D_STATE]
            Cm = xBC[..., D_INNER + D_STATE:]
            A = -jnp.exp(A_log)
            y = _ssd(dt, A, xh, Bm, Cm) + Dp[None, None, :, None] * xh
            y = y.reshape(Bsz, L, D_INNER) * jax.nn.silu(z)
            y = y * jax.lax.rsqrt(jnp.mean(y * y, -1, keepdims=True) + EPS) * norm_w
            return y @ out_w.T
        out_fwd = _mamba2(x, f_in_w, f_conv_w, f_conv_b, f_dt_bias, f_A_log, f_Dp, f_norm_w, f_out_w)
        x_rev = jnp.flip(x, 1)
        out_bwd = _mamba2(x_rev, b_in_w, b_conv_w, b_conv_b, b_dt_bias, b_A_log, b_Dp, b_norm_w, b_out_w)
        return out_fwd + jnp.flip(out_bwd, 1)

    def _L1_xattn_ref(x, y, mask, W_q, W_k, W_v, W_o):
        import jax, jax.numpy as jnp
        import numpy as np
        B, S, D = (2, 256, 128)
        H, DK = (16, 64)

        def _split_heads(t):
            b, s, _ = t.shape
            return t.reshape(b, s, H, DK).transpose(0, 2, 1, 3)
        Q = _split_heads(x @ W_q)
        K = _split_heads(y @ W_k)
        V = _split_heads(y @ W_v)
        E = jnp.einsum('bhqd,bhkd->bhqk', Q, K) / jnp.sqrt(jnp.float32(DK))
        if mask is not None:
            E = E + mask * -1000000000.0
        A = jax.nn.softmax(E, axis=-1)
        M = jnp.einsum('bhqk,bhkd->bhqd', A, V)
        M = M.transpose(0, 2, 1, 3).reshape(x.shape[0], -1, H * DK)
        return M @ W_o

    def _L1_ffn_ref(inputs, gate_w, gate_b, expert_w, expert_b):
        import jax, jax.numpy as jnp
        import numpy as np
        THRESHOLD = 0.1
        d = inputs.shape[-1]
        x = inputs.reshape(-1, d)
        gate_logits = jax.nn.softmax(x @ gate_w + gate_b, axis=-1)
        selected = (gate_logits >= THRESHOLD).astype(x.dtype)
        weights = gate_logits * selected
        wsum = jnp.sum(weights, axis=-1, keepdims=True)
        weights = weights / jnp.where(wsum == 0, jnp.ones_like(wsum), wsum)
        E = expert_w.shape[0]
        out = jnp.zeros((x.shape[0], expert_w.shape[-1]), dtype=x.dtype)
        for e in range(E):
            out = out + weights[:, e:e + 1] * (x @ expert_w[e] + expert_b[e])
        return out.reshape(*inputs.shape[:-1], out.shape[-1])
    x = x + _L0_attn_ref(_layernorm(x, axis=-1), L0_attn_Wkv, L0_attn_bkv, L0_attn_Wq, L0_attn_bq, L0_attn_Wp, L0_attn_bp)
    x = x + _L0_xattn_ref(_layernorm(x, axis=-1), ctx_1024, itok_BxSx64_0_2047, L0_xattn_W_q, L0_xattn_W_kv_down, L0_xattn_W_kv_up, L0_xattn_W_out)
    x = x + _L0_ffn_ref(_layernorm(x, axis=-1), L0_ffn_ln_scale, L0_ffn_ln_bias, L0_ffn_gate_w, L0_ffn_Wg, L0_ffn_Wu, L0_ffn_Wd, L0_ffn_sWg, L0_ffn_sWu, L0_ffn_sWd)
    x = x + _L1_attn_ref(_layernorm(x, axis=-1), L1_attn_f_in_w, L1_attn_f_conv_w, L1_attn_f_conv_b, L1_attn_f_dt_bias, L1_attn_f_A_log, L1_attn_f_Dp, L1_attn_f_norm_w, L1_attn_f_out_w, L1_attn_b_in_w, L1_attn_b_conv_w, L1_attn_b_conv_b, L1_attn_b_dt_bias, L1_attn_b_A_log, L1_attn_b_Dp, L1_attn_b_norm_w, L1_attn_b_out_w)
    x = x + _L1_xattn_ref(_layernorm(x, axis=-1), ctx_1024, mask_Bx1xSxS2_fk1, L1_xattn_W_q, L1_xattn_W_k, L1_xattn_W_v, L1_xattn_W_o)
    x = x + _L1_ffn_ref(_layernorm(x, axis=-1), L1_ffn_gate_w, L1_ffn_gate_b, L1_ffn_expert_w, L1_ffn_expert_b)
    return x

_drawn_inputs = setup_inputs


def setup_inputs(seed=0):
    import zlib

    import numpy as np

    out = dict(_drawn_inputs(seed))
    spreads = {'L0_ffn_ln_scale': (1.0, 0.2),
     'L0_ffn_ln_bias': (0.0, 0.1),
     'L1_attn_f_conv_b': (0.0, 0.1),
     'L1_attn_f_Dp': (1.0, 0.2),
     'L1_attn_f_norm_w': (1.0, 0.2),
     'L1_attn_b_conv_b': (0.0, 0.1),
     'L1_attn_b_Dp': (1.0, 0.2),
     'L1_attn_b_norm_w': (1.0, 0.2),
     'L1_ffn_gate_b': (0.0, 0.734),
     'L1_ffn_expert_b': (0.0, 0.423)}
    factors = {'L1_attn_f_A_log': 23.616, 'L1_xattn_W_q': 2.884, 'L1_xattn_W_k': 2.867}
    for name, (base, spread) in spreads.items():
        noise = np.random.default_rng([zlib.crc32(name.encode()), seed]).standard_normal(out[name].shape)
        drawn = base * np.exp(spread * noise) if base else spread * noise
        out[name] = jnp.asarray(drawn.astype(out[name].dtype))
    for name, factor in factors.items():
        out[name] = (out[name] * factor).astype(out[name].dtype)
    return out
```

```python
from contextlib import ExitStack

import concourse.bass as bass
from concourse import mybir

F32 = mybir.dt.float32
I32 = mybir.dt.int32
BF16 = mybir.dt.bfloat16
ALU = mybir.AluOpType
ACT = mybir.ActivationFunctionType
AX = mybir.AxisListType.X

P = 128
B, S, D = 16, 256, 128
TOK = B * S
NT = TOK // P
SUP = 4
NSUP = NT // SUP
EPS = 1e-5


class Scope:

    def __init__(self, nc, stack, prefix):
        self.nc, self.stack, self.prefix = nc, stack, prefix
        self.sems = []
        stack.callback(self.wipe)

    def sb(self, name, shape, dt=F32):
        return self.stack.enter_context(self.nc.sbuf_tensor(f"{self.prefix}_{name}", shape, dt))

    def ps(self, name, shape, dt=F32):
        return self.stack.enter_context(self.nc.psum_tensor(f"{self.prefix}_{name}", shape, dt))

    def sem(self, name):
        self.sems.append(self.nc.alloc_semaphore(f"{self.prefix}_{name}"))
        return self.sems[-1]

    def wipe(self):
        if self.sems:
            self.nc.clear_and_free_semaphores(self.sems)
            self.nc.all_engine_barrier()


def bcast(ap, n, where):
    return ap.unsqueeze(where).to_broadcast(list(ap.shape[:where]) + [n] + list(ap.shape[where:]))


class Norm:

    def __init__(self, m):
        self.stats = m.sb("stats", [P, NT, 6])
        self.tmp = m.sb("tmp", [P, 8, NT])
        self.mean = m.sb("mean", [P, NT])
        self.rstd = m.sb("rstd", [P, NT])
        self.counted = m.sem("stats_counted")
        self.var_ready = m.sem("var_ready")
        self.std_ready = m.sem("std_ready")
        self.done = m.sem("norm_done")

    def dve(self, dve, x):
        st, tmp = self.stats, self.tmp
        with dve.Fori(0, NT) as t:
            dve.bn_stats(st[:, t, :], x[:, t, :]).then_inc(self.counted, 1)
        dve.wait_ge(self.counted, NT)
        me, mo, ve, vo = st[:, :, 1], st[:, :, 4], st[:, :, 2], st[:, :, 5]
        dve.tensor_tensor(tmp[:, 0, :], me, mo, ALU.add).then_inc(self.counted, 1)
        dve.tensor_tensor(tmp[:, 1, :], me, mo, ALU.subtract).then_inc(self.counted, 1)
        dve.tensor_tensor(tmp[:, 2, :], ve, vo, ALU.add).then_inc(self.counted, 1)
        dve.wait_ge(self.counted, NT + 3)
        dve.tensor_scalar(self.mean[:, :], tmp[:, 0, :], 0.5, None, ALU.mult).then_inc(self.counted, 1)
        dve.tensor_scalar(tmp[:, 3, :], tmp[:, 1, :], 0.5, None, ALU.mult).then_inc(self.counted, 1)
        dve.tensor_scalar(tmp[:, 4, :], tmp[:, 2, :], 1.0 / D, EPS, ALU.mult, ALU.add).then_inc(self.counted, 1)
        dve.wait_ge(self.counted, NT + 6)
        dve.tensor_tensor(tmp[:, 5, :], tmp[:, 3, :], tmp[:, 3, :], ALU.mult).then_inc(self.counted, 1)
        dve.wait_ge(self.counted, NT + 7)
        dve.tensor_tensor(tmp[:, 6, :], tmp[:, 5, :], tmp[:, 4, :], ALU.add).then_inc(self.var_ready, 1)
        dve.wait_ge(self.std_ready, 1)
        dve.reciprocal(self.rstd[:, :], tmp[:, 7, :]).then_inc(self.done, 1)
        dve.wait_ge(self.done, 1)

    def act(self, act):
        act.wait_ge(self.var_ready, 1)
        act.activation(self.tmp[:, 7, :], self.tmp[:, 6, :], ACT.Sqrt).then_inc(self.std_ready, 1)

    def tile(self, dve, out, x, t):
        return dve.tensor_scalar(out, x[:, t, :], self.mean[:, bass.ds(t, 1)], self.rstd[:, bass.ds(t, 1)],
                                 ALU.subtract, ALU.mult)


def load_x(nc, x, ident, x_dram, ident_dram):
    with ExitStack() as stack:
        m = Scope(nc, stack, "lx")
        loaded = m.sem("loaded")
        with nc.Block() as block:

            @block.sync
            def _(sp):
                for u in range(2):
                    sp.dma_start(x[:, B * u : B * u + B, :],
                                 x_dram[P * B * u : P * B * (u + 1), :].rearrange("(p b) d -> p b d", b=B)).then_inc(loaded, 16)
                sp.dma_start(ident[:, :], ident_dram).then_inc(loaded, 16)
                sp.wait_ge(loaded, 48)


def store_x(nc, x, out_dram):
    with ExitStack() as stack:
        m = Scope(nc, stack, "st")
        stored = m.sem("stored")
        with nc.Block() as block:

            @block.sync
            def _(sp):
                for u in range(2):
                    sp.dma_start(out_dram.rearrange("b (u p) d -> u p b d", u=2)[u], x[:, B * u : B * u + B, :]).then_inc(stored, 16)
                sp.wait_ge(stored, 32)


def self_attention(nc, x_dram, ident_dram, mask_dram, wq_dram, wkv_dram, bq_dram, bk_dram, bv_dram, wp_dram, bp_dram, out_dram):
    H, HD = 16, 64
    HP = H // 2
    SCALE = 1.0 / HD**0.5
    Q = 32
    NB = P // Q
    NQKV = 2 * HP + 2 * SUP
    with ExitStack() as stack:
        m = Scope(nc, stack, "sa")
        x = m.sb("x", [P, NT, D])
        ident = m.sb("ident", [P, P])
        mask = m.sb("mask", [P, Q])
        wq = m.sb("wq", [P, H * HD])
        wkv = m.sb("wkv", [P, 2 * H * HD])
        bq = m.sb("bq", [P, HP])
        bk = m.sb("bk", [P, HP])
        bv = m.sb("bv", [P, HP])
        wp = m.sb("wp", [P, HP, D])
        bp = m.sb("bp", [1, D])
        one = m.sb("one", [1, P])
        crow = m.sb("crow", [1, D])
        norm = Norm(m)
        xn = m.sb("xn", [P, 2, SUP, D])
        xnT = m.sb("xnT", [P, SUP * P])
        qT = m.sb("qT", [P, HP, SUP * P])
        kT = m.sb("kT", [P, HP, SUP * P])
        v = m.sb("v", [P, SUP, H * HD])
        logits = m.sb("logits", [P, 2, H, Q])
        shifted = m.sb("shifted", [P, 2, H, Q])
        probs = m.sb("probs", [P, 2, H, Q])
        normed = m.sb("normed", [P, 2, H, Q])
        rowmax = m.sb("rowmax", [P, 2, H])
        rowsum = m.sb("rowsum", [P, 2, H])
        rinv = m.sb("rinv", [P, 2, H])
        probsT = m.sb("probsT", [P, 2, H, P])
        oT = m.sb("oT", [P, 2, HP, P])

        ps_q = [m.ps(f"ps_q{n}", [P, 512]) for n in range(2)]
        ps_s = [[m.ps(f"ps_s{n}{o}", [P, HP, 2 * Q]) for o in range(2)] for n in range(2)]
        ps_o = [m.ps(f"ps_o{n}", [P, HP // 2, P]) for n in range(2)]

        x_loaded = m.sem("x_loaded")
        w_loaded = m.sem("w_loaded")
        ones_ready = m.sem("ones_ready")
        zeroed = m.sem("probsT_zeroed")
        const_mm = m.sem("const_mm")
        const_ready = m.sem("const_ready")
        xn_ready = m.sem("xn_ready")
        xn_transposed = m.sem("xn_transposed")
        xnT_ready = m.sem("xnT_ready")
        qkv_mm = m.sem("qkv_mm")
        qkv_ready = m.sem("qkv_ready")
        scores_begun = m.sem("scores_begun")
        scored = m.sem("scored")
        logits_ready = m.sem("logits_ready")
        max_ready = m.sem("max_ready")
        shifted_ready = m.sem("shifted_ready")
        exp_ready = m.sem("exp_ready")
        sum_ready = m.sem("sum_ready")
        rinv_ready = m.sem("rinv_ready")
        normed_ready = m.sem("probs_normed")
        probsT_ready = m.sem("probsT_ready")
        attended = m.sem("attended")
        oT_ready = m.sem("oT_ready")
        projected = m.sem("projected")
        x_out = m.sem("x_out")
        stored = m.sem("stored")

        with nc.Block() as block:

            @block.sync
            def _(sp):
                rows = x_dram.rearrange("(t p) d -> p t d", p=P)
                sp.dma_start(x[:, :, :], rows).then_inc(x_loaded, 16)
                for dst, src in ((ident[:, :], ident_dram), (mask[:, :], mask_dram), (wq[:, :], wq_dram),
                                 (wkv[:, :], wkv_dram), (bq[:, :], bq_dram), (bk[:, :], bk_dram),
                                 (bv[:, :], bv_dram), (wp[:, :, :], wp_dram.rearrange("(c p) n -> p c n", p=P)),
                                 (bp[:, :], bp_dram)):
                    sp.dma_start(dst, src).then_inc(w_loaded, 16)
                out_rows = out_dram.rearrange("(t p) d -> p t d", p=P)
                with sp.Fori(0, NSUP) as i:
                    sp.wait_ge(x_out, SUP * i + SUP + 1)
                    sp.dma_start(out_rows[:, bass.ds(SUP * i, SUP), :], x[:, bass.ds(SUP * i, SUP), :]).then_inc(stored, 16)
                sp.wait_ge(stored, 16 * NSUP)

            @block.gpsimd
            def _(pool):
                pool.memset(one[:, :], 1.0).then_inc(ones_ready, 1)
                pool.memset(probsT[:, :, :, :], 0.0).then_inc(zeroed, 1)

            @block.tensor
            def _(pe):
                pe.wait_ge(w_loaded, 16 * 9)
                pe.wait_ge(ones_ready, 1)
                for c in range(HP):
                    pe.matmul(ps_q[0][0:1, 0:D], bv[:, c : c + 1], wp[:, c, :], start=(c == 0), stop=False)
                pe.matmul(ps_q[0][0:1, 0:D], one[:, 0:1], bp[:, :], start=False, stop=True).then_inc(const_mm, 1)
                pe.sem_inc(qkv_ready, 2)
                pe.sem_inc(xn_transposed, 1)
                pe.sem_inc(logits_ready, 4)
                pe.wait_ge(const_ready, 1)

                def scores(i, g):
                    pe.wait_ge(logits_ready, 2 * (SUP * i + g) + 2)
                    pe.sem_inc(scores_begun, 1)
                    for h in range(H):
                        r, c = HD * (h % 2), h // 2
                        for j in range(NB):
                            cols = slice(P * g + Q * j, P * g + Q * j + Q)
                            mm = pe.matmul(ps_s[g % 2][h % 2][Q * j : Q * j + Q, c, 0:Q], qT[r : r + HD, c, cols],
                                           kT[r : r + HD, c, cols], start=True, stop=True, skip_group_check=True)
                    mm.then_inc(scored, 1)

                def attend(i, g):
                    pe.wait_ge(probsT_ready, SUP * i + g + 1)
                    pe.wait_ge(oT_ready, 2 * (SUP * i + g) + 1)
                    for h in range(H):
                        r, c = HD * (h % 2), h // 2
                        mm = pe.matmul(ps_o[c // (HP // 2)][r : r + HD, c % (HP // 2), :], v[:, g, h * HD : (h + 1) * HD],
                                       probsT[:, g % 2, HP * (h % 2) + c, :], start=True, stop=True, skip_group_check=True)
                        if h % (H // 2) == H // 2 - 1:
                            mm.then_inc(attended, 1)

                def project(i, g):
                    pe.wait_ge(oT_ready, 2 * (SUP * i + g) + 3)
                    if g >= 2:
                        pe.wait_ge(x_out, SUP * i + g)
                    y = ps_q[g % 2][:, 0:D]
                    pe.matmul(y, one[:, :], crow[:, :], start=True, stop=False)
                    for c in range(HP):
                        mm = pe.matmul(y, oT[:, g % 2, c, :], wp[:, c, :], start=False, stop=(c == HP - 1))
                    mm.then_inc(projected, 1)

                with pe.Fori(0, NSUP) as i:
                    pe.wait_ge(xn_ready, SUP * i + SUP)
                    pe.wait_ge(x_out, SUP * i + 1)
                    for g in range(SUP):
                        mm = pe.transpose(ps_q[0][:, P * g : P * g + P], xn[:, 0, g, :], ident[:, :])
                    mm.then_inc(xn_transposed, 1)
                    pe.wait_ge(xnT_ready, i + 1)
                    for n in range(NQKV):
                        pe.wait_ge(qkv_ready, NQKV * i + n + 1)
                        if n < 2 * HP:
                            w, c = (wq, n) if n < HP else (wkv, n - HP)
                            mm = pe.matmul(ps_q[n % 2][:, :], w[:, P * c : P * c + P], xnT[:, :], start=True, stop=True)
                        else:
                            g, half = (n - 2 * HP) // 2, n % 2
                            at = H * HD + 512 * half
                            mm = pe.matmul(ps_q[n % 2][:, :], xnT[:, P * g : P * g + P], wkv[:, at : at + 512], start=True, stop=True)
                        mm.then_inc(qkv_mm, 1)
                    pe.wait_ge(qkv_ready, NQKV * i + NQKV + 2)
                    scores(i, 0)
                    scores(i, 1)
                    scores(i, 2)
                    attend(i, 0)
                    scores(i, 3)
                    project(i, 0)
                    attend(i, 1)
                    attend(i, 2)
                    project(i, 1)
                    project(i, 2)
                    attend(i, 3)
                    project(i, 3)

            @block.scalar
            def _(act):
                act.wait_ge(const_mm, 1)
                act.activation(crow[:, :], ps_q[0][0:1, 0:D], ACT.Copy).then_inc(const_ready, 1)
                norm.act(act)
                act.sem_inc(oT_ready, 1)

                def exp(i, g):
                    act.wait_ge(shifted_ready, SUP * i + g + 1)
                    act.activation(probs[:, g % 2, :, :], shifted[:, g % 2, :, :], ACT.Exp).then_inc(exp_ready, 1)

                def out(i, g):
                    for half in range(2):
                        act.wait_ge(attended, 2 * (SUP * i + g) + half + 1)
                        act.activation(oT[:, g % 2, half * (HP // 2) : (half + 1) * (HP // 2), :], ps_o[half][:, :, :],
                                       ACT.Copy).then_inc(oT_ready, 1)

                with act.Fori(0, NSUP) as i:
                    act.wait_ge(xn_transposed, i + 2)
                    act.activation(xnT[:, :], ps_q[0][:, :], ACT.Copy).then_inc(xnT_ready, 1)
                    for n in range(NQKV):
                        act.wait_ge(qkv_mm, NQKV * i + n + 1)
                        if n < 2 * HP:
                            dst, b, c = (qT, bq, n) if n < HP else (kT, bk, n - HP)
                            op = act.activation(dst[:, c, :], ps_q[n % 2][:, :], ACT.Identity, bias=b[:, c : c + 1])
                        else:
                            g, half = (n - 2 * HP) // 2, n % 2
                            op = act.activation(v[:, g, 512 * half : 512 * half + 512], ps_q[n % 2][:, :], ACT.Copy)
                        op.then_inc(qkv_ready, 1)
                    exp(i, 0)
                    exp(i, 1)
                    exp(i, 2)
                    out(i, 0)
                    exp(i, 3)
                    out(i, 1)
                    out(i, 2)
                    out(i, 3)

            @block.vector
            def _(dve):
                dve.wait_ge(x_loaded, 16)
                norm.dve(dve, x)
                dve.wait_ge(w_loaded, 16 * 9)
                dve.wait_ge(zeroed, 1)
                dve.sem_inc(x_out, 1)

                def shift(i, g):
                    n = SUP * i + g + 1
                    u = g % 2
                    dve.wait_ge(scored, n)
                    for o in range(2):
                        dve.scalar_tensor_tensor(logits[:, u, HP * o : HP * o + HP, :], ps_s[u][o][:, :, 0:Q], SCALE,
                                                 bcast(mask[:, :], HP, 1), ALU.mult, ALU.add).then_inc(logits_ready, 1)
                    dve.wait_ge(logits_ready, 2 * n + 4)
                    dve.tensor_reduce(rowmax[:, u, :], logits[:, u, :, :], AX, ALU.max).then_inc(max_ready, 1)
                    dve.wait_ge(max_ready, n)
                    dve.tensor_tensor(shifted[:, u, :, :], logits[:, u, :, :], bcast(rowmax[:, u, :], Q, 2),
                                      ALU.subtract).then_inc(shifted_ready, 1)

                def normalise(i, g):
                    n = SUP * i + g + 1
                    u = g % 2
                    dve.wait_ge(exp_ready, n)
                    dve.tensor_reduce(rowsum[:, u, :], probs[:, u, :, :], AX, ALU.add).then_inc(sum_ready, 1)
                    dve.wait_ge(sum_ready, n)
                    dve.reciprocal(rinv[:, u, :], rowsum[:, u, :]).then_inc(rinv_ready, 1)
                    dve.wait_ge(rinv_ready, n)
                    dve.tensor_tensor(normed[:, u, :, :], probs[:, u, :, :], bcast(rinv[:, u, :], Q, 2),
                                      ALU.mult).then_inc(normed_ready, 1)
                    dve.wait_ge(normed_ready, n)
                    if g >= 2:
                        dve.wait_ge(attended, 2 * (SUP * i + g - 1))
                    for j in range(NB):
                        rows = slice(Q * j, Q * j + Q)
                        op = dve.transpose(probsT[rows, u, :, rows], normed[rows, u, :, :])
                    op.then_inc(probsT_ready, 1)

                def add(i, g):
                    dve.wait_ge(projected, SUP * i + g + 1)
                    dve.tensor_tensor(x[:, SUP * i + g, :], x[:, SUP * i + g, :], ps_q[g % 2][:, 0:D], ALU.add).then_inc(x_out, 1)

                with dve.Fori(0, NSUP) as i:
                    dve.wait_ge(xn_transposed, i + 1)
                    for g in range(SUP):
                        norm.tile(dve, xn[:, 0, g, :], x, SUP * i + g).then_inc(xn_ready, 1)
                    shift(i, 0)
                    shift(i, 1)
                    normalise(i, 0)
                    shift(i, 2)
                    normalise(i, 1)
                    shift(i, 3)
                    add(i, 0)
                    normalise(i, 2)
                    normalise(i, 3)
                    add(i, 1)
                    add(i, 2)
                    add(i, 3)


def count_indices(nc, idx_dram, bins_dram, bias):
    K = 64
    NEVER = -1e30
    with ExitStack() as stack:
        m = Scope(nc, stack, "ci")
        raw = m.sb("raw", [P, NT * K], I32)
        bins = m.sb("bins", [P, K])
        val = m.sb("val", [P, 4, NT * K])
        idx = m.sb("idx", [P, NT * K], BF16)
        same = m.sb("same", [P, NT, K], BF16)
        part = m.sb("part", [P, NT, K], BF16)
        cnt = m.sb("cnt", [P, NT, K])
        loaded = m.sem("loaded")
        prep = m.sem("prep")
        summed = m.sem("summed")
        logged = m.sem("logged")
        STEPS = 6
        with nc.Block() as block:

            @block.sync
            def _(sp):
                sp.dma_start(raw[:, :], idx_dram).then_inc(loaded, 16)
                sp.dma_start(bins[:, :], bins_dram).then_inc(loaded, 16)

            @block.scalar
            def _(act):
                act.wait_ge(prep, 6)
                act.activation(val[:, 3, :], val[:, 0, :], ACT.Ln).then_inc(logged, 1)

            @block.vector
            def _(dve):
                dve.wait_ge(loaded, 32)
                dve.tensor_copy(val[:, 0, :], raw[:, :]).then_inc(prep, 1)
                dve.wait_ge(prep, 1)
                dve.tensor_scalar(val[:, 1, :], val[:, 0, :], 0.0, float(K), ALU.is_lt, ALU.mult).then_inc(prep, 1)
                dve.wait_ge(prep, 2)
                dve.tensor_tensor(val[:, 2, :], val[:, 0, :], val[:, 1, :], ALU.add).then_inc(prep, 1)
                dve.wait_ge(prep, 3)
                dve.tensor_scalar(idx[:, :], val[:, 2, :], 0.0, float(K - 1), ALU.max, ALU.min).then_inc(prep, 1)
                dve.wait_ge(prep, 4)
                dve.sem_inc(summed, 1)
                with dve.Fori(0, K) as j:
                    dve.wait_ge(summed, STEPS * j + 1)
                    dve.tensor_scalar(same[:, :, :].rearrange("p t k -> p (t k)"), idx[:, :], bins[:, bass.ds(j, 1)], None,
                                      ALU.is_equal).then_inc(summed, 1)
                    src, at, n = same[:, :, :], 0, K // 2
                    for level in range(4):
                        dve.wait_ge(summed, STEPS * j + level + 2)
                        dst = part[:, :, at : at + n]
                        dve.tensor_tensor(dst, src[:, :, 0:n], src[:, :, n : 2 * n], ALU.add).then_inc(summed, 1)
                        src, at, n = dst, at + n, n // 2
                    dve.wait_ge(summed, STEPS * j + 6)
                    dve.tensor_reduce(cnt[:, :, j], src, AX, ALU.add).then_inc(summed, 1)
                dve.wait_ge(summed, STEPS * K + 1)
                cflat = cnt[:, :, :].rearrange("p t k -> p (t k)")
                dve.tensor_scalar(val[:, 0, :], cflat, 1.0, None, ALU.max).then_inc(prep, 1)
                dve.tensor_scalar(val[:, 1, :], cflat, 0.0, NEVER, ALU.is_equal, ALU.mult).then_inc(prep, 1)
                dve.wait_ge(logged, 1)
                dve.wait_ge(prep, 6)
                dve.tensor_tensor(bias[:, :, :].rearrange("p t k -> p (t k)"), val[:, 1, :], val[:, 3, :],
                                  ALU.add).then_inc(prep, 1)
                dve.wait_ge(prep, 7)


def gathered_attention(nc, x, bias, ident, ctxT_dram, downT_dram, upT_dram, qT_dram, outT_dram, hmask_dram, pmask_dram):
    H, HD, K = 16, 8, 64
    HP, VW = H // 2, 2 * (HD + 1)
    SCALE = 1.0 / HD**0.5
    HK = H * K
    with ExitStack() as stack:
        m = Scope(nc, stack, "ga")
        ctxT = m.sb("ctxT", [D, B * K])
        downT = m.sb("downT", [D, D])
        upT = m.sb("upT", [D, 2 * D])
        qW = m.sb("qW", [D, D])
        oW = m.sb("oW", [D, D])
        hmask = m.sb("hmask", [P, H])
        pmask = m.sb("pmask", [P, 2])
        cT = m.sb("cT", [P, B, 2, K])
        kT = m.sb("kT", [P, B, K])
        keys = m.sb("keys", [P, B, H, K])
        vals = m.sb("vals", [P, B, HP, VW])
        norm = Norm(m)
        xn = m.sb("xn", [P, 2, D])
        xnT = m.sb("xnT", [P, 2 * P])
        qT = m.sb("qT", [P, 2 * P])
        logits = m.sb("logits", [P, 2, H, K])
        rowmax = m.sb("rowmax", [P, 2, H])
        shifted = m.sb("shifted", [P, 2, H, K])
        probs = m.sb("probs", [P, 2, HK])
        probsT = m.sb("probsT", [P, 2, HP, P])
        rinv = m.sb("rinv", [P, 2, HP, 2])
        o = m.sb("o", [P, 2, D])
        oT = m.sb("oT", [P, 2, P])
        ps_s = [m.ps(f"ps_s{u}", [P, H, K]) for u in range(2)]
        ps_p = m.ps("ps_p", [P, HP, P])
        ps_m = m.ps("ps_m", [P, 512])
        ps_o = m.ps("ps_o", [P, 512])

        loaded = m.sem("loaded")
        ctx_mm, ctx_ready = m.sem("ctx_mm"), m.sem("ctx_ready")
        key_mm, key_ready = m.sem("key_mm"), m.sem("key_ready")
        val_mm, val_ready = m.sem("val_mm"), m.sem("val_ready")
        keys_ready = m.sem("keys_ready")
        ones_ready = m.sem("ones_ready")
        xn_ready, xn_transposed, xnT_ready = m.sem("xn_ready"), m.sem("xn_transposed"), m.sem("xnT_ready")
        q_mm, qT_ready = m.sem("q_mm"), m.sem("qT_ready")
        scored, logits_ready, max_ready = m.sem("scored"), m.sem("logits_ready"), m.sem("max_ready")
        shifted_ready, exp_ready = m.sem("shifted_ready"), m.sem("exp_ready")
        probs_transposed, probsT_ready = m.sem("probs_transposed"), m.sem("probsT_ready")
        attended, rinv_ready, o_ready = m.sem("attended"), m.sem("rinv_ready"), m.sem("o_ready")
        o_transposed, oT_ready = m.sem("o_transposed"), m.sem("oT_ready")
        projected, x_out = m.sem("projected"), m.sem("x_out")
        NLOAD = 7

        with nc.Block() as block:

            @block.sync
            def _(sp):
                for dst, src in ((ctxT, ctxT_dram), (downT, downT_dram), (upT, upT_dram), (qW, qT_dram),
                                 (oW, outT_dram), (hmask, hmask_dram), (pmask, pmask_dram)):
                    sp.dma_start(dst[:, :], src).then_inc(loaded, 16)

            @block.gpsimd
            def _(pool):
                pool.wait_ge(loaded, 16 * NLOAD)
                for h2 in range(2):
                    col = vals[:, :, :, h2 * (HD + 1) + HD].rearrange("p b c -> p (b c)")
                    pool.tensor_copy(col, bcast(pmask[:, h2], B * HP, 1)).then_inc(ones_ready, 1)
                pool.wait_ge(key_ready, 2)
                with pool.Fori(0, B) as b:
                    pool.tensor_tensor(keys[:, b, :, :], bcast(kT[:, b, :], H, 1), bcast(hmask[:, :], K, 2),
                                       ALU.mult).then_inc(keys_ready, 1)

            @block.tensor
            def _(pe):
                pe.wait_ge(loaded, 16 * NLOAD)
                for n in range(2):
                    pe.matmul(ps_s[0][:, 8 * n : 8 * n + 8, :], downT[:, :], ctxT[:, 512 * n : 512 * n + 512],
                              start=True, stop=True).then_inc(ctx_mm, 1)
                pe.wait_ge(ctx_ready, 4)
                for n in range(2):
                    pe.matmul(ps_s[1][:, 8 * n : 8 * n + 8, :], upT[:, 0:D], cT[:, 8 * n : 8 * n + 8, 0, :],
                              start=True, stop=True).then_inc(key_mm, 1)
                banks = [ps_p[:, 0:4, :], ps_p[:, 4:8, :]]
                for b in range(B):
                    if b in (8, 12):
                        pe.wait_ge(val_ready, (b - 4) // 4)
                    mm = pe.matmul(banks[(b // 4) % 2][:, b % 4, :], cT[:, b, :, :].rearrange("p e k -> p (e k)"), upT[:, D : 2 * D],
                                   start=True, stop=True)
                    if b % 4 == 3:
                        mm.then_inc(val_mm, 1)
                pe.wait_ge(val_ready, B // 4)
                pe.wait_ge(ones_ready, 2)
                pe.wait_ge(key_ready, 2)
                pe.sem_inc(logits_ready, 1)
                pe.sem_inc(probsT_ready, 1)
                pe.sem_inc(rinv_ready, 1)

                def turn_x(b):
                    pe.wait_ge(xn_ready, 2 * b + 2)
                    for u in range(2):
                        mm = pe.transpose(ps_m[:, P * u : P * u + P], xn[:, u, :], ident[:, :])
                    mm.then_inc(xn_transposed, 1)

                def queries(b):
                    pe.wait_ge(xnT_ready, b + 1)
                    pe.matmul(ps_m[:, 256:512], qW[:, :], xnT[:, :], start=True, stop=True).then_inc(q_mm, 1)

                def scores(b, u):
                    if u == 0:
                        pe.wait_ge(qT_ready, b + 1)
                        pe.wait_ge(keys_ready, b + 1)
                    for n in range(2):
                        mm = pe.matmul(ps_s[u][:, 8 * n : 8 * n + 8, :], qT[:, P * u : P * u + P],
                                       keys[:, b, 8 * n : 8 * n + 8, :], start=True, stop=True)
                    mm.then_inc(scored, 1)

                def turn_probs(b, u):
                    pe.wait_ge(exp_ready, 2 * b + u + 1)
                    for c in range(HP):
                        mm = pe.transpose(ps_p[:, c, :], probs[:, u, P * c : P * c + P], ident[:, :])
                        if c % 4 == 3:
                            mm.then_inc(probs_transposed, 1)

                def attend(b, u):
                    pe.wait_ge(probsT_ready, 2 * (2 * b + u) + 3)
                    for c in range(HP):
                        mm = pe.matmul(ps_o[:, VW * c : VW * c + VW], probsT[:, u, c, :], vals[:, b, c, :],
                                       start=True, stop=True)
                    mm.then_inc(attended, 1)

                def finish(b):
                    pe.wait_ge(o_ready, 2 * b + 2)
                    for u in range(2):
                        mm = pe.transpose(ps_p[:, u, :], o[:, u, :], ident[:, :])
                    mm.then_inc(o_transposed, 1)
                    pe.wait_ge(oT_ready, b + 1)
                    for u in range(2):
                        mm = pe.matmul(ps_p[:, 4 + u, :], oT[:, u, :], oW[:, :], start=True, stop=True)
                    mm.then_inc(projected, 1)

                turn_x(0)
                queries(0)
                scores(0, 0)
                scores(0, 1)
                with pe.Fori(1, B) as b:
                    turn_x(b)
                    turn_probs(b - 1, 0)
                    queries(b)
                    attend(b - 1, 0)
                    scores(b, 0)
                    pe.wait_ge(o_ready, 2 * b - 1)
                    turn_probs(b - 1, 1)
                    attend(b - 1, 1)
                    scores(b, 1)
                    finish(b - 1)
                    pe.wait_ge(x_out, b)
                turn_probs(B - 1, 0)
                attend(B - 1, 0)
                pe.wait_ge(o_ready, 2 * B - 1)
                turn_probs(B - 1, 1)
                attend(B - 1, 1)
                finish(B - 1)

            @block.scalar
            def _(act):
                for n in range(2):
                    act.wait_ge(ctx_mm, n + 1)
                    for e in range(2):
                        act.activation(cT[:, 8 * n : 8 * n + 8, e, :], ps_s[0][:, 8 * n : 8 * n + 8, :], ACT.Copy).then_inc(ctx_ready, 1)
                for n in range(2):
                    act.wait_ge(key_mm, n + 1)
                    act.activation(kT[:, 8 * n : 8 * n + 8, :], ps_s[1][:, 8 * n : 8 * n + 8, :], ACT.Copy).then_inc(key_ready, 1)
                norm.act(act)

                def copy_x(b):
                    act.wait_ge(xn_transposed, b + 1)
                    act.activation(xnT[:, :], ps_m[:, 0:256], ACT.Copy).then_inc(xnT_ready, 1)

                def copy_q(b):
                    act.wait_ge(q_mm, b + 1)
                    act.activation(qT[:, :], ps_m[:, 256:512], ACT.Copy, scale=SCALE).then_inc(qT_ready, 1)

                def exp(b, u):
                    act.wait_ge(shifted_ready, 2 * b + u + 1)
                    act.activation(probs[:, u, :], shifted[:, u, :, :].rearrange("p h k -> p (h k)"), ACT.Exp).then_inc(exp_ready, 1)

                def copy_probs(b, u):
                    for n in range(2):
                        act.wait_ge(probs_transposed, 2 * (2 * b + u) + n + 1)
                        act.activation(probsT[:, u, 4 * n : 4 * n + 4, :], ps_p[:, 4 * n : 4 * n + 4, :], ACT.Copy).then_inc(probsT_ready, 1)

                def copy_o(b):
                    act.wait_ge(o_transposed, b + 1)
                    act.activation(oT[:, :, :], ps_p[:, 0:2, :], ACT.Copy).then_inc(oT_ready, 1)

                copy_x(0)
                copy_q(0)
                exp(0, 0)
                exp(0, 1)
                with act.Fori(1, B) as b:
                    copy_x(b)
                    copy_probs(b - 1, 0)
                    copy_q(b)
                    copy_probs(b - 1, 1)
                    exp(b, 0)
                    exp(b, 1)
                    copy_o(b - 1)
                copy_probs(B - 1, 0)
                copy_probs(B - 1, 1)
                copy_o(B - 1)

            @block.vector
            def _(dve):
                norm.dve(dve, x)
                dve.wait_ge(loaded, 16 * NLOAD)
                banks = [ps_p[:, 0:4, :], ps_p[:, 4:8, :]]
                for n in range(B // 4):
                    dve.wait_ge(val_mm, n + 1)
                    dst = vals[:, 4 * n : 4 * n + 4, :, :].rearrange("p b c (e w) -> p (b c) e w", e=2)[:, :, :, 0:HD]
                    src = banks[n % 2].rearrange("p b (c e d) -> p (b c) e d", e=2, d=HD)
                    dve.tensor_tensor(dst, src, bcast(bcast(pmask[:, :], HD, 2), 4 * HP, 1), ALU.mult).then_inc(val_ready, 1)

                def norm_x(b):
                    for u in range(2):
                        norm.tile(dve, xn[:, u, :], x, B * u + b).then_inc(xn_ready, 1)

                def shift(b, u):
                    n = 2 * b + u + 1
                    dve.wait_ge(scored, n)
                    dve.tensor_tensor(logits[:, u, :, :], ps_s[u][:, :, :], bcast(bias[:, B * u + b, :], H, 1),
                                      ALU.add).then_inc(logits_ready, 1)
                    dve.wait_ge(logits_ready, n + 1)
                    dve.tensor_reduce(rowmax[:, u, :], logits[:, u, :, :], AX, ALU.max).then_inc(max_ready, 1)
                    dve.wait_ge(max_ready, n)
                    dve.tensor_tensor(shifted[:, u, :, :], logits[:, u, :, :], bcast(rowmax[:, u, :], K, 2),
                                      ALU.subtract).then_inc(shifted_ready, 1)

                def divide(b, u):
                    n = 2 * b + u + 1
                    dve.wait_ge(attended, n)
                    out = ps_o[:, 0 : HP * VW].rearrange("p (c e w) -> p c e w", c=HP, e=2)
                    dve.reciprocal(rinv[:, u, :, :], out[:, :, :, HD]).then_inc(rinv_ready, 1)
                    dve.wait_ge(rinv_ready, n + 1)
                    dve.tensor_tensor(o[:, u, :].rearrange("p (c e d) -> p c e d", c=HP, e=2), out[:, :, :, 0:HD],
                                      bcast(rinv[:, u, :, :], HD, 3), ALU.mult).then_inc(o_ready, 1)

                def add(b):
                    dve.wait_ge(projected, b + 1)
                    view = x[:, :, :].rearrange("p (u b) d -> p u b d", u=2)[:, :, b, :]
                    dve.tensor_tensor(view, view, ps_p[:, 4:6, :], ALU.add).then_inc(x_out, 1)

                norm_x(0)
                shift(0, 0)
                shift(0, 1)
                with dve.Fori(1, B) as b:
                    norm_x(b)
                    divide(b - 1, 0)
                    shift(b, 0)
                    divide(b - 1, 1)
                    shift(b, 1)
                    add(b - 1)
                divide(B - 1, 0)
                divide(B - 1, 1)
                add(B - 1)
                dve.wait_ge(x_out, B)


def gated_experts(nc, x, ident, scale_dram, bias_dram, gateT_dram, wg_dram, wu_dram, wd_dram, lower_dram):
    E, F, TOP = 8, 256, 2
    C = F // P
    NE = E + 1
    with ExitStack() as stack:
        m = Scope(nc, stack, "ge")
        lns = m.sb("ln_scale", [D, 1])
        lnb = m.sb("ln_bias", [D, 1])
        lnbB = m.sb("ln_bias_rows", [D, P])
        gateT = m.sb("gateT", [D, E])
        gateS = m.sb("gateS", [D, E])
        lower = m.sb("lower", [P, E, E])
        wg = m.sb("wg", [D, NE, F])
        wu = m.sb("wu", [D, NE, F])
        wd = m.sb("wd", [P, NE, C, D])
        norm = Norm(m)
        xn = m.sb("xn", [P, SUP, D])
        xnT = m.sb("xnT", [D, SUP * P])
        xT = m.sb("xT", [D, TOK])
        gbias = m.sb("gbias", [P, E])
        raw = m.sb("raw_logits", [P, NT, E])
        gt = m.sb("gate", [P, 12, NT, E])
        gs = m.sb("gate_stats", [P, 8, NT])
        cmp = m.sb("cmp", [P, 4, NT, E * E])
        weight = m.sb("weight", [P, NT, E])
        sg = m.sb("silu_g", [P, 2, SUP * P])
        hT = m.sb("hT", [P, 6, SUP * P])
        ps_u = [[m.ps(f"ps_{k}{n}", [P, SUP * P]) for k in "gu"] for n in range(2)]
        ps_y = [m.ps(f"ps_y{n}", [P, SUP, D]) for n in range(3)]
        ps_m = m.ps("ps_m", [P, 512])

        loaded = m.sem("loaded")
        gate_prep = m.sem("gate_prep")
        gbias_mm = m.sem("gbias_mm")
        gbias_ready = m.sem("gbias_ready")
        xn_ready, xn_transposed, xnT_ready = m.sem("xn_ready"), m.sem("xn_transposed"), m.sem("xnT_ready")
        xT_ready, logits_mm, raw_ready = m.sem("xT_ready"), m.sem("logits_mm"), m.sem("raw_ready")
        gated = m.sem("gated")
        gate_sqrt, gate_exp = m.sem("gate_sqrt"), m.sem("gate_exp")
        up_mm, silu_ready, h_ready = m.sem("up_mm"), m.sem("silu_ready"), m.sem("h_ready")
        down_mm, added = m.sem("down_mm"), m.sem("added")
        NLOAD = 7

        with nc.Block() as block:

            @block.sync
            def _(sp):
                for dst, src in ((lns[:, :], scale_dram), (lnb[:, :], bias_dram), (gateT[:, :], gateT_dram),
                                 (lower[:, :, :], lower_dram), (wg[:, :, :], wg_dram), (wu[:, :, :], wu_dram),
                                 (wd[:, :, :, :], wd_dram)):
                    sp.dma_start(dst, src).then_inc(loaded, 16)

            @block.gpsimd
            def _(pool):
                pool.sem_inc(xT_ready, 1)
                with pool.Fori(0, NSUP) as i:
                    pool.wait_ge(xnT_ready, i + 1)
                    pool.tensor_copy(xT[:, bass.ds(SUP * P * i, SUP * P)], xnT[:, :]).then_inc(xT_ready, 1)

            @block.tensor
            def _(pe):
                pe.wait_ge(gate_prep, 2)
                pe.matmul(ps_m[:, 0:E], lnbB[:, :], gateT[:, :], start=True, stop=True).then_inc(gbias_mm, 1)
                pe.wait_ge(gbias_ready, 1)
                with pe.Fori(0, NSUP) as i:
                    pe.wait_ge(xn_ready, SUP * i + SUP)
                    for g in range(SUP):
                        mm = pe.transpose(ps_u[0][0][:, P * g : P * g + P], xn[:, g, :], ident[:, :])
                    mm.then_inc(xn_transposed, 1)
                    pe.wait_ge(xnT_ready, i + 1)
                    pe.wait_ge(raw_ready, i + 1)
                    for g in range(SUP):
                        mm = pe.matmul(ps_m[:, E * g : E * g + E], xnT[:, P * g : P * g + P], gateS[:, :], start=True, stop=True)
                    mm.then_inc(logits_mm, 1)
                pe.wait_ge(xT_ready, NSUP + 1)
                pe.sem_inc(h_ready, 2)
                pe.sem_inc(added, 3)

                def up(i, e, c):
                    pe.wait_ge(h_ready, C * NE * i + C * e + c + 1)
                    for w, bank in zip((wg, wu), ps_u[c]):
                        mm = pe.matmul(bank[:, :], w[:, e, P * c : P * c + P], xT[:, bass.ds(SUP * P * i, SUP * P)],
                                       start=True, stop=True)
                        mm.then_inc(up_mm, 1)

                def down(i, e):
                    pe.wait_ge(h_ready, C * NE * i + C * e + C + 2)
                    pe.wait_ge(added, NE * i + e + 1)
                    for g in range(SUP):
                        for c in range(C):
                            mm = pe.matmul(ps_y[e % 3][:, g, :], hT[:, (C * e + c) % 6, P * g : P * g + P], wd[:, e, c, :],
                                           start=(c == 0), stop=(c == C - 1))
                    mm.then_inc(down_mm, 1)

                with pe.Fori(0, NSUP) as i:
                    for e in range(NE):
                        for c in range(C):
                            up(i, e, c)
                        if e:
                            down(i, e - 1)
                    down(i, NE - 1)

            @block.scalar
            def _(act):
                norm.act(act)
                with act.Fori(0, NSUP) as i:
                    act.wait_ge(xn_transposed, i + 1)
                    act.wait_ge(xT_ready, i + 1)
                    act.activation(xnT[:, :], ps_u[0][0][:, :], ACT.Copy).then_inc(xnT_ready, 1)
                act.wait_ge(gated, 2)
                act.activation(gs[:, 2, :], gs[:, 1, :], ACT.Sqrt).then_inc(gate_sqrt, 1)
                act.wait_ge(gated, 7)
                act.activation(gt[:, 3, :, :], gt[:, 2, :, :], ACT.Exp).then_inc(gate_exp, 1)
                with act.Fori(0, NSUP) as i:
                    for n in range(C * NE):
                        act.wait_ge(up_mm, 2 * (C * NE * i + n) + 1)
                        act.activation(sg[:, n % 2, :], ps_u[n % 2][0][:, :], ACT.Silu).then_inc(silu_ready, 1)

            @block.vector
            def _(dve):
                norm.dve(dve, x)
                dve.wait_ge(loaded, 16 * NLOAD)
                dve.tensor_copy(lnbB[:, :], bcast(lnb[:, 0], P, 1)).then_inc(gate_prep, 1)
                dve.tensor_scalar(gateS[:, :], gateT[:, :], lns[:, 0:1], None, ALU.mult).then_inc(gate_prep, 1)
                dve.wait_ge(gbias_mm, 1)
                dve.tensor_copy(gbias[:, :], ps_m[:, 0:E]).then_inc(gbias_ready, 1)
                dve.sem_inc(raw_ready, 1)

                with dve.Fori(0, NSUP) as i:
                    dve.wait_ge(raw_ready, i + 1)
                    for g in range(SUP):
                        norm.tile(dve, xn[:, g, :], x, SUP * i + g).then_inc(xn_ready, 1)
                    dve.wait_ge(logits_mm, i + 1)
                    dve.tensor_copy(raw[:, bass.ds(SUP * i, SUP), :],
                                    ps_m[:, 0 : SUP * E].rearrange("p (g e) -> p g e", e=E)).then_inc(raw_ready, 1)
                dve.wait_ge(raw_ready, NSUP + 1)

                g = lambda k: gt[:, k, :, :]
                dve.tensor_tensor(gs[:, 0, :], norm.rstd[:, :], norm.rstd[:, :], ALU.mult).then_inc(gated, 1)
                dve.wait_ge(gated, 1)
                dve.tensor_scalar(gs[:, 1, :], gs[:, 0, :], -EPS, 1.0 + EPS, ALU.mult, ALU.add).then_inc(gated, 1)
                dve.wait_ge(gate_sqrt, 1)
                dve.reciprocal(gs[:, 3, :], gs[:, 2, :]).then_inc(gated, 1)
                dve.wait_ge(gated, 3)
                dve.tensor_tensor(g(0), raw[:, :, :], bcast(gs[:, 3, :], E, 2), ALU.mult).then_inc(gated, 1)
                dve.wait_ge(gated, 4)
                dve.tensor_tensor(g(1), g(0), bcast(gbias[:, :], NT, 1), ALU.add).then_inc(gated, 1)
                dve.wait_ge(gated, 5)
                dve.tensor_reduce(gs[:, 4, :], g(1), AX, ALU.max).then_inc(gated, 1)
                dve.wait_ge(gated, 6)
                dve.tensor_tensor(g(2), g(1), bcast(gs[:, 4, :], E, 2), ALU.subtract).then_inc(gated, 1)
                dve.wait_ge(gate_exp, 1)
                dve.tensor_reduce(gs[:, 5, :], g(3), AX, ALU.add).then_inc(gated, 1)
                dve.wait_ge(gated, 8)
                dve.reciprocal(gs[:, 6, :], gs[:, 5, :]).then_inc(gated, 1)
                dve.wait_ge(gated, 9)
                dve.tensor_tensor(g(4), g(3), bcast(gs[:, 6, :], E, 2), ALU.mult).then_inc(gated, 1)
                dve.wait_ge(gated, 10)
                sq = lambda k: cmp[:, k, :, :].rearrange("p t (e f) -> p t e f", e=E)
                mine, other = bcast(g(4), E, 3), bcast(g(4), E, 2)
                dve.tensor_tensor(sq(0), other, mine, ALU.is_gt).then_inc(gated, 1)
                dve.tensor_tensor(sq(1), other, mine, ALU.is_equal).then_inc(gated, 1)
                dve.wait_ge(gated, 12)
                dve.tensor_tensor(sq(2), sq(1), bcast(lower[:, :, :], NT, 1), ALU.mult).then_inc(gated, 1)
                dve.wait_ge(gated, 13)
                dve.tensor_tensor(cmp[:, 3, :, :], cmp[:, 0, :, :], cmp[:, 2, :, :], ALU.add).then_inc(gated, 1)
                dve.wait_ge(gated, 14)
                dve.tensor_reduce(g(5), sq(3), AX, ALU.add).then_inc(gated, 1)
                dve.wait_ge(gated, 15)
                dve.tensor_scalar(g(6), g(5), TOP - 0.5, None, ALU.is_lt).then_inc(gated, 1)
                dve.wait_ge(gated, 16)
                dve.tensor_tensor(g(7), g(6), g(4), ALU.mult).then_inc(gated, 1)
                dve.wait_ge(gated, 17)
                dve.tensor_reduce(gs[:, 7, :], g(7), AX, ALU.add).then_inc(gated, 1)
                dve.wait_ge(gated, 18)
                dve.tensor_scalar(norm.tmp[:, 0, :], gs[:, 7, :], EPS, None, ALU.add).then_inc(gated, 1)
                dve.wait_ge(gated, 19)
                dve.reciprocal(norm.tmp[:, 1, :], norm.tmp[:, 0, :]).then_inc(gated, 1)
                dve.wait_ge(gated, 20)
                dve.tensor_tensor(weight[:, :, :], g(7), bcast(norm.tmp[:, 1, :], E, 2), ALU.mult).then_inc(gated, 1)
                dve.wait_ge(gated, 21)

                def hidden(i, e):
                    for c in range(C):
                        n = C * NE * i + C * e + c + 1
                        dve.wait_ge(silu_ready, n)
                        dve.wait_ge(up_mm, 2 * n)
                        dve.tensor_tensor(hT[:, (C * e + c) % 6, :], sg[:, c, :], ps_u[c][1][:, :], ALU.mult).then_inc(h_ready, 1)

                def add(i, e):
                    dve.wait_ge(down_mm, NE * i + e + 1)
                    dve.wait_ge(added, NE * i + e + 3)
                    if e == 0:
                        view = x[:, bass.ds(SUP * i, SUP), :]
                        dve.tensor_tensor(view, view, ps_y[0][:, :, :], ALU.add).then_inc(added, 1)
                    else:
                        for g in range(SUP):
                            t = SUP * i + g
                            op = dve.scalar_tensor_tensor(x[:, t, :], ps_y[e % 3][:, g, :], weight[:, t, e - 1 : e], x[:, t, :],
                                                          ALU.mult, ALU.add)
                        op.then_inc(added, 1)

                with dve.Fori(0, NSUP) as i:
                    for e in range(NE):
                        hidden(i, e)
                        if e:
                            add(i, e - 1)
                    add(i, NE - 1)
                dve.wait_ge(added, NE * NSUP + 3)


def norm_statistics(nc, x, norm):
    with nc.Block() as block:

        @block.scalar
        def _(act):
            norm.act(act)

        @block.vector
        def _(dve):
            norm.dve(dve, x)


INNER, STATE, TAPS, HEADS = 256, 64, 4, 4
HEADDIM = INNER // HEADS


def ssm_inputs(nc, x, ident, norm, m, backward, w, store):
    CH = 3
    NB = 2
    ZD = INNER + HEADS
    with ExitStack() as stack:
        k = Scope(nc, stack, m.prefix + "i")
        win = k.sb("win", [D, 2 * INNER + 2 * STATE + HEADS])
        wzd = k.sb("wzd", [D, ZD])
        cw = k.sb("conv_w", [P, CH, TAPS])
        cb = k.sb("conv_b", [P, CH])
        pick = k.sb("pick", [P, P])
        xn = k.sb("xn", [P, SUP, D])
        xnT = k.sb("xnT", [D, SUP * P])
        pad = k.sb("pad", [P, CH, NB, S + TAPS - 1])
        acc = k.sb("acc", [P, CH, NB, S])
        xs = k.sb("xs", [P, CH, NB, S])
        cs = k.sb("cs", [P, SUP * P])
        ps_a = [k.ps(f"ps_a{n}", [P, 512]) for n in range(4)]
        ps_b = [k.ps(f"ps_b{n}", [P, 512]) for n in range(4)]
        loaded, padded = k.sem("loaded"), k.sem("padded")
        xn_ready, xn_transposed, xnT_ready = k.sem("xn_ready"), k.sem("xn_transposed"), k.sem("xnT_ready")
        in_mm, in_ready = k.sem("in_mm"), k.sem("in_ready")
        z_mm, z_ready, dt_ready = k.sem("z_mm"), k.sem("z_ready"), k.sem("dt_ready")
        conv, xs_ready = k.sem("conv"), k.sem("xs_ready")
        c_mm, c_ready, c_kept = k.sem("c_mm"), k.sem("c_ready"), k.sem("c_kept")
        g_mm, g_ready = k.sem("g_mm"), k.sem("g_ready")
        turned, x_ready, b_ready = k.sem("turned"), k.sem("x_ready"), k.sem("b_ready")
        NLOAD = 5
        first = 0 if backward else TAPS - 1
        hole = S if backward else 0
        CONV = CH * TAPS

        def tiles(buf, i, g):
            return buf[:, B * (g % 2) + NB * i + g // 2, :]

        with nc.Block() as block:

            @block.sync
            def _(sp):
                for dst, src in ((win[:, :], w["in"]), (wzd[:, 0:INNER], w["in"][:, 0:INNER]),
                                 (cw[:, :, :], w["conv_w"]), (cb[:, :], w["conv_b"]), (pick[:, :], w["pick"])):
                    sp.dma_start(dst, src).then_inc(loaded, 16)

            @block.gpsimd
            def _(pool):
                pool.memset(pad[:, :, :, hole : hole + TAPS - 1], 0.0).then_inc(padded, 1)
                pool.wait_ge(loaded, 16 * NLOAD)
                pool.tensor_copy(wzd[:, INNER:ZD], win[:, 2 * INNER + 2 * STATE :]).then_inc(padded, 1)
                pool.sem_inc(c_kept, 1)
                with pool.Fori(0, NSUP) as i:
                    pool.wait_ge(c_ready, i + 1)
                    for g in range(SUP):
                        op = pool.tensor_copy(tiles(store["c"], i, g), cs[0:STATE, P * g : P * g + P])
                    op.then_inc(c_kept, 1)

            @block.tensor
            def _(pe):
                pe.wait_ge(loaded, 16 * NLOAD)
                pe.wait_ge(padded, 2)
                with pe.Fori(0, NSUP) as i:
                    pe.wait_ge(xn_ready, SUP * i + SUP)
                    for g in range(SUP):
                        mm = pe.transpose(ps_a[0][:, P * g : P * g + P], xn[:, g, :], ident[:, :])
                    mm.then_inc(xn_transposed, 1)
                    pe.wait_ge(xnT_ready, i + 1)
                    for c in range(CH):
                        mm = pe.matmul(ps_a[1 + c][:, :], win[:, INNER + P * c : INNER + P * c + P], xnT[:, :], start=True, stop=True)
                        mm.then_inc(in_mm, 1)
                    for g in range(SUP):
                        mm = pe.matmul(ps_b[g][:, 0:ZD], xnT[:, P * g : P * g + P], wzd[:, :], start=True, stop=True)
                        mm.then_inc(z_mm, 1)
                    pe.wait_ge(xs_ready, CH * i + CH)
                    pe.matmul(ps_a[0][:, :], pick[:, :], xs[:, 2, :, :], start=True, stop=True).then_inc(c_mm, 1)
                    for g in range(SUP):
                        pe.wait_ge(z_ready, SUP * i + g + 1)
                        pe.wait_ge(dt_ready, SUP * i + g + 1)
                        for c in range(CH):
                            mm = pe.transpose(ps_b[g][:, P * c : P * c + P], xs[:, c, g // 2, P * (g % 2) : P * (g % 2) + P], ident[:, :])
                        mm.then_inc(turned, 1)
                    pe.wait_ge(c_ready, i + 1)
                    for g in range(SUP):
                        mm = pe.matmul(ps_a[1][:, P * g : P * g + P], xs[:, 2, g // 2, P * (g % 2) : P * (g % 2) + P],
                                       cs[:, P * g : P * g + P], start=True, stop=True)
                    mm.then_inc(g_mm, 1)
                    pe.wait_ge(g_ready, i + 1)
                    pe.wait_ge(x_ready, SUP * i + SUP)
                    pe.wait_ge(b_ready, SUP * i + SUP + 1)

            @block.scalar
            def _(act):
                act.wait_ge(padded, 1)
                with act.Fori(0, NSUP) as i:
                    act.wait_ge(xn_transposed, i + 1)
                    act.activation(xnT[:, :], ps_a[0][:, :], ACT.Copy).then_inc(xnT_ready, 1)
                    for c in range(CH):
                        act.wait_ge(in_mm, CH * i + c + 1)
                        act.activation(pad[:, c, :, first : first + S], ps_a[1 + c][:, :].rearrange("p (b s) -> p b s", b=NB),
                                       ACT.Copy).then_inc(in_ready, 1)
                    for g in range(SUP):
                        act.wait_ge(z_mm, SUP * i + g + 1)
                        act.activation(tiles(store["z"], i, g), ps_b[g][:, 0:INNER], ACT.Silu).then_inc(z_ready, 1)
                    for c in range(CH):
                        act.wait_ge(conv, CONV * i + CH * (TAPS - 1) + c + 1)
                        act.activation(xs[:, c, :, :], acc[:, c, :, :], ACT.Silu).then_inc(xs_ready, 1)
                    act.wait_ge(c_mm, i + 1)
                    act.wait_ge(c_kept, i + 1)
                    act.activation(cs[:, :], ps_a[0][:, :], ACT.Copy).then_inc(c_ready, 1)
                    for g in range(SUP):
                        act.wait_ge(turned, SUP * i + g + 1)
                        act.activation(tiles(store["x"], i, g), ps_b[g][:, 0:INNER], ACT.Copy).then_inc(x_ready, 1)

            @block.vector
            def _(dve):
                dve.wait_ge(loaded, 16 * NLOAD)
                dve.sem_inc(b_ready, 1)
                with dve.Fori(0, NSUP) as i:
                    dve.wait_ge(b_ready, SUP * i + 1)
                    for g in range(SUP):
                        norm.tile(dve, xn[:, g, :], x, B * (g % 2) + NB * i + g // 2).then_inc(xn_ready, 1)
                    for n in range(TAPS):
                        at = TAPS - 1 - n if backward else n
                        for c in range(CH):
                            src = pad[:, c, :, at : at + S]
                            if n == 0:
                                dve.wait_ge(in_ready, CH * i + c + 1)
                                op = dve.tensor_scalar(acc[:, c, :, :], src, cw[:, c, 0:1], cb[:, c : c + 1], ALU.mult, ALU.add)
                            else:
                                dve.wait_ge(conv, CONV * i + CH * (n - 1) + c + 1)
                                op = dve.scalar_tensor_tensor(acc[:, c, :, :], src, cw[:, c, n : n + 1], acc[:, c, :, :],
                                                              ALU.mult, ALU.add)
                            op.then_inc(conv, 1)
                        if n == 0:
                            for g in range(SUP):
                                dve.wait_ge(z_mm, SUP * i + g + 1)
                                dve.wait_ge(z_ready, SUP * i + g + 1)
                                dve.tensor_copy(tiles(store["dt"], i, g), ps_b[g][:, INNER:ZD]).then_inc(dt_ready, 1)
                    for g in range(SUP):
                        dve.wait_ge(turned, SUP * i + g + 1)
                        dve.wait_ge(x_ready, SUP * i + g + 1)
                        dve.tensor_copy(tiles(store["b"], i, g), ps_b[g][:, INNER : INNER + STATE]).then_inc(b_ready, 1)
                    dve.wait_ge(g_mm, i + 1)
                    for g in range(SUP):
                        op = dve.tensor_tensor(tiles(store["g"], i, g), ps_a[1][:, P * g : P * g + P], w["inc"][:, :], ALU.mult)
                    op.then_inc(g_ready, 1)


def ssm_scan(nc, ident, m, backward, w, store, y_out, ssq):
    FAR = -120.0
    GX = HEADS * P
    with ExitStack() as stack:
        k = Scope(nc, stack, m.prefix + "s")
        small = k.sb("small", [P, 10, NT, HEADS])
        dtb = k.sb("dt_bias", [P, HEADS])
        alog = k.sb("a_log", [P, HEADS])
        aneg = k.sb("a_neg", [P, HEADS])
        dp = k.sb("dp", [P, HEADS])
        nw = k.sb("norm_w", [P, 2])
        ow_raw = k.sb("out_w_raw", [P, 2, D])
        ow = k.sb("out_w", [P, 2, D])
        strict = k.sb("strict", [P, P])
        an = k.sb("a_masked", [P, 2, HEADS, P])
        ex = k.sb("decay", [P, 2, HEADS, P])
        mt = k.sb("mt", [P, 2, HEADS, P])
        u = k.sb("u", [P, 2, HEADS, HEADDIM])
        ud = k.sb("u_decayed", [P, HEADS, HEADDIM])
        xd = k.sb("x_skip", [P, 2, HEADS, HEADDIM])
        bs = k.sb("b_staged", [P, STATE])
        cst = k.sb("c_staged", [STATE, P])
        st = k.sb("state", [STATE, INNER])
        eb = k.sb("edge_decay", [P, 2, HEADS])
        yi = k.sb("y_inter", [P, HEADS, HEADDIM])
        y1 = k.sb("y1", [P, 2, INNER])
        y2 = k.sb("y2", [P, 2, INNER])
        y3 = k.sb("y3", [P, 2, INNER])
        sq = k.sb("squares", [P, 2, INNER])
        yT = k.sb("yT", [P, 2, 2, P])
        ps_d = [k.ps(f"ps_d{n}", [P, HEADS, P]) for n in range(2)]
        ps_y = [k.ps(f"ps_y{n}", [P, 512]) for n in range(2)]
        ps_e = k.ps("ps_e", [P, 512])
        ps_s = k.ps("ps_s", [P, 512])
        ps_t = [k.ps(f"ps_t{n}", [P, 512]) for n in range(2)]
        loaded, prep, a_sem = k.sem("loaded"), k.sem("prep"), k.sem("act_prep")
        masked_ready, d_mm, ex_ready = k.sem("a_masked_ready"), k.sem("d_mm"), k.sem("ex_ready")
        staged, edge_mm, edge_ready = k.sem("staged"), k.sem("edge_mm"), k.sem("edge_ready")
        u_ready, mt_ready, ud_ready = k.sem("u_ready"), k.sem("mt_ready"), k.sem("ud_ready")
        state_mm, state_ready, inter_mm, inter_ready = k.sem("state_mm"), k.sem("state_ready"), k.sem("inter_mm"), k.sem("inter_ready")
        y_mm, y1_ready, y2_ready, y3_ready = k.sem("y_mm"), k.sem("y1_ready"), k.sem("y2_ready"), k.sem("y3_ready")
        sq_ready, turned, yT_ready, out_mm, out_ready = (k.sem("sq_ready"), k.sem("turned"), k.sem("yT_ready"),
                                                         k.sem("out_mm"), k.sem("out_ready"))
        xd_ready = k.sem("xd_ready")
        NLOAD = 6
        order = (1, 0) if backward else (0, 1)

        def tile(q, b):
            return B * order[q] + b

        dt, a = small[:, 8, :, :], small[:, 9, :, :]
        with nc.Block() as block:

            @block.sync
            def _(sp):
                for dst, src in ((dtb[:, :], w["dt_bias"]), (alog[:, :], w["a_log"]), (dp[:, :], w["dp"]),
                                 (nw[:, :], w["norm_w"]), (ow_raw[:, :, :], w["out_w"]), (strict[:, :], w["strict"])):
                    sp.dma_start(dst, src).then_inc(loaded, 16)

            @block.gpsimd
            def _(pool):
                pool.wait_ge(prep, 9)
                pool.sem_inc(staged, 2)
                with pool.Fori(0, B) as b:
                    for q in range(2):
                        n = 2 * b + q
                        pool.wait_ge(d_mm, n + 1)
                        pool.tensor_tensor(an[:, q, :, :], bcast(w["inc"][:, :], HEADS, 1), bcast(a[:, tile(q, b), :], P, 2),
                                           ALU.mult).then_inc(masked_ready, 1)
                        if q == 0:
                            pool.wait_ge(state_mm, b + 1)
                            pool.tensor_copy(bs[:, :], store["b"][:, tile(0, b), :]).then_inc(staged, 1)
                        else:
                            pool.wait_ge(inter_mm, b + 1)
                            pool.tensor_copy(cst[:, :], store["c"][:, tile(1, b), :]).then_inc(staged, 1)

            @block.tensor
            def _(pe):
                pe.wait_ge(prep, 9)
                pe.sem_inc(d_mm, 2)
                pe.sem_inc(state_mm, 1)
                pe.sem_inc(inter_mm, 1)

                def decays(b, q):
                    n = 2 * b + q
                    pe.wait_ge(masked_ready, n + 1)
                    pe.wait_ge(ex_ready, n + 1)
                    pe.matmul(ps_d[q][:, :, :], strict[:, :], an[:, q, :, :], start=True, stop=True).then_inc(d_mm, 1)
                    pe.wait_ge(edge_ready, n + 1)
                    lhs = strict if q == 0 else w["inc"]
                    pe.matmul(ps_e[:, 0:HEADS], lhs[:, :], a[:, tile(q, b), :], start=True, stop=True).then_inc(edge_mm, 1)

                def product(b, q):
                    n = 2 * b + q
                    pe.wait_ge(mt_ready, n + 1)
                    pe.wait_ge(u_ready, n + 1)
                    pe.wait_ge(y1_ready, n + 1)
                    for h in range(HEADS):
                        mm = pe.matmul(ps_y[q][:, HEADDIM * h : HEADDIM * h + HEADDIM], mt[:, q, h, :], u[:, q, h, :], start=True, stop=True)
                    mm.then_inc(y_mm, 1)

                def carry(b, q):
                    pe.wait_ge(staged, 2 * b + q + 3)
                    if q == 0:
                        pe.wait_ge(ud_ready, b + 1)
                        pe.matmul(ps_s[0:STATE, 0:INNER], bs[:, :], ud[:, :, :], start=True, stop=True).then_inc(state_mm, 1)
                    else:
                        pe.wait_ge(state_ready, b + 1)
                        pe.matmul(ps_s[:, 0:INNER], cst[:, :], st[:, :], start=True, stop=True).then_inc(inter_mm, 1)

                def out(b, q):
                    n = 2 * b + q
                    pe.wait_ge(y3_ready, n + 1)
                    pe.wait_ge(out_ready, n + 1)
                    for c in range(2):
                        mm = pe.transpose(ps_t[q][:, P * c : P * c + P], y3[:, q, P * c : P * c + P], ident[:, :])
                    mm.then_inc(turned, 1)
                    pe.wait_ge(yT_ready, n + 1)
                    for c in range(2):
                        mm = pe.matmul(ps_t[q][:, INNER : INNER + D], yT[:, q, c, :], ow[:, c, :], start=(c == 0), stop=(c == 1))
                    mm.then_inc(out_mm, 1)

                with pe.Fori(0, B) as b:
                    decays(b, 0)
                    decays(b, 1)
                    carry(b, 0)
                    product(b, 0)
                    carry(b, 1)
                    product(b, 1)
                    out(b, 0)
                    out(b, 1)

            @block.scalar
            def _(act):
                act.wait_ge(loaded, 16 * NLOAD)
                act.activation(aneg[:, :], alog[:, :], ACT.Exp).then_inc(a_sem, 1)
                act.wait_ge(prep, 4)
                act.activation(small[:, 3, :, :], small[:, 2, :, :], ACT.Exp, scale=-1.0).then_inc(a_sem, 1)
                act.wait_ge(a_sem, 2)
                act.activation(small[:, 4, :, :], small[:, 3, :, :], ACT.Ln, bias=1.0).then_inc(a_sem, 1)
                act.wait_ge(a_sem, 3)
                act.sem_inc(ex_ready, 2)
                act.sem_inc(edge_ready, 1)

                def decays(b, q):
                    n = 2 * b + q
                    act.wait_ge(d_mm, n + 3)
                    act.activation(ex[:, q, :, :], ps_d[q][:, :, :], ACT.Exp).then_inc(ex_ready, 1)
                    act.wait_ge(edge_mm, n + 1)
                    act.activation(eb[:, q, :], ps_e[:, 0:HEADS], ACT.Exp).then_inc(edge_ready, 1)

                def finish(b, q):
                    n = 2 * b + q
                    t = tile(q, b)
                    act.wait_ge(y3_ready, n + 1)
                    act.activation(sq[:, q, :], y3[:, q, :], ACT.Square, accum_out=ssq[:, bass.ds(t, 1)]).then_inc(sq_ready, 1)
                    act.wait_ge(turned, n + 1)
                    act.activation(yT[:, q, :, :], ps_t[q][:, 0:INNER].rearrange("p (c j) -> p c j", c=2), ACT.Copy).then_inc(yT_ready, 1)
                    act.wait_ge(out_mm, n + 1)
                    act.activation(y_out[:, t, :], ps_t[q][:, INNER : INNER + D], ACT.Copy).then_inc(out_ready, 1)

                act.sem_inc(out_ready, 2)
                with act.Fori(0, B) as b:
                    decays(b, 0)
                    decays(b, 1)
                    act.wait_ge(state_mm, b + 2)
                    act.activation(st[:, :], ps_s[0:STATE, 0:INNER], ACT.Copy).then_inc(state_ready, 1)
                    finish(b, 0)
                    finish(b, 1)
                act.wait_ge(out_ready, NT + 2)

            @block.vector
            def _(dve):
                dve.wait_ge(loaded, 16 * NLOAD)
                s = lambda n: small[:, n, :, :]
                dve.tensor_tensor(s(0), store["dt"][:, :, :], bcast(dtb[:, :], NT, 1), ALU.add).then_inc(prep, 1)
                dve.wait_ge(prep, 1)
                dve.tensor_scalar(s(1), s(0), -1.0, None, ALU.mult).then_inc(prep, 1)
                dve.tensor_scalar(s(5), s(0), 0.0, None, ALU.max).then_inc(prep, 1)
                dve.wait_ge(prep, 3)
                dve.tensor_tensor(s(2), s(0), s(1), ALU.max).then_inc(prep, 1)
                for c in range(2):
                    dve.tensor_scalar(ow[:, c, :], ow_raw[:, c, :], nw[:, c : c + 1], None, ALU.mult).then_inc(prep, 1)
                dve.wait_ge(a_sem, 3)
                dve.tensor_tensor(dt, s(4), s(5), ALU.add).then_inc(prep, 1)
                dve.wait_ge(prep, 7)
                dve.scalar_tensor_tensor(s(6), dt, -1.0, bcast(aneg[:, :], NT, 1), ALU.mult, ALU.mult).then_inc(prep, 1)
                dve.wait_ge(prep, 8)
                dve.tensor_scalar(a, s(6), FAR, None, ALU.max).then_inc(prep, 1)
                dve.wait_ge(prep, 9)
                dve.sem_inc(y1_ready, 2)

                def inputs(b, q):
                    t = tile(q, b)
                    view = store["x"][:, t, :].rearrange("p (h d) -> p h d", h=HEADS)
                    dve.tensor_tensor(u[:, q, :, :], view, bcast(dt[:, t, :], HEADDIM, 2), ALU.mult).then_inc(u_ready, 1)
                    dve.tensor_tensor(xd[:, q, :, :], view, bcast(dp[:, :], HEADDIM, 2), ALU.mult).then_inc(xd_ready, 1)
                    if q == 0:
                        dve.wait_ge(edge_ready, 2 * b + 2)
                        dve.wait_ge(u_ready, 2 * b + 1)
                        dve.tensor_tensor(ud[:, :, :], u[:, 0, :, :], bcast(eb[:, 0, :], HEADDIM, 2), ALU.mult).then_inc(ud_ready, 1)
                    dve.wait_ge(ex_ready, 2 * b + q + 3)
                    dve.tensor_tensor(mt[:, q, :, :], ex[:, q, :, :], bcast(store["g"][:, t, :], HEADS, 1), ALU.mult).then_inc(mt_ready, 1)

                def gate(b, q):
                    n, t = 2 * b + q, tile(q, b)
                    flat = lambda ap: ap.rearrange("p h d -> p (h d)")
                    skip = flat(xd[:, q, :, :])
                    if q == 1:
                        dve.wait_ge(inter_mm, b + 2)
                        dve.wait_ge(edge_ready, 2 * b + 3)
                        dve.tensor_tensor(yi[:, :, :], ps_s[:, 0:INNER].rearrange("p (h d) -> p h d", h=HEADS),
                                          bcast(eb[:, 1, :], HEADDIM, 2), ALU.mult).then_inc(inter_ready, 1)
                        dve.wait_ge(inter_ready, 2 * b + 1)
                        dve.wait_ge(xd_ready, n + 1)
                        dve.tensor_tensor(y1[:, 0, :], flat(yi[:, :, :]), skip, ALU.add).then_inc(inter_ready, 1)
                        dve.wait_ge(inter_ready, 2 * b + 2)
                        skip = y1[:, 0, :]
                    dve.wait_ge(y_mm, n + 1)
                    dve.wait_ge(xd_ready, n + 1)
                    dve.tensor_tensor(y2[:, q, :], ps_y[q][:, 0:INNER], skip, ALU.add).then_inc(y1_ready, 1)
                    dve.wait_ge(y1_ready, n + 3)
                    dve.tensor_tensor(y3[:, q, :], y2[:, q, :], store["z"][:, t, :], ALU.mult).then_inc(y3_ready, 1)

                with dve.Fori(0, B) as b:
                    inputs(b, 0)
                    inputs(b, 1)
                    gate(b, 0)
                    gate(b, 1)


def state_space(nc, x, ident, dirs):
    with ExitStack() as stack:
        m = Scope(nc, stack, "ss")
        norm = Norm(m)
        norm_statistics(nc, x, norm)
        y_out = [m.sb(f"y_out{n}", [P, NT, D]) for n in range(2)]
        ssq = [m.sb(f"ssq{n}", [P, NT]) for n in range(2)]
        inc = m.sb("inclusive", [P, P])
        store = {
            "z": m.sb("silu_z", [P, NT, INNER]), "x": m.sb("x_tok", [P, NT, INNER]), "b": m.sb("b_tok", [P, NT, STATE]),
            "c": m.sb("c_feat", [STATE, NT, P]), "g": m.sb("scores", [P, NT, P]), "dt": m.sb("dt_raw", [P, NT, HEADS]),
        }
        inc_loaded = m.sem("inc_loaded")
        for n, w in enumerate(dirs):
            with nc.Block() as block:

                @block.sync
                def _(sp):
                    sp.dma_start(inc[:, :], w["inclusive"]).then_inc(inc_loaded, 16)
                    sp.wait_ge(inc_loaded, 16 * n + 16)

            w = dict(w, inc=inc)
            k = Scope(nc, stack, f"ss{n}")
            ssm_inputs(nc, x, ident, norm, k, n == 1, w, store)
            ssm_scan(nc, ident, k, n == 1, w, store, y_out[n], ssq[n])

        mean = m.sb("mean_square", [P, 2, NT])
        root = m.sb("root", [P, 2, NT])
        r = m.sb("rms", [P, 2, NT])
        meant, rooted, inv, added = m.sem("meant"), m.sem("rooted"), m.sem("inverted"), m.sem("added")
        with nc.Block() as block:

            @block.scalar
            def _(act):
                act.wait_ge(meant, 2)
                act.activation(root[:, :, :], mean[:, :, :], ACT.Sqrt).then_inc(rooted, 1)

            @block.vector
            def _(dve):
                for n in range(2):
                    dve.tensor_scalar(mean[:, n, :], ssq[n][:, :], 1.0 / INNER, EPS, ALU.mult, ALU.add).then_inc(meant, 1)
                dve.wait_ge(rooted, 1)
                dve.reciprocal(r[:, :, :], root[:, :, :]).then_inc(inv, 1)
                dve.wait_ge(inv, 1)
                for n in range(2):
                    with dve.Fori(0, NT) as t:
                        dve.scalar_tensor_tensor(x[:, t, :], y_out[n][:, t, :], r[:, n, bass.ds(t, 1)], x[:, t, :],
                                                 ALU.mult, ALU.add).then_inc(added, 1)
                    dve.wait_ge(added, NT * (n + 1))


def cross_attention(nc, x, ident, ctxT_dram, ctx2T_dram, mask_dram, wq_dram, wk_dram, wv_dram, wo_dram):
    H, HD, K = 16, 64, 64
    HP = H // 2
    SCALE = 1.0 / HD**0.5
    with ExitStack() as stack:
        m = Scope(nc, stack, "xa")
        norm = Norm(m)
        mask = m.sb("mask", [P, NT, K])
        wq = m.sb("wq", [D, H * HD])
        wo = m.sb("wo", [P, HP, D])
        keys = m.sb("keys", [P, HP, B, K])
        vals = m.sb("vals", [P, B, HP, HD])
        kblock = m.sb("kblock", [P, HP, 2, K])
        vblock = m.sb("vblock", [P, HP, 2, HD])
        load_done = m.sem("loaded")
        zeroed = m.sem("blocks_zeroed")
        with ExitStack() as inner:
            k = Scope(nc, inner, "xk")
            ctxT = k.sb("ctxT", [D, B * K])
            ctx2T = k.sb("ctx2T", [D, B, 2 * K])
            wk = k.sb("wk", [D, H * HD])
            wv = k.sb("wv", [D, H * HD])
            ps_k = [k.ps(f"ps_k{n}", [P, 8, K]) for n in range(4)]
            ps_v = [k.ps(f"ps_v{n}", [P, HP, 2, HD]) for n in range(2)]
            key_mm, key_ready = k.sem("key_mm"), k.sem("key_ready")
            val_mm, val_low, val_high = k.sem("val_mm"), k.sem("val_low"), k.sem("val_high")
            ctx_copied, raw_masked = k.sem("ctx_copied"), k.sem("masked")
            NLOAD = 7
            with nc.Block() as block:

                @block.sync
                def _(sp):
                    for dst, src in ((ctxT[:, :], ctxT_dram), (wk[:, :], wk_dram), (ctx2T[:, :, :], ctx2T_dram), (wv[:, :], wv_dram),
                                     (mask[:, :, :], mask_dram), (wq[:, :], wq_dram),
                                     (wo[:, :, :], wo_dram.rearrange("(c p) n -> p c n", p=P))):
                        sp.dma_start(dst, src).then_inc(load_done, 16)

                @block.gpsimd
                def _(pool):
                    pool.memset(kblock[:, :, :, :], 0.0).then_inc(zeroed, 1)
                    pool.memset(vblock[:, :, :, :], 0.0).then_inc(zeroed, 1)

                @block.tensor
                def _(pe):
                    pe.wait_ge(load_done, 16 * NLOAD)
                    for c in range(HP):
                        for n in range(2):
                            f = 2 * c + n
                            if f >= 4:
                                pe.wait_ge(key_ready, f - 3)
                            pe.matmul(ps_k[f % 4][:, :, :], wk[:, P * c : P * c + P], ctxT[:, 512 * n : 512 * n + 512],
                                      start=True, stop=True).then_inc(key_mm, 1)
                    for b in range(B):
                        if b >= 2:
                            pe.wait_ge(val_low, b - 1)
                            pe.wait_ge(val_high, b - 1)
                        for n in range(2):
                            mm = pe.matmul(ps_v[b % 2][:, 4 * n : 4 * n + 4, :, :], ctx2T[:, b, :], wv[:, 512 * n : 512 * n + 512],
                                           start=True, stop=True)
                        mm.then_inc(val_mm, 1)

                @block.scalar
                def _(act):
                    norm.act(act)
                    for f in range(2 * HP):
                        act.wait_ge(key_mm, f + 1)
                        act.activation(keys[:, f // 2, 8 * (f % 2) : 8 * (f % 2) + 8, :], ps_k[f % 4][:, :, :], ACT.Copy).then_inc(key_ready, 1)
                    for b in range(B):
                        act.wait_ge(val_mm, b + 1)
                        act.activation(vals[0:K, b, :, :], ps_v[b % 2][0:K, :, 0, :], ACT.Copy).then_inc(val_low, 1)

                @block.vector
                def _(dve):
                    norm.dve(dve, x)
                    dve.wait_ge(load_done, 16 * NLOAD)
                    dve.tensor_scalar(mask[:, :, :], mask[:, :, :], -1.0e9, None, ALU.mult).then_inc(raw_masked, 1)
                    for b in range(B):
                        dve.wait_ge(val_mm, b + 1)
                        dve.tensor_copy(vals[K:P, b, :, :], ps_v[b % 2][K:P, :, 1, :]).then_inc(val_high, 1)

        xn = m.sb("xn", [P, 2, D])
        xnT = m.sb("xnT", [D, 2 * P])
        qT = m.sb("qT", [P, HP, 2 * P])
        logits = m.sb("logits", [P, 2, H, K])
        rowmax = m.sb("rowmax", [P, 2, H])
        shifted = m.sb("shifted", [P, 2, H, K])
        probs = m.sb("probs", [P, 2, H, K])
        rowsum = m.sb("rowsum", [P, 2, H])
        rinv = m.sb("rinv", [P, 2, H])
        normed = m.sb("normed", [P, 2, H * K])
        probsT = m.sb("probsT", [P, HP, P])
        oT = m.sb("oT", [P, 2, HP, P])
        ps_m = [m.ps(f"ps_m{n}", [P, 512]) for n in range(2)]
        ps_s = [m.ps(f"ps_s{n}", [P, H, K]) for n in range(2)]
        ps_a = [m.ps(f"ps_a{n}", [P, HP // 2, P]) for n in range(2)]
        xn_ready, xn_transposed, xnT_ready = m.sem("xn_ready"), m.sem("xn_transposed"), m.sem("xnT_ready")
        q_mm, q_ready = m.sem("q_mm"), m.sem("q_ready")
        kblock_ready, vblock_ready = m.sem("kblock_ready"), m.sem("vblock_ready")
        scored, logits_ready, max_ready = m.sem("scored"), m.sem("logits_ready"), m.sem("max_ready")
        shifted_ready, exp_ready = m.sem("shifted_ready"), m.sem("exp_ready")
        sum_ready, rinv_ready, normed_ready = m.sem("sum_ready"), m.sem("rinv_ready"), m.sem("normed_ready")
        probs_transposed, probsT_ready = m.sem("probs_transposed"), m.sem("probsT_ready")
        attended, oT_ready, projected, x_out = m.sem("attended"), m.sem("oT_ready"), m.sem("projected"), m.sem("x_out")
        QF = HP // 2

        with nc.Block() as block:

            @block.gpsimd
            def _(pool):
                def stage(b):
                    for e in range(2):
                        rows = slice(K * e, K * e + K)
                        pool.tensor_copy(kblock[rows, :, e, :], keys[rows, :, b, :]).then_inc(kblock_ready, 1)

                def stage_values(b):
                    for e in range(2):
                        rows = slice(K * e, K * e + K)
                        pool.tensor_copy(vblock[rows, :, e, :], vals[rows, b, :, :]).then_inc(vblock_ready, 1)

                stage(0)
                stage_values(0)
                with pool.Fori(1, B) as b:
                    pool.wait_ge(scored, 2 * b)
                    stage(b)
                    pool.wait_ge(attended, 4 * b)
                    stage_values(b)

            @block.tensor
            def _(pe):
                def turn_x(b):
                    pe.wait_ge(xn_ready, 2 * b + 2)
                    for u in range(2):
                        mm = pe.transpose(ps_m[0][:, P * u : P * u + P], xn[:, u, :], ident[:, :])
                    mm.then_inc(xn_transposed, 1)

                def queries(b, first):
                    if first:
                        pe.wait_ge(xnT_ready, b + 1)
                    for f in range(1) if first else range(1, QF):
                        if f >= 2:
                            pe.wait_ge(q_ready, QF * b + f - 1)
                        for c in range(2):
                            w = 2 * f + c
                            mm = pe.matmul(ps_m[(f + 1) % 2][:, 256 * c : 256 * c + 256], wq[:, P * w : P * w + P], xnT[:, :],
                                           start=True, stop=True)
                        mm.then_inc(q_mm, 1)

                def scores(b, u):
                    if u == 0:
                        pe.wait_ge(q_ready, QF * b + QF)
                        pe.wait_ge(kblock_ready, 2 * b + 2)
                    for c in range(HP):
                        mm = pe.matmul(ps_s[u][:, 2 * c : 2 * c + 2, :], qT[:, c, P * u : P * u + P], kblock[:, c, :, :],
                                       start=True, stop=True)
                    mm.then_inc(scored, 1)

                def turn_probs(b, u):
                    pe.wait_ge(normed_ready, 2 * b + u + 1)
                    for c in range(HP):
                        mm = pe.transpose(ps_a[c // 4][:, c % 4, :], normed[:, u, P * c : P * c + P], ident[:, :])
                        if c % 4 == 3:
                            mm.then_inc(probs_transposed, 1)

                def attend(b, u):
                    pe.wait_ge(vblock_ready, 2 * b + 2)
                    for n in range(2):
                        pe.wait_ge(probsT_ready, 2 * (2 * b + u) + n + 1)
                        for c in range(4 * n, 4 * n + 4):
                            mm = pe.matmul(ps_a[n][:, c % 4, :], vblock[:, c, :, :], probsT[:, c, :], start=True, stop=True)
                        mm.then_inc(attended, 1)

                def project(b, u):
                    pe.wait_ge(oT_ready, 2 * (2 * b + u) + 2)
                    for c in range(HP):
                        mm = pe.matmul(ps_m[(u + 1) % 2][:, 0:D], oT[:, u, c, :], wo[:, c, :], start=(c == 0), stop=(c == HP - 1))
                    mm.then_inc(projected, 1)

                turn_x(0)
                queries(0, True)
                queries(0, False)
                scores(0, 0)
                scores(0, 1)
                with pe.Fori(1, B) as b:
                    turn_x(b)
                    turn_probs(b - 1, 0)
                    queries(b, True)
                    attend(b - 1, 0)
                    queries(b, False)
                    pe.wait_ge(oT_ready, 4 * b - 2)
                    turn_probs(b - 1, 1)
                    scores(b, 0)
                    attend(b - 1, 1)
                    project(b - 1, 0)
                    scores(b, 1)
                    project(b - 1, 1)
                    pe.wait_ge(oT_ready, 4 * b)
                    pe.wait_ge(x_out, 2 * b)
                turn_probs(B - 1, 0)
                attend(B - 1, 0)
                pe.wait_ge(oT_ready, 4 * B - 2)
                turn_probs(B - 1, 1)
                attend(B - 1, 1)
                project(B - 1, 0)
                project(B - 1, 1)

            @block.scalar
            def _(act):
                def copy_x(b):
                    act.wait_ge(xn_transposed, b + 1)
                    act.activation(xnT[:, :], ps_m[0][:, 0:256], ACT.Copy).then_inc(xnT_ready, 1)

                def copy_q(b, fills):
                    for f in fills:
                        act.wait_ge(q_mm, QF * b + f + 1)
                        act.activation(qT[:, 2 * f : 2 * f + 2, :], ps_m[(f + 1) % 2][:, :].rearrange("p (c j) -> p c j", c=2),
                                       ACT.Copy, scale=SCALE).then_inc(q_ready, 1)

                def exp(b, u):
                    act.wait_ge(shifted_ready, 2 * b + u + 1)
                    act.activation(probs[:, u, :, :], shifted[:, u, :, :], ACT.Exp).then_inc(exp_ready, 1)

                def copy_probs(b, u):
                    for n in range(2):
                        act.wait_ge(probs_transposed, 2 * (2 * b + u) + n + 1)
                        act.activation(probsT[:, 4 * n : 4 * n + 4, :], ps_a[n][:, :, :], ACT.Copy).then_inc(probsT_ready, 1)

                def copy_o(b, u):
                    for n in range(2):
                        act.wait_ge(attended, 2 * (2 * b + u) + n + 1)
                        act.activation(oT[:, u, 4 * n : 4 * n + 4, :], ps_a[n][:, :, :], ACT.Copy).then_inc(oT_ready, 1)

                copy_x(0)
                copy_q(0, range(QF))
                exp(0, 0)
                exp(0, 1)
                with act.Fori(1, B) as b:
                    copy_x(b)
                    copy_probs(b - 1, 0)
                    copy_q(b, range(1))
                    copy_o(b - 1, 0)
                    copy_q(b, range(1, QF))
                    copy_probs(b - 1, 1)
                    copy_o(b - 1, 1)
                    exp(b, 0)
                    exp(b, 1)
                copy_probs(B - 1, 0)
                copy_o(B - 1, 0)
                copy_probs(B - 1, 1)
                copy_o(B - 1, 1)

            @block.vector
            def _(dve):
                def norm_x(b):
                    for u in range(2):
                        norm.tile(dve, xn[:, u, :], x, B * u + b).then_inc(xn_ready, 1)

                def shift(b, u):
                    n = 2 * b + u + 1
                    dve.wait_ge(scored, n)
                    dve.tensor_tensor(logits[:, u, :, :], ps_s[u][:, :, :], bcast(mask[:, B * u + b, :], H, 1),
                                      ALU.add).then_inc(logits_ready, 1)
                    dve.wait_ge(logits_ready, n)
                    dve.tensor_reduce(rowmax[:, u, :], logits[:, u, :, :], AX, ALU.max).then_inc(max_ready, 1)
                    dve.wait_ge(max_ready, n)
                    dve.tensor_tensor(shifted[:, u, :, :], logits[:, u, :, :], bcast(rowmax[:, u, :], K, 2),
                                      ALU.subtract).then_inc(shifted_ready, 1)

                def divide(b, u):
                    n = 2 * b + u + 1
                    dve.wait_ge(exp_ready, n)
                    dve.tensor_reduce(rowsum[:, u, :], probs[:, u, :, :], AX, ALU.add).then_inc(sum_ready, 1)
                    dve.wait_ge(sum_ready, n)
                    dve.reciprocal(rinv[:, u, :], rowsum[:, u, :]).then_inc(rinv_ready, 1)
                    dve.wait_ge(rinv_ready, n)
                    dve.tensor_tensor(normed[:, u, :].rearrange("p (h k) -> p h k", h=H), probs[:, u, :, :],
                                      bcast(rinv[:, u, :], K, 2), ALU.mult).then_inc(normed_ready, 1)

                def add(b, u):
                    dve.wait_ge(projected, 2 * b + u + 1)
                    t = B * u + b
                    dve.tensor_tensor(x[:, t, :], x[:, t, :], ps_m[(u + 1) % 2][:, 0:D], ALU.add).then_inc(x_out, 1)

                norm_x(0)
                shift(0, 0)
                shift(0, 1)
                divide(0, 0)
                divide(0, 1)
                with dve.Fori(1, B) as b:
                    norm_x(b)
                    shift(b, 0)
                    add(b - 1, 0)
                    shift(b, 1)
                    add(b - 1, 1)
                    divide(b, 0)
                    divide(b, 1)
                add(B - 1, 0)
                add(B - 1, 1)
                dve.wait_ge(x_out, 2 * B)


def threshold_experts(nc, x, ident, gw_dram, gb_dram, ew_dram, eb_dram):
    E, THRESHOLD = 8, 0.1
    with ExitStack() as stack:
        m = Scope(nc, stack, "te")
        gw = m.sb("gate_w", [D, E])
        gb = m.sb("gate_b", [P, E])
        ew = m.sb("expert_w", [D, E * D])
        eb = m.sb("expert_b", [E, D])
        norm = Norm(m)
        xn = m.sb("xn", [P, SUP, D])
        xnT = m.sb("xnT", [D, SUP * P])
        gt = m.sb("gate", [P, 8, SUP, E])
        gs = m.sb("gate_stats", [P, 6, SUP])
        weight = m.sb("weight", [P, SUP, E])
        wT = m.sb("weightT", [E, SUP * P])
        acc = m.sb("acc", [P, 2, SUP, D])
        both = m.sb("both", [P, SUP, D])
        ps_t = m.ps("ps_t", [P, 512])
        ps_l = m.ps("ps_l", [P, 512])
        ps_w = m.ps("ps_w", [P, 512])
        ps_b = m.ps("ps_b", [P, SUP, D])
        ps_e = [m.ps(f"ps_e{n}", [P, E, D]) for n in range(2)]
        loaded = m.sem("loaded")
        xn_ready, xn_transposed, xnT_ready = m.sem("xn_ready"), m.sem("xn_transposed"), m.sem("xnT_ready")
        logits_mm, gate_step, gate_exp, weighted = m.sem("logits_mm"), m.sem("gate_step"), m.sem("gate_exp"), m.sem("weighted")
        expert_mm, acc_step = m.sem("expert_mm"), m.sem("acc_step")
        turned, wT_ready, bias_mm, x_step = m.sem("turned"), m.sem("wT_ready"), m.sem("bias_mm"), m.sem("x_step")
        NLOAD, GSTEPS = 4, 11
        ACCS = E * SUP

        with nc.Block() as block:

            @block.sync
            def _(sp):
                for dst, src in ((gw, gw_dram), (gb, gb_dram), (ew, ew_dram), (eb, eb_dram)):
                    sp.dma_start(dst[:, :], src).then_inc(loaded, 16)

            @block.tensor
            def _(pe):
                pe.wait_ge(loaded, 16 * NLOAD)
                with pe.Fori(0, NSUP) as i:
                    pe.wait_ge(xn_ready, SUP * i + SUP)
                    for g in range(SUP):
                        mm = pe.transpose(ps_t[:, P * g : P * g + P], xn[:, g, :], ident[:, :])
                    mm.then_inc(xn_transposed, 1)
                    pe.wait_ge(xnT_ready, i + 1)
                    for g in range(SUP):
                        mm = pe.matmul(ps_l[:, E * g : E * g + E], xnT[:, P * g : P * g + P], gw[:, :], start=True, stop=True)
                    mm.then_inc(logits_mm, 1)
                    for g in range(SUP):
                        if g < 2:
                            pe.wait_ge(acc_step, ACCS * i + 1)
                        if g >= 2:
                            pe.wait_ge(acc_step, ACCS * i + E * (g - 1) + 1)
                        for n in range(2):
                            mm = pe.matmul(ps_e[g % 2][:, 4 * n : 4 * n + 4, :], xnT[:, P * g : P * g + P],
                                           ew[:, 512 * n : 512 * n + 512], start=True, stop=True)
                        mm.then_inc(expert_mm, 1)
                        if g == 1:
                            pe.wait_ge(weighted, i + 1)
                            for t in range(SUP):
                                mm = pe.transpose(ps_w[0:E, P * t : P * t + P], weight[:, t, :], ident[:, :])
                            mm.then_inc(turned, 1)
                    pe.wait_ge(wT_ready, i + 1)
                    for t in range(SUP):
                        mm = pe.matmul(ps_b[:, t, :], wT[:, P * t : P * t + P], eb[:, :], start=True, stop=True)
                    mm.then_inc(bias_mm, 1)

            @block.scalar
            def _(act):
                norm.act(act)
                with act.Fori(0, NSUP) as i:
                    act.wait_ge(xn_transposed, i + 1)
                    act.activation(xnT[:, :], ps_t[:, :], ACT.Copy).then_inc(xnT_ready, 1)
                    act.wait_ge(gate_step, GSTEPS * i + 4)
                    act.activation(gt[:, 2, :, :], gt[:, 1, :, :], ACT.Exp).then_inc(gate_exp, 1)
                    act.wait_ge(turned, i + 1)
                    act.activation(wT[:, :], ps_w[0:E, :], ACT.Copy).then_inc(wT_ready, 1)

            @block.vector
            def _(dve):
                norm.dve(dve, x)
                dve.wait_ge(loaded, 16 * NLOAD)
                dve.sem_inc(acc_step, 1)
                dve.sem_inc(x_step, 1)
                dve.sem_inc(gate_step, 1)
                with dve.Fori(0, NSUP) as i:
                    dve.wait_ge(x_step, 3 * i + 1)
                    for g in range(SUP):
                        norm.tile(dve, xn[:, g, :], x, SUP * i + g).then_inc(xn_ready, 1)

                    g_ = lambda n: gt[:, n, :, :]
                    done = lambda n: dve.wait_ge(gate_step, GSTEPS * i + n + 1)
                    dve.wait_ge(logits_mm, i + 1)
                    dve.tensor_tensor(g_(0), ps_l[:, 0 : SUP * E].rearrange("p (g e) -> p g e", e=E),
                                      bcast(gb[:, :], SUP, 1), ALU.add).then_inc(gate_step, 1)
                    done(1)
                    dve.tensor_reduce(gs[:, 0, :], g_(0), AX, ALU.max).then_inc(gate_step, 1)
                    done(2)
                    dve.tensor_tensor(g_(1), g_(0), bcast(gs[:, 0, :], E, 2), ALU.subtract).then_inc(gate_step, 1)
                    dve.wait_ge(gate_exp, i + 1)
                    dve.tensor_reduce(gs[:, 1, :], g_(2), AX, ALU.add).then_inc(gate_step, 1)
                    done(4)
                    dve.reciprocal(gs[:, 2, :], gs[:, 1, :]).then_inc(gate_step, 1)
                    done(5)
                    dve.tensor_tensor(g_(3), g_(2), bcast(gs[:, 2, :], E, 2), ALU.mult).then_inc(gate_step, 1)
                    done(6)
                    dve.scalar_tensor_tensor(g_(4), g_(3), THRESHOLD, g_(3), ALU.is_ge, ALU.mult).then_inc(gate_step, 1)
                    done(7)
                    dve.tensor_reduce(gs[:, 3, :], g_(4), AX, ALU.add).then_inc(gate_step, 1)
                    done(8)
                    dve.scalar_tensor_tensor(gs[:, 4, :], gs[:, 3, :], 0.0, gs[:, 3, :], ALU.is_equal, ALU.add).then_inc(gate_step, 1)
                    done(9)
                    dve.reciprocal(gs[:, 5, :], gs[:, 4, :]).then_inc(gate_step, 1)
                    done(10)
                    dve.tensor_tensor(weight[:, :, :], g_(4), bcast(gs[:, 5, :], E, 2), ALU.mult).then_inc(weighted, 1)
                    dve.wait_ge(weighted, i + 1)
                    dve.sem_inc(gate_step, 1)

                    for g in range(SUP):
                        dve.wait_ge(expert_mm, SUP * i + g + 1)
                        for e in range(E):
                            out, src = acc[:, e % 2, g, :], ps_e[g % 2][:, e, :]
                            if e < 2:
                                op = dve.tensor_scalar(out, src, weight[:, g, e : e + 1], None, ALU.mult)
                            else:
                                dve.wait_ge(acc_step, ACCS * i + E * g + e)
                                op = dve.scalar_tensor_tensor(out, src, weight[:, g, e : e + 1], out, ALU.mult, ALU.add)
                            op.then_inc(acc_step, 1)
                    dve.wait_ge(acc_step, ACCS * i + ACCS + 1)
                    dve.tensor_tensor(both[:, :, :], acc[:, 0, :, :], acc[:, 1, :, :], ALU.add).then_inc(x_step, 1)
                    dve.wait_ge(x_step, 3 * i + 2)
                    dve.wait_ge(bias_mm, i + 1)
                    dve.tensor_tensor(acc[:, 0, :, :], both[:, :, :], ps_b[:, :, :], ALU.add).then_inc(x_step, 1)
                    dve.wait_ge(x_step, 3 * i + 3)
                    view = x[:, bass.ds(SUP * i, SUP), :]
                    dve.tensor_tensor(view, view, acc[:, 0, :, :], ALU.add).then_inc(x_step, 1)
                dve.wait_ge(x_step, 3 * NSUP + 1)


def decoder(nc, a, x1_dram, out_dram):
    take = lambda *names: [a[n] for n in names]
    self_attention(nc, *take("x", "ident", "sa_mask", "sa_wq", "sa_wkv", "sa_bq", "sa_bk", "sa_bv", "sa_wp", "sa_bp"), x1_dram)
    with ExitStack() as stack:
        m = Scope(nc, stack, "g")
        x = m.sb("x", [P, NT, D])
        ident = m.sb("ident", [P, P])
        load_x(nc, x, ident, x1_dram, a["ident"])
        with ExitStack() as inner:
            bias = Scope(nc, inner, "gb").sb("bias", [P, NT, 64])
            count_indices(nc, *take("idx", "bins"), bias)
            gathered_attention(nc, x, bias, ident, *take("ctxT", "ga_downT", "ga_upT", "ga_qT", "ga_outT", "ga_hmask", "ga_pmask"))
        gated_experts(nc, x, ident, *take("ge_scale", "ge_bias", "ge_gateT", "ge_wg", "ge_wu", "ge_wd", "ge_lower"))
        dirs = [dict({n[2:]: v for n, v in a.items() if n[:2] == d + "_"}, pick=a["pick"]) for d in "fb"]
        state_space(nc, x, ident, dirs)
        cross_attention(nc, x, ident, *take("ctxT", "ctx2T", "xa_mask", "xa_wq", "xa_wk", "xa_wv", "xa_wo"))
        threshold_experts(nc, x, ident, *take("te_gw", "te_gb", "te_ew", "te_eb"))
        store_x(nc, x, out_dram)


def kernel(**inp):
    import numpy as np
    import concourse.bacc as bacc
    from concourse.bass_utils import run_bass_kernel_spmd as run

    c = np.ascontiguousarray
    rows = lambda v: c(np.broadcast_to(v[None], (P,) + v.shape))
    cols = lambda v: c(v.reshape(-1, P).T)
    K = 64
    k = np.arange(P)
    pick = np.zeros((P, P), np.float32)
    pick[64 + np.arange(64), np.arange(64)] = 1.0
    ctxT = c(inp["ctx_1024"].reshape(B * K, D).T)
    tiles = lambda v: c(v.reshape(B, 2, P, K).transpose(2, 1, 0, 3))
    arr = {
        "x": c(inp["x"].transpose(1, 0, 2).reshape(TOK, D)),
        "ident": np.eye(P, dtype=np.float32), "pick": pick,
        "sa_mask": np.where((k[:, None] // B) % 2 == np.arange(32)[None] // B, 0.0, -1e30).astype(np.float32),
        "sa_wq": inp["L0_attn_Wq"], "sa_wkv": inp["L0_attn_Wkv"], "sa_bq": cols(inp["L0_attn_bq"]),
        "sa_bk": cols(inp["L0_attn_bkv"][:1024]), "sa_bv": cols(inp["L0_attn_bkv"][1024:]),
        "sa_wp": inp["L0_attn_Wp"], "sa_bp": inp["L0_attn_bp"].reshape(1, D),
        "idx": tiles(inp["itok_BxSx64_0_2047"]).reshape(P, NT * K), "bins": rows(np.arange(K, dtype=np.float32)),
        "ctxT": ctxT, "ctx2T": c(np.broadcast_to(ctxT.reshape(D, B, 1, K), (D, B, 2, K)).reshape(D, B, 2 * K)),
        "ga_downT": c(inp["L0_xattn_W_kv_down"].T), "ga_upT": c(inp["L0_xattn_W_kv_up"].T),
        "ga_qT": c(inp["L0_xattn_W_q"].T), "ga_outT": c(inp["L0_xattn_W_out"].T),
        "ga_hmask": (k[:, None] // 8 == np.arange(16)[None]).astype(np.float32),
        "ga_pmask": (k[:, None] // 64 == np.arange(2)[None]).astype(np.float32),
        "ge_scale": c(inp["L0_ffn_ln_scale"].reshape(D, 1)), "ge_bias": c(inp["L0_ffn_ln_bias"].reshape(D, 1)),
        "ge_gateT": c(inp["L0_ffn_gate_w"].T),
        "ge_wg": c(np.concatenate([inp["L0_ffn_sWg"][None], inp["L0_ffn_Wg"]]).transpose(1, 0, 2)),
        "ge_wu": c(np.concatenate([inp["L0_ffn_sWu"][None], inp["L0_ffn_Wu"]]).transpose(1, 0, 2)),
        "ge_wd": c(np.concatenate([inp["L0_ffn_sWd"][None], inp["L0_ffn_Wd"]]).reshape(9, 2, P, D).transpose(2, 0, 1, 3)),
        "ge_lower": rows(np.tril(np.ones((8, 8), np.float32), -1)),
        "f_strict": (k[:, None] > k[None]).astype(np.float32), "b_strict": (k[:, None] < k[None]).astype(np.float32),
        "f_inclusive": (k[:, None] <= k[None]).astype(np.float32), "b_inclusive": (k[:, None] >= k[None]).astype(np.float32),
        "xa_mask": tiles(inp["mask_Bx1xSxS2_fk1"]).reshape(P, NT, K),
        "xa_wq": inp["L1_xattn_W_q"], "xa_wk": inp["L1_xattn_W_k"], "xa_wv": inp["L1_xattn_W_v"], "xa_wo": inp["L1_xattn_W_o"],
        "te_gw": inp["L1_ffn_gate_w"], "te_gb": rows(inp["L1_ffn_gate_b"]),
        "te_ew": c(inp["L1_ffn_expert_w"].transpose(1, 0, 2).reshape(D, 8 * D)), "te_eb": inp["L1_ffn_expert_b"],
    }
    for d in "fb":
        g = lambda n: inp[f"L1_attn_{d}_{n}"]
        arr.update({
            f"{d}_in": c(g("in_w").T), f"{d}_conv_w": c(g("conv_w").reshape(3, P, 4).transpose(1, 0, 2)),
            f"{d}_conv_b": cols(g("conv_b")), f"{d}_dt_bias": rows(g("dt_bias")), f"{d}_a_log": rows(g("A_log")),
            f"{d}_dp": rows(g("Dp")), f"{d}_norm_w": cols(g("norm_w")),
            f"{d}_out_w": c(g("out_w").T.reshape(2, P, D).transpose(1, 0, 2)),
        })
    nc = bacc.Bacc("TRN2", target_bir_lowering=False, num_devices=1)
    a = {n: nc.dram_tensor(f"in_{n}", v.shape, mybir.dt.from_np(v.dtype), kind="ExternalInput").ap() for n, v in arr.items()}
    x1 = nc.dram_tensor("x1", (TOK, D), F32, kind="Internal").ap()
    out = nc.dram_tensor("out", (B, S, D), F32, kind="ExternalOutput").ap()
    decoder(nc, a, x1, out)
    return run(nc, [{f"in_{n}": v for n, v in arr.items()}], core_ids=[0]).results[0]["out"]
```

```python
from contextlib import ExitStack

import concourse.bass as bass
from concourse import mybir

F32 = mybir.dt.float32
I32 = mybir.dt.int32
BF16 = mybir.dt.bfloat16
ALU = mybir.AluOpType
ACT = mybir.ActivationFunctionType
AX = mybir.AxisListType.X

P = 128
B, S, D = 16, 256, 128
TOK = B * S
NT = TOK // P
SUP = 4
NSUP = NT // SUP
EPS = 1e-5


class Scope:

    def __init__(self, nc, stack, prefix):
        self.nc, self.stack, self.prefix = nc, stack, prefix
        self.sems = []
        stack.callback(self.wipe)

    def sb(self, name, shape, dt=F32):
        return self.stack.enter_context(self.nc.sbuf_tensor(f"{self.prefix}_{name}", shape, dt))

    def ps(self, name, shape, dt=F32):
        return self.stack.enter_context(self.nc.psum_tensor(f"{self.prefix}_{name}", shape, dt))

    def sem(self, name):
        self.sems.append(self.nc.alloc_semaphore(f"{self.prefix}_{name}"))
        return self.sems[-1]

    def wipe(self):
        if self.sems:
            self.nc.clear_and_free_semaphores(self.sems)
            self.nc.all_engine_barrier()


def bcast(ap, n, where):
    return ap.unsqueeze(where).to_broadcast(list(ap.shape[:where]) + [n] + list(ap.shape[where:]))


class Norm:

    def __init__(self, m):
        self.stats = m.sb("stats", [P, NT, 6])
        self.tmp = m.sb("tmp", [P, 8, NT])
        self.mean = m.sb("mean", [P, NT])
        self.rstd = m.sb("rstd", [P, NT])
        self.counted = m.sem("stats_counted")
        self.var_ready = m.sem("var_ready")
        self.std_ready = m.sem("std_ready")
        self.done = m.sem("norm_done")

    def dve(self, dve, x):
        st, tmp = self.stats, self.tmp
        with dve.Fori(0, NSUP) as i:
            for g in range(SUP):
                t = SUP * i + g
                dve.bn_stats(st[:, t, :], x[:, t, :]).then_inc(self.counted, 1)
        dve.wait_ge(self.counted, NT)
        me, mo, ve, vo = st[:, :, 1], st[:, :, 4], st[:, :, 2], st[:, :, 5]
        dve.tensor_tensor(tmp[:, 0, :], me, mo, ALU.add).then_inc(self.counted, 1)
        dve.tensor_tensor(tmp[:, 1, :], me, mo, ALU.subtract).then_inc(self.counted, 1)
        dve.tensor_tensor(tmp[:, 2, :], ve, vo, ALU.add).then_inc(self.counted, 1)
        dve.wait_ge(self.counted, NT + 3)
        dve.tensor_scalar(self.mean[:, :], tmp[:, 0, :], 0.5, None, ALU.mult).then_inc(self.counted, 1)
        dve.tensor_scalar(tmp[:, 3, :], tmp[:, 1, :], 0.5, None, ALU.mult).then_inc(self.counted, 1)
        dve.tensor_scalar(tmp[:, 4, :], tmp[:, 2, :], 1.0 / D, EPS, ALU.mult, ALU.add).then_inc(self.counted, 1)
        dve.wait_ge(self.counted, NT + 6)
        dve.tensor_tensor(tmp[:, 5, :], tmp[:, 3, :], tmp[:, 3, :], ALU.mult).then_inc(self.counted, 1)
        dve.wait_ge(self.counted, NT + 7)
        dve.tensor_tensor(tmp[:, 6, :], tmp[:, 5, :], tmp[:, 4, :], ALU.add).then_inc(self.var_ready, 1)
        dve.wait_ge(self.std_ready, 1)
        dve.reciprocal(self.rstd[:, :], tmp[:, 7, :]).then_inc(self.done, 1)
        dve.wait_ge(self.done, 1)

    def act(self, act, then=None):
        act.preload_act_table(ACT.Sqrt)
        act.wait_ge(self.var_ready, 1)
        act.activation(self.tmp[:, 7, :], self.tmp[:, 6, :], ACT.Sqrt).then_inc(self.std_ready, 1)
        if then is not None:
            act.preload_act_table(then)

    def tile(self, dve, out, x, t):
        return dve.tensor_scalar(out, x[:, t, :], self.mean[:, bass.ds(t, 1)], self.rstd[:, bass.ds(t, 1)],
                                 ALU.subtract, ALU.mult)


def load_x(nc, x, ident, x_dram, ident_dram):
    with ExitStack() as stack:
        m = Scope(nc, stack, "lx")
        loaded = m.sem("loaded")
        with nc.Block() as block:

            @block.sync
            def _(sp):
                for u in range(2):
                    sp.dma_start(x[:, B * u : B * u + B, :],
                                 x_dram[P * B * u : P * B * (u + 1), :].rearrange("(p b) d -> p b d", b=B)).then_inc(loaded, 16)
                sp.dma_start(ident[:, :], ident_dram).then_inc(loaded, 16)
                sp.wait_ge(loaded, 48)


def store_x(nc, x, out_dram):
    with ExitStack() as stack:
        m = Scope(nc, stack, "st")
        stored = m.sem("stored")
        with nc.Block() as block:

            @block.sync
            def _(sp):
                for u in range(2):
                    sp.dma_start(out_dram.rearrange("b (u p) d -> u p b d", u=2)[u], x[:, B * u : B * u + B, :]).then_inc(stored, 16)
                sp.wait_ge(stored, 32)


def self_attention(nc, x_dram, ident_dram, mask_dram, wq_dram, wkv_dram, bq_dram, bk_dram, bv_dram, wp_dram, bp_dram, out_dram,
                   idx_dram, bins_dram, bias):
    H, HD = 16, 64
    HP = H // 2
    SCALE = 1.0 / HD**0.5
    Q = 32
    NB = P // Q
    NQKV = 2 * HP + 2 * SUP
    NLOAD = 11
    K = 64
    BINS = K // NSUP
    STEPS = 5
    NEVER = -1e30
    with ExitStack() as stack:
        m = Scope(nc, stack, "sa")
        x = m.sb("x", [P, NT, D])
        ident = m.sb("ident", [P, P])
        mask = m.sb("mask", [P, Q])
        wq = m.sb("wq", [P, H * HD])
        wkv = m.sb("wkv", [P, 2 * H * HD])
        bq = m.sb("bq", [P, HP])
        bk = m.sb("bk", [P, HP])
        bv = m.sb("bv", [P, HP])
        wp = m.sb("wp", [P, HP, D])
        bp = m.sb("bp", [1, D])
        one = m.sb("one", [1, P])
        crow = m.sb("crow", [1, D])
        raw = m.sb("raw", [P, NT * K], I32)
        bins = m.sb("bins", [P, K])
        val = m.sb("val", [P, 2, NT * K])
        idx = m.sb("idx", [P, NT * K], BF16)
        same = m.sb("same", [P, 2, NT, K], BF16)
        part = m.sb("part", [P, 2, NT, K], BF16)
        cnt = m.sb("cnt", [P, NT, K])
        norm = Norm(m)
        xn = m.sb("xn", [P, SUP, D])
        xnT = m.sb("xnT", [P, SUP * P])
        qT = m.sb("qT", [P, HP, SUP * P])
        kT = m.sb("kT", [P, HP, SUP * P])
        v = m.sb("v", [P, SUP, H * HD])
        logits = m.sb("logits", [P, 2, H, Q])
        shifted = m.sb("shifted", [P, 2, H, Q])
        probs = m.sb("probs", [P, 2, H, Q])
        normed = m.sb("normed", [P, 2, H, Q])
        rowmax = m.sb("rowmax", [P, 2, H])
        rowsum = m.sb("rowsum", [P, 2, H])
        rinv = m.sb("rinv", [P, 2, H])
        turned = m.sb("turned", [P, 2, H, Q])
        probsT = m.sb("probsT", [P, 2, H, P])
        oT = m.sb("oT", [P, 2, HP, P])

        ps_s = [[m.ps(f"ps_s{n}{o}", [P, HP, 2 * Q]) for o in range(2)] for n in range(2)]
        ps_q = [m.ps(f"ps_q{n}", [P, 512]) for n in range(4)]
        ps_o = [ps_q[2 + n][:, :].rearrange("p (c q) -> p c q", q=P) for n in range(2)]

        x_loaded = m.sem("x_loaded")
        w_loaded = m.sem("w_loaded")
        ones_ready = m.sem("ones_ready")
        zeroed = m.sem("probsT_zeroed")
        const_mm = m.sem("const_mm")
        const_ready = m.sem("const_ready")
        xn_ready = m.sem("xn_ready")
        xn_transposed = m.sem("xn_transposed")
        xnT_ready = m.sem("xnT_ready")
        qkv_mm = m.sem("qkv_mm")
        qkv_ready = m.sem("qkv_ready")
        scores_begun = m.sem("scores_begun")
        scored = m.sem("scored")
        logits_ready = m.sem("logits_ready")
        max_ready = m.sem("max_ready")
        shifted_ready = m.sem("shifted_ready")
        exp_ready = m.sem("exp_ready")
        sum_ready = m.sem("sum_ready")
        rinv_ready = m.sem("rinv_ready")
        normed_ready = m.sem("probs_normed")
        turned_ready = m.sem("turned_ready")
        probsT_ready = m.sem("probsT_ready")
        attended = m.sem("attended")
        oT_ready = m.sem("oT_ready")
        projected = m.sem("projected")
        x_out = m.sem("x_out")
        stored = m.sem("stored")
        prep = m.sem("index_prep")
        summed = m.sem("summed")
        logged = m.sem("logged")

        with nc.Block() as block:

            @block.sync
            def _(sp):
                rows = x_dram.rearrange("(t p) d -> p t d", p=P)
                sp.dma_start(x[:, :, :], rows).then_inc(x_loaded, 16)
                for dst, src in ((ident[:, :], ident_dram), (mask[:, :], mask_dram), (wq[:, :], wq_dram),
                                 (wkv[:, :], wkv_dram), (bq[:, :], bq_dram), (bk[:, :], bk_dram),
                                 (bv[:, :], bv_dram), (wp[:, :, :], wp_dram.rearrange("(c p) n -> p c n", p=P)),
                                 (bp[:, :], bp_dram), (raw[:, :], idx_dram), (bins[:, :], bins_dram)):
                    sp.dma_start(dst, src).then_inc(w_loaded, 16)
                out_rows = out_dram.rearrange("(t p) d -> p t d", p=P)
                with sp.Fori(0, NSUP) as i:
                    sp.wait_ge(x_out, SUP * i + SUP + 1)
                    sp.dma_start(out_rows[:, bass.ds(SUP * i, SUP), :], x[:, bass.ds(SUP * i, SUP), :]).then_inc(stored, 16)
                sp.wait_ge(stored, 16 * NSUP)

            @block.gpsimd
            def _(pool):
                pool.memset(one[:, :], 1.0).then_inc(ones_ready, 1)
                pool.memset(probsT[:, :, :, :], 0.0).then_inc(zeroed, 1)

            @block.tensor
            def _(pe):
                pe.wait_ge(w_loaded, 16 * NLOAD)
                pe.wait_ge(ones_ready, 1)
                for c in range(HP):
                    pe.matmul(ps_q[0][0:1, 0:D], bv[:, c : c + 1], wp[:, c, :], start=(c == 0), stop=False)
                pe.matmul(ps_q[0][0:1, 0:D], one[:, 0:1], bp[:, :], start=False, stop=True).then_inc(const_mm, 1)
                pe.sem_inc(qkv_ready, 4)
                pe.sem_inc(xn_transposed, 1)
                pe.sem_inc(logits_ready, 4)
                pe.wait_ge(const_ready, 1)

                def scores(i, g):
                    pe.wait_ge(logits_ready, 2 * (SUP * i + g) + 2)
                    pe.sem_inc(scores_begun, 1)
                    for h in range(H):
                        r, c = HD * (h % 2), h // 2
                        for j in range(NB):
                            cols = slice(P * g + Q * j, P * g + Q * j + Q)
                            mm = pe.matmul(ps_s[g % 2][h % 2][Q * j : Q * j + Q, c, 0:Q], qT[r : r + HD, c, cols],
                                           kT[r : r + HD, c, cols], start=True, stop=True, skip_group_check=True)
                    mm.then_inc(scored, 1)

                def attend(i, g):
                    pe.wait_ge(probsT_ready, SUP * i + g + 1)
                    pe.wait_ge(oT_ready, 2 * (SUP * i + g) + 1)
                    for h in range(H):
                        r, c = HD * (h % 2), h // 2
                        mm = pe.matmul(ps_o[c // (HP // 2)][r : r + HD, c % (HP // 2), :], v[:, g, h * HD : (h + 1) * HD],
                                       probsT[:, g % 2, HP * (h % 2) + c, :], start=True, stop=True, skip_group_check=True)
                        if h % (H // 2) == H // 2 - 1:
                            mm.then_inc(attended, 1)

                def project(i, g):
                    pe.wait_ge(oT_ready, 2 * (SUP * i + g) + 3)
                    if g >= 2:
                        pe.wait_ge(x_out, SUP * i + g)
                    y = ps_q[g % 2][:, 0:D]
                    pe.matmul(y, one[:, :], crow[:, :], start=True, stop=False)
                    for c in range(HP):
                        mm = pe.matmul(y, oT[:, g % 2, c, :], wp[:, c, :], start=False, stop=(c == HP - 1))
                    mm.then_inc(projected, 1)

                def turn_x(i):
                    pe.wait_ge(xn_ready, SUP * i + SUP)
                    for g in range(SUP):
                        mm = pe.transpose(ps_s[0][0][:, :, :].rearrange("p c k -> p (c k)")[:, P * g : P * g + P], xn[:, g, :], ident[:, :])
                    mm.then_inc(xn_transposed, 1)

                def fill(i, n):
                    pe.wait_ge(qkv_ready, NQKV * i + n + 1)
                    bank = ps_q[n % 4][:, :]
                    if n < 2 * HP:
                        w, c = (wq, n) if n < HP else (wkv, n - HP)
                        mm = pe.matmul(bank, w[:, P * c : P * c + P], xnT[:, :], start=True, stop=True)
                    else:
                        g, half = (n - 2 * HP) // 2, n % 2
                        at = H * HD + 512 * half
                        mm = pe.matmul(bank, xnT[:, P * g : P * g + P], wkv[:, at : at + 512], start=True, stop=True)
                    mm.then_inc(qkv_mm, 1)

                def super_tile(i, last):
                    pe.wait_ge(xnT_ready, i + 1)
                    pe.wait_ge(x_out, SUP * i + 1)
                    pe.wait_ge(oT_ready, 2 * SUP * i + 1)
                    for n in range(2 * HP):
                        fill(i, n)
                    pe.wait_ge(qkv_ready, NQKV * i + 2 * HP + 4)
                    for g in range(SUP):
                        scores(i, g)
                        fill(i, 2 * HP + 2 * g)
                        fill(i, 2 * HP + 2 * g + 1)
                    pe.wait_ge(qkv_ready, NQKV * i + NQKV + 4)
                    attend(i, 0)
                    project(i, 0)
                    attend(i, 1)
                    if not last:
                        pe.wait_ge(logits_ready, 2 * (SUP * i + SUP) + 4)
                        turn_x(i + 1)
                    project(i, 1)
                    attend(i, 2)
                    project(i, 2)
                    attend(i, 3)
                    project(i, 3)

                turn_x(0)
                with pe.Fori(0, NSUP - 1) as i:
                    super_tile(i, False)
                super_tile(NSUP - 1, True)

            @block.scalar
            def _(act):
                act.wait_ge(const_mm, 1)
                act.activation(crow[:, :], ps_q[0][0:1, 0:D], ACT.Copy).then_inc(const_ready, 1)
                norm.act(act, ACT.Exp)
                act.sem_inc(oT_ready, 1)

                def exp(i, g):
                    act.wait_ge(shifted_ready, SUP * i + g + 1)
                    act.activation(probs[:, g % 2, :, :], shifted[:, g % 2, :, :], ACT.Exp).then_inc(exp_ready, 1)

                def out(i, g):
                    for half in range(2):
                        act.wait_ge(attended, 2 * (SUP * i + g) + half + 1)
                        act.activation(oT[:, g % 2, half * (HP // 2) : (half + 1) * (HP // 2), :], ps_o[half],
                                       ACT.Copy).then_inc(oT_ready, 1)

                def copy_x(i):
                    act.wait_ge(xn_transposed, i + 2)
                    act.activation(xnT[:, :], ps_s[0][0][:, :, :].rearrange("p c k -> p (c k)"), ACT.Copy).then_inc(xnT_ready, 1)

                def copy_fill(i, n):
                    act.wait_ge(qkv_mm, NQKV * i + n + 1)
                    bank = ps_q[n % 4][:, :]
                    if n < 2 * HP:
                        dst, b, c = (qT, bq, n) if n < HP else (kT, bk, n - HP)
                        op = act.activation(dst[:, c, :], bank, ACT.Identity, bias=b[:, c : c + 1])
                    else:
                        g, half = (n - 2 * HP) // 2, n % 2
                        op = act.activation(v[:, g, 512 * half : 512 * half + 512], bank, ACT.Copy)
                    op.then_inc(qkv_ready, 1)

                def spread(i, g):
                    act.wait_ge(turned_ready, SUP * i + g + 1)
                    if g >= 2:
                        act.wait_ge(attended, 2 * (SUP * i + g - 1))
                    for j in range(NB):
                        rows = slice(Q * j, Q * j + Q)
                        op = act.activation(probsT[rows, g % 2, :, rows], turned[rows, g % 2, :, :], ACT.Copy)
                    op.then_inc(probsT_ready, 1)

                def super_tile(i, last):
                    for n in range(2 * HP):
                        copy_fill(i, n)
                    for g in range(SUP):
                        copy_fill(i, 2 * HP + 2 * g)
                        copy_fill(i, 2 * HP + 2 * g + 1)
                        exp(i, g)
                        if 0 < g < 3:
                            spread(i, g - 1)
                    out(i, 0)
                    spread(i, 2)
                    out(i, 1)
                    if not last:
                        copy_x(i + 1)
                    spread(i, 3)
                    out(i, 2)
                    out(i, 3)

                copy_x(0)
                with act.Fori(0, NSUP - 1) as i:
                    super_tile(i, False)
                super_tile(NSUP - 1, True)
                act.wait_ge(prep, 5)
                act.activation(val[:, 1, :], val[:, 0, :], ACT.Ln).then_inc(logged, 1)

            @block.vector
            def _(dve):
                dve.wait_ge(x_loaded, 16)
                norm.dve(dve, x)
                dve.wait_ge(xn_transposed, 1)
                for g in range(SUP):
                    norm.tile(dve, xn[:, g, :], x, g).then_inc(xn_ready, 1)
                dve.wait_ge(w_loaded, 16 * NLOAD)
                dve.wait_ge(zeroed, 1)
                dve.sem_inc(x_out, 1)

                def shift(i, g):
                    n = SUP * i + g + 1
                    u = g % 2
                    dve.wait_ge(scored, n)
                    for o in range(2):
                        dve.scalar_tensor_tensor(logits[:, u, HP * o : HP * o + HP, :], ps_s[u][o][:, :, 0:Q], SCALE,
                                                 bcast(mask[:, :], HP, 1), ALU.mult, ALU.add).then_inc(logits_ready, 1)
                    dve.wait_ge(logits_ready, 2 * n + 4)
                    dve.tensor_reduce(rowmax[:, u, :], logits[:, u, :, :], AX, ALU.max).then_inc(max_ready, 1)
                    dve.wait_ge(max_ready, n)
                    dve.tensor_tensor(shifted[:, u, :, :], logits[:, u, :, :], bcast(rowmax[:, u, :], Q, 2),
                                      ALU.subtract).then_inc(shifted_ready, 1)

                def normalise(i, g):
                    n = SUP * i + g + 1
                    u = g % 2
                    dve.wait_ge(exp_ready, n)
                    dve.tensor_reduce(rowsum[:, u, :], probs[:, u, :, :], AX, ALU.add).then_inc(sum_ready, 1)
                    dve.wait_ge(sum_ready, n)
                    dve.reciprocal(rinv[:, u, :], rowsum[:, u, :]).then_inc(rinv_ready, 1)
                    dve.wait_ge(rinv_ready, n)
                    dve.tensor_tensor(normed[:, u, :, :], probs[:, u, :, :], bcast(rinv[:, u, :], Q, 2),
                                      ALU.mult).then_inc(normed_ready, 1)
                    dve.wait_ge(normed_ready, n)
                    if g >= 2:
                        dve.wait_ge(probsT_ready, SUP * i + g - 1)
                    dve.transpose(turned[:, u, :, :], normed[:, u, :, :]).then_inc(turned_ready, 1)

                def add(i, g):
                    dve.wait_ge(projected, SUP * i + g + 1)
                    dve.tensor_tensor(x[:, SUP * i + g, :], x[:, SUP * i + g, :], ps_q[g % 2][:, 0:D], ALU.add).then_inc(x_out, 1)

                def norm_x(i):
                    dve.wait_ge(xn_transposed, i + 1)
                    for g in range(SUP):
                        norm.tile(dve, xn[:, g, :], x, SUP * i + g).then_inc(xn_ready, 1)

                def count(i, first, n):
                    for j in range(first, first + n, 2):
                        at = BINS * i + j
                        base = STEPS * at
                        for u in range(2):
                            dve.wait_ge(summed, base + 1)
                            dve.tensor_scalar(same[:, u, :, :].rearrange("p t k -> p (t k)"), idx[:, :],
                                              bins[:, bass.ds(at + u, 1)], None, ALU.is_equal).then_inc(summed, 1)
                        n_slots, off = K // 2, 0
                        src = [same[:, u, :, :] for u in range(2)]
                        for level in range(3):
                            for u in range(2):
                                dve.wait_ge(summed, base + 2 * level + u + 2)
                                dst = part[:, u, :, off : off + n_slots]
                                dve.tensor_tensor(dst, src[u][:, :, 0:n_slots], src[u][:, :, n_slots : 2 * n_slots],
                                                  ALU.add).then_inc(summed, 1)
                                src[u] = dst
                            off, n_slots = off + n_slots, n_slots // 2
                        for u in range(2):
                            dve.wait_ge(summed, base + 8 + u)
                            dve.tensor_reduce(cnt[:, :, bass.ds(at + u, 1)], src[u], AX, ALU.add).then_inc(summed, 1)

                dve.tensor_copy(val[:, 0, :], raw[:, :]).then_inc(prep, 1)
                dve.wait_ge(prep, 1)
                dve.tensor_scalar(val[:, 1, :], val[:, 0, :], 0.0, float(K), ALU.is_lt, ALU.mult).then_inc(prep, 1)
                dve.wait_ge(prep, 2)
                dve.tensor_tensor(val[:, 0, :], val[:, 0, :], val[:, 1, :], ALU.add).then_inc(prep, 1)
                dve.wait_ge(prep, 3)
                dve.tensor_scalar(idx[:, :], val[:, 0, :], 0.0, float(K - 1), ALU.max, ALU.min).then_inc(prep, 1)
                dve.wait_ge(prep, 4)
                dve.sem_inc(summed, 1)

                def super_tile(i, last):
                    if not last:
                        norm_x(i + 1)
                    count(i, 0, 6)
                    shift(i, 0)
                    shift(i, 1)
                    normalise(i, 0)
                    shift(i, 2)
                    normalise(i, 1)
                    shift(i, 3)
                    normalise(i, 2)
                    add(i, 0)
                    normalise(i, 3)
                    add(i, 1)
                    count(i, 6, 2)
                    add(i, 2)
                    add(i, 3)

                with dve.Fori(0, NSUP - 1) as i:
                    super_tile(i, False)
                super_tile(NSUP - 1, True)
                cflat = cnt[:, :, :].rearrange("p t k -> p (t k)")
                bflat = bias[:, :, :].rearrange("p t k -> p (t k)")
                dve.wait_ge(summed, STEPS * K + 1)
                dve.tensor_scalar(val[:, 0, :], cflat, 1.0, None, ALU.max).then_inc(prep, 1)
                dve.tensor_scalar(bflat, cflat, 0.0, NEVER, ALU.is_equal, ALU.mult).then_inc(prep, 1)
                dve.wait_ge(logged, 1)
                dve.wait_ge(prep, 6)
                dve.tensor_tensor(bflat, bflat, val[:, 1, :], ALU.add).then_inc(prep, 1)
                dve.wait_ge(prep, 7)
def gathered_attention(nc, x, bias, ident, ctxT_dram, downT_dram, upT_dram, qT_dram, outT_dram, hmask_dram, pmask_dram):
    H, HD, K = 16, 8, 64
    HP, VW = H // 2, 2 * (HD + 1)
    SCALE = 1.0 / HD**0.5
    HK = H * K
    with ExitStack() as stack:
        m = Scope(nc, stack, "ga")
        ctxT = m.sb("ctxT", [D, B * K])
        downT = m.sb("downT", [D, D])
        upT = m.sb("upT", [D, 2 * D])
        qW = m.sb("qW", [D, D])
        oW = m.sb("oW", [D, D])
        hmask = m.sb("hmask", [P, H])
        pmask = m.sb("pmask", [P, 2])
        cT = m.sb("cT", [P, B, 2, K])
        kT = m.sb("kT", [P, B, K])
        keys = m.sb("keys", [P, B, H, K])
        vals = m.sb("vals", [P, B, HP, VW])
        norm = Norm(m)
        xn = m.sb("xn", [P, 2, D])
        xnT = m.sb("xnT", [P, 2 * P])
        qT = m.sb("qT", [P, 2 * P])
        logits = m.sb("logits", [P, 2, H, K])
        rowmax = m.sb("rowmax", [P, 2, H])
        shifted = m.sb("shifted", [P, 2, H, K])
        probs = m.sb("probs", [P, 2, HK])
        probsT = m.sb("probsT", [P, 2, HP, P])
        rinv = m.sb("rinv", [P, 2, HP, 2])
        o = m.sb("o", [P, 2, D])
        oT = m.sb("oT", [P, 2, P])
        ps_s = [m.ps(f"ps_s{u}", [P, H, K]) for u in range(2)]
        ps_p = m.ps("ps_p", [P, HP, P])
        ps_m = m.ps("ps_m", [P, 512])
        ps_o = m.ps("ps_o", [P, 512])

        loaded = m.sem("loaded")
        ctx_mm, ctx_ready = m.sem("ctx_mm"), m.sem("ctx_ready")
        key_mm, key_ready = m.sem("key_mm"), m.sem("key_ready")
        val_mm, val_ready = m.sem("val_mm"), m.sem("val_ready")
        keys_ready = m.sem("keys_ready")
        ones_ready = m.sem("ones_ready")
        xn_ready, xn_transposed, xnT_ready = m.sem("xn_ready"), m.sem("xn_transposed"), m.sem("xnT_ready")
        q_mm, qT_ready = m.sem("q_mm"), m.sem("qT_ready")
        scored, logits_ready, max_ready = m.sem("scored"), m.sem("logits_ready"), m.sem("max_ready")
        shifted_ready, exp_ready = m.sem("shifted_ready"), m.sem("exp_ready")
        probs_transposed, probsT_ready = m.sem("probs_transposed"), m.sem("probsT_ready")
        attended, rinv_ready, o_ready = m.sem("attended"), m.sem("rinv_ready"), m.sem("o_ready")
        o_transposed, oT_ready = m.sem("o_transposed"), m.sem("oT_ready")
        projected, x_out = m.sem("projected"), m.sem("x_out")
        NLOAD = 7

        with nc.Block() as block:

            @block.sync
            def _(sp):
                for dst, src in ((ctxT, ctxT_dram), (downT, downT_dram), (upT, upT_dram), (qW, qT_dram),
                                 (oW, outT_dram), (hmask, hmask_dram), (pmask, pmask_dram)):
                    sp.dma_start(dst[:, :], src).then_inc(loaded, 16)

            @block.gpsimd
            def _(pool):
                pool.wait_ge(loaded, 16 * NLOAD)
                for h2 in range(2):
                    col = vals[:, :, :, h2 * (HD + 1) + HD].rearrange("p b c -> p (b c)")
                    pool.tensor_copy(col, bcast(pmask[:, h2], B * HP, 1)).then_inc(ones_ready, 1)
                pool.wait_ge(key_ready, 2)
                with pool.Fori(0, B) as b:
                    pool.tensor_tensor(keys[:, b, :, :], bcast(kT[:, b, :], H, 1), bcast(hmask[:, :], K, 2),
                                       ALU.mult).then_inc(keys_ready, 1)

            @block.tensor
            def _(pe):
                pe.wait_ge(loaded, 16 * NLOAD)
                for n in range(2):
                    pe.matmul(ps_s[0][:, 8 * n : 8 * n + 8, :], downT[:, :], ctxT[:, 512 * n : 512 * n + 512],
                              start=True, stop=True).then_inc(ctx_mm, 1)
                pe.wait_ge(ctx_ready, 4)
                for n in range(2):
                    pe.matmul(ps_s[1][:, 8 * n : 8 * n + 8, :], upT[:, 0:D], cT[:, 8 * n : 8 * n + 8, 0, :],
                              start=True, stop=True).then_inc(key_mm, 1)
                banks = [ps_p[:, 0:4, :], ps_p[:, 4:8, :]]
                for b in range(B):
                    if b in (8, 12):
                        pe.wait_ge(val_ready, (b - 4) // 4)
                    mm = pe.matmul(banks[(b // 4) % 2][:, b % 4, :], cT[:, b, :, :].rearrange("p e k -> p (e k)"), upT[:, D : 2 * D],
                                   start=True, stop=True)
                    if b % 4 == 3:
                        mm.then_inc(val_mm, 1)
                pe.wait_ge(val_ready, B // 4)
                pe.wait_ge(ones_ready, 2)
                pe.wait_ge(key_ready, 2)

                def turn_x(b):
                    pe.wait_ge(xn_ready, 2 * b + 2)
                    for u in range(2):
                        mm = pe.transpose(ps_m[:, P * u : P * u + P], xn[:, u, :], ident[:, :])
                    mm.then_inc(xn_transposed, 1)

                def queries(b):
                    pe.wait_ge(xnT_ready, b + 1)
                    pe.matmul(ps_m[:, 256:512], qW[:, :], xnT[:, :], start=True, stop=True).then_inc(q_mm, 1)

                def scores(b, u, first=False):
                    if not first:
                        pe.wait_ge(logits_ready, 2 * b + u - 1)
                    if u == 0:
                        pe.wait_ge(qT_ready, b + 1)
                        pe.wait_ge(keys_ready, b + 1)
                    for n in range(2):
                        mm = pe.matmul(ps_s[u][:, 8 * n : 8 * n + 8, :], qT[:, P * u : P * u + P],
                                       keys[:, b, 8 * n : 8 * n + 8, :], start=True, stop=True)
                    mm.then_inc(scored, 1)

                def turn_probs(b, u):
                    pe.wait_ge(exp_ready, 2 * b + u + 1)
                    for c in range(HP):
                        mm = pe.transpose(ps_p[:, c, :], probs[:, u, P * c : P * c + P], ident[:, :])
                        if c % 4 == 3:
                            mm.then_inc(probs_transposed, 1)

                def attend(b, u, first=False):
                    if not first:
                        pe.wait_ge(o_ready, 2 * b + u)
                    pe.wait_ge(probsT_ready, 2 * (2 * b + u) + 2)
                    for c in range(HP):
                        mm = pe.matmul(ps_o[:, VW * c : VW * c + VW], probsT[:, u, c, :], vals[:, b, c, :],
                                       start=True, stop=True)
                    mm.then_inc(attended, 1)

                def turn_o(b):
                    pe.wait_ge(o_ready, 2 * b + 2)
                    for u in range(2):
                        mm = pe.transpose(ps_m[:, P * u : P * u + P], o[:, u, :], ident[:, :])
                    mm.then_inc(o_transposed, 1)

                def project(b):
                    pe.wait_ge(oT_ready, b + 1)
                    for u in range(2):
                        mm = pe.matmul(ps_m[:, 256 + P * u : 256 + P * u + P], oT[:, u, :], oW[:, :], start=True, stop=True)
                    mm.then_inc(projected, 1)

                def batch(b, first, last):
                    if not first:
                        turn_probs(b - 1, 1)
                        pe.wait_ge(x_out, b)
                    if not last:
                        turn_x(b + 1)
                    scores(b, 1, first)
                    if not last:
                        queries(b + 1)
                    if not first:
                        attend(b - 1, 1)
                    turn_probs(b, 0)
                    if not last:
                        scores(b + 1, 0)
                    if not first:
                        turn_o(b - 1)
                    attend(b, 0, first)
                    if not first:
                        project(b - 1)

                turn_x(0)
                queries(0)
                scores(0, 0, True)
                batch(0, True, False)
                with pe.Fori(1, B - 1) as b:
                    batch(b, False, False)
                batch(B - 1, False, True)
                turn_probs(B - 1, 1)
                attend(B - 1, 1)
                pe.wait_ge(x_out, B)
                turn_o(B - 1)
                project(B - 1)

            @block.scalar
            def _(act):
                for n in range(2):
                    act.wait_ge(ctx_mm, n + 1)
                    for e in range(2):
                        act.activation(cT[:, 8 * n : 8 * n + 8, e, :], ps_s[0][:, 8 * n : 8 * n + 8, :], ACT.Copy).then_inc(ctx_ready, 1)
                for n in range(2):
                    act.wait_ge(key_mm, n + 1)
                    act.activation(kT[:, 8 * n : 8 * n + 8, :], ps_s[1][:, 8 * n : 8 * n + 8, :], ACT.Copy).then_inc(key_ready, 1)
                norm.act(act, ACT.Exp)

                def copy_x(b):
                    act.wait_ge(xn_transposed, b + 1)
                    act.activation(xnT[:, :], ps_m[:, 0:256], ACT.Copy).then_inc(xnT_ready, 1)

                def copy_q(b):
                    act.wait_ge(q_mm, b + 1)
                    act.activation(qT[:, :], ps_m[:, 256:512], ACT.Copy, scale=SCALE).then_inc(qT_ready, 1)

                def exp(b, u):
                    act.wait_ge(shifted_ready, 2 * b + u + 1)
                    act.activation(probs[:, u, :], shifted[:, u, :, :].rearrange("p h k -> p (h k)"), ACT.Exp).then_inc(exp_ready, 1)

                def copy_probs(b, u):
                    for n in range(2):
                        act.wait_ge(probs_transposed, 2 * (2 * b + u) + n + 1)
                        act.activation(probsT[:, u, 4 * n : 4 * n + 4, :], ps_p[:, 4 * n : 4 * n + 4, :], ACT.Copy).then_inc(probsT_ready, 1)

                def copy_o(b):
                    act.wait_ge(o_transposed, b + 1)
                    act.activation(oT[:, :, :], ps_m[:, 0:256].rearrange("p (u q) -> p u q", u=2), ACT.Copy).then_inc(oT_ready, 1)

                def batch(b, first, last):
                    if not first:
                        exp(b - 1, 1)
                        copy_probs(b - 1, 1)
                    if not last:
                        copy_x(b + 1)
                        copy_q(b + 1)
                    exp(b, 0)
                    copy_probs(b, 0)
                    if not first:
                        copy_o(b - 1)

                copy_x(0)
                copy_q(0)
                batch(0, True, False)
                with act.Fori(1, B - 1) as b:
                    batch(b, False, False)
                batch(B - 1, False, True)
                exp(B - 1, 1)
                copy_probs(B - 1, 1)
                copy_o(B - 1)

            @block.vector
            def _(dve):
                norm.dve(dve, x)
                dve.wait_ge(loaded, 16 * NLOAD)
                banks = [ps_p[:, 0:4, :], ps_p[:, 4:8, :]]
                for n in range(B // 4):
                    dve.wait_ge(val_mm, n + 1)
                    dst = vals[:, 4 * n : 4 * n + 4, :, :].rearrange("p b c (e w) -> p (b c) e w", e=2)[:, :, :, 0:HD]
                    src = banks[n % 2].rearrange("p b (c e d) -> p (b c) e d", e=2, d=HD)
                    dve.tensor_tensor(dst, src, bcast(bcast(pmask[:, :], HD, 2), 4 * HP, 1), ALU.mult).then_inc(val_ready, 1)

                def norm_x(b):
                    for u in range(2):
                        norm.tile(dve, xn[:, u, :], x, B * u + b).then_inc(xn_ready, 1)

                def bias_scores(b, u, first):
                    dve.wait_ge(scored, 2 * b + u + 1)
                    if not first:
                        dve.wait_ge(shifted_ready, 2 * b + u - 1)
                    dve.tensor_tensor(logits[:, u, :, :], ps_s[u][:, :, :], bcast(bias[:, B * u + b, :], H, 1),
                                      ALU.add).then_inc(logits_ready, 1)

                def shift(b, u):
                    n = 2 * b + u + 1
                    dve.wait_ge(logits_ready, n)
                    dve.tensor_reduce(rowmax[:, u, :], logits[:, u, :, :], AX, ALU.max).then_inc(max_ready, 1)
                    dve.wait_ge(max_ready, n)
                    dve.tensor_tensor(shifted[:, u, :, :], logits[:, u, :, :], bcast(rowmax[:, u, :], K, 2),
                                      ALU.subtract).then_inc(shifted_ready, 1)

                def divide(b, u):
                    n = 2 * b + u + 1
                    dve.wait_ge(attended, n)
                    out = ps_o[:, 0 : HP * VW].rearrange("p (c e w) -> p c e w", c=HP, e=2)
                    dve.reciprocal(rinv[:, u, :, :], out[:, :, :, HD]).then_inc(rinv_ready, 1)
                    dve.wait_ge(rinv_ready, n)
                    dve.tensor_tensor(o[:, u, :].rearrange("p (c e d) -> p c e d", c=HP, e=2), out[:, :, :, 0:HD],
                                      bcast(rinv[:, u, :, :], HD, 3), ALU.mult).then_inc(o_ready, 1)

                def add(b):
                    dve.wait_ge(projected, b + 1)
                    view = x[:, :, :].rearrange("p (u b) d -> p u b d", u=2)[:, :, b, :]
                    dve.tensor_tensor(view, view, ps_m[:, 256:512].rearrange("p (u d) -> p u d", u=2), ALU.add).then_inc(x_out, 1)

                def batch(b, nth, norms):
                    for u in range(2):
                        bias_scores(b, u, nth == 0)
                        if nth > 0:
                            divide(b - 1, u)
                        if nth > 1 and u == 0:
                            add(b - 2)
                        shift(b, u)
                    if norms:
                        dve.wait_ge(xn_transposed, b + 2)
                        norm_x(b + 2)

                dve.sem_inc(x_out, 1)
                norm_x(0)
                dve.wait_ge(xn_transposed, 1)
                norm_x(1)
                batch(0, 0, True)
                batch(1, 1, True)
                with dve.Fori(2, B - 2) as b:
                    batch(b, 2, True)
                batch(B - 2, 2, False)
                batch(B - 1, 2, False)
                divide(B - 1, 0)
                add(B - 2)
                divide(B - 1, 1)
                add(B - 1)
                dve.wait_ge(x_out, B + 1)


def gated_experts(nc, x, ident, scale_dram, bias_dram, gateT_dram, wg_dram, wu_dram, wd_dram, lower_dram):
    E, F, TOP = 8, 256, 2
    C = F // P
    NE = E + 1
    with ExitStack() as stack:
        m = Scope(nc, stack, "ge")
        lns = m.sb("ln_scale", [D, 1])
        lnb = m.sb("ln_bias", [D, 1])
        lnbB = m.sb("ln_bias_rows", [D, P])
        gateT = m.sb("gateT", [D, E])
        gateS = m.sb("gateS", [D, E])
        lower = m.sb("lower", [P, E, E])
        wg = m.sb("wg", [D, NE, F])
        wu = m.sb("wu", [D, NE, F])
        wd = m.sb("wd", [P, NE, C, D])
        norm = Norm(m)
        xn = m.sb("xn", [P, SUP, D])
        xnT = m.sb("xnT", [D, SUP * P])
        xT = m.sb("xT", [D, TOK])
        gbias = m.sb("gbias", [P, E])
        raw = m.sb("raw_logits", [P, NT, E])
        gt = m.sb("gate", [P, 12, NT, E])
        gs = m.sb("gate_stats", [P, 8, NT])
        cmp = m.sb("cmp", [P, 4, NT, E * E])
        weight = m.sb("weight", [P, NT, E])
        sg = m.sb("silu_g", [P, 2, SUP * P])
        hT = m.sb("hT", [P, 6, SUP * P])
        ps_u = [[m.ps(f"ps_{k}{n}", [P, SUP * P]) for k in "gu"] for n in range(2)]
        ps_y = [m.ps(f"ps_y{n}", [P, SUP, D]) for n in range(3)]
        ps_m = m.ps("ps_m", [P, 512])

        loaded = m.sem("loaded")
        gate_prep = m.sem("gate_prep")
        gbias_mm = m.sem("gbias_mm")
        gbias_ready = m.sem("gbias_ready")
        xn_ready, xn_transposed, xnT_ready = m.sem("xn_ready"), m.sem("xn_transposed"), m.sem("xnT_ready")
        xT_ready, logits_mm, raw_ready = m.sem("xT_ready"), m.sem("logits_mm"), m.sem("raw_ready")
        gated = m.sem("gated")
        gate_sqrt, gate_exp = m.sem("gate_sqrt"), m.sem("gate_exp")
        up_mm, silu_ready, h_ready = m.sem("up_mm"), m.sem("silu_ready"), m.sem("h_ready")
        down_mm, added = m.sem("down_mm"), m.sem("added")
        NLOAD = 7

        with nc.Block() as block:

            @block.sync
            def _(sp):
                for dst, src in ((lns[:, :], scale_dram), (lnb[:, :], bias_dram), (gateT[:, :], gateT_dram),
                                 (lower[:, :, :], lower_dram), (wg[:, :, :], wg_dram), (wu[:, :, :], wu_dram),
                                 (wd[:, :, :, :], wd_dram)):
                    sp.dma_start(dst, src).then_inc(loaded, 16)

            @block.gpsimd
            def _(pool):
                pool.sem_inc(xT_ready, 1)
                with pool.Fori(0, NSUP) as i:
                    pool.wait_ge(xnT_ready, i + 1)
                    pool.tensor_copy(xT[:, bass.ds(SUP * P * i, SUP * P)], xnT[:, :]).then_inc(xT_ready, 1)

            @block.tensor
            def _(pe):
                pe.wait_ge(gate_prep, 2)
                pe.matmul(ps_m[:, 0:E], lnbB[:, :], gateT[:, :], start=True, stop=True).then_inc(gbias_mm, 1)
                pe.wait_ge(gbias_ready, 1)
                with pe.Fori(0, NSUP) as i:
                    pe.wait_ge(xn_ready, SUP * i + SUP)
                    for g in range(SUP):
                        mm = pe.transpose(ps_u[0][0][:, P * g : P * g + P], xn[:, g, :], ident[:, :])
                    mm.then_inc(xn_transposed, 1)
                    pe.wait_ge(xnT_ready, i + 1)
                    pe.wait_ge(raw_ready, i + 1)
                    for g in range(SUP):
                        mm = pe.matmul(ps_m[:, E * g : E * g + E], xnT[:, P * g : P * g + P], gateS[:, :], start=True, stop=True)
                    mm.then_inc(logits_mm, 1)
                pe.wait_ge(xT_ready, NSUP + 1)
                pe.sem_inc(h_ready, 2)
                pe.sem_inc(added, 3)

                def up(i, e, c):
                    pe.wait_ge(h_ready, C * NE * i + C * e + c + 1)
                    for w, bank in zip((wg, wu), ps_u[c]):
                        mm = pe.matmul(bank[:, :], w[:, e, P * c : P * c + P], xT[:, bass.ds(SUP * P * i, SUP * P)],
                                       start=True, stop=True)
                        mm.then_inc(up_mm, 1)

                def down(i, e):
                    pe.wait_ge(h_ready, C * NE * i + C * e + C + 2)
                    pe.wait_ge(added, NE * i + e + 1)
                    for g in range(SUP):
                        for c in range(C):
                            mm = pe.matmul(ps_y[e % 3][:, g, :], hT[:, (C * e + c) % 6, P * g : P * g + P], wd[:, e, c, :],
                                           start=(c == 0), stop=(c == C - 1))
                    mm.then_inc(down_mm, 1)

                with pe.Fori(0, NSUP) as i:
                    for e in range(NE):
                        for c in range(C):
                            up(i, e, c)
                        if e:
                            down(i, e - 1)
                    down(i, NE - 1)

            @block.scalar
            def _(act):
                norm.act(act)
                with act.Fori(0, NSUP) as i:
                    act.wait_ge(xn_transposed, i + 1)
                    act.wait_ge(xT_ready, i + 1)
                    act.activation(xnT[:, :], ps_u[0][0][:, :], ACT.Copy).then_inc(xnT_ready, 1)
                act.wait_ge(gated, 2)
                act.activation(gs[:, 2, :], gs[:, 1, :], ACT.Sqrt).then_inc(gate_sqrt, 1)
                act.wait_ge(gated, 7)
                act.activation(gt[:, 3, :, :], gt[:, 2, :, :], ACT.Exp).then_inc(gate_exp, 1)
                act.preload_act_table(ACT.Silu)
                with act.Fori(0, NSUP) as i:
                    for n in range(C * NE):
                        act.wait_ge(up_mm, 2 * (C * NE * i + n) + 1)
                        act.activation(sg[:, n % 2, :], ps_u[n % 2][0][:, :], ACT.Silu).then_inc(silu_ready, 1)

            @block.vector
            def _(dve):
                norm.dve(dve, x)
                dve.wait_ge(loaded, 16 * NLOAD)
                dve.tensor_copy(lnbB[:, :], bcast(lnb[:, 0], P, 1)).then_inc(gate_prep, 1)
                dve.tensor_scalar(gateS[:, :], gateT[:, :], lns[:, 0:1], None, ALU.mult).then_inc(gate_prep, 1)
                dve.wait_ge(gbias_mm, 1)
                dve.tensor_copy(gbias[:, :], ps_m[:, 0:E]).then_inc(gbias_ready, 1)
                dve.sem_inc(raw_ready, 1)

                with dve.Fori(0, NSUP) as i:
                    dve.wait_ge(raw_ready, i + 1)
                    for g in range(SUP):
                        norm.tile(dve, xn[:, g, :], x, SUP * i + g).then_inc(xn_ready, 1)
                    dve.wait_ge(logits_mm, i + 1)
                    dve.tensor_copy(raw[:, bass.ds(SUP * i, SUP), :],
                                    ps_m[:, 0 : SUP * E].rearrange("p (g e) -> p g e", e=E)).then_inc(raw_ready, 1)
                dve.wait_ge(raw_ready, NSUP + 1)

                g = lambda k: gt[:, k, :, :]
                dve.tensor_tensor(gs[:, 0, :], norm.rstd[:, :], norm.rstd[:, :], ALU.mult).then_inc(gated, 1)
                dve.wait_ge(gated, 1)
                dve.tensor_scalar(gs[:, 1, :], gs[:, 0, :], -EPS, 1.0 + EPS, ALU.mult, ALU.add).then_inc(gated, 1)
                dve.wait_ge(gate_sqrt, 1)
                dve.reciprocal(gs[:, 3, :], gs[:, 2, :]).then_inc(gated, 1)
                dve.wait_ge(gated, 3)
                dve.tensor_tensor(g(0), raw[:, :, :], bcast(gs[:, 3, :], E, 2), ALU.mult).then_inc(gated, 1)
                dve.wait_ge(gated, 4)
                dve.tensor_tensor(g(1), g(0), bcast(gbias[:, :], NT, 1), ALU.add).then_inc(gated, 1)
                dve.wait_ge(gated, 5)
                dve.tensor_reduce(gs[:, 4, :], g(1), AX, ALU.max).then_inc(gated, 1)
                dve.wait_ge(gated, 6)
                dve.tensor_tensor(g(2), g(1), bcast(gs[:, 4, :], E, 2), ALU.subtract).then_inc(gated, 1)
                dve.wait_ge(gate_exp, 1)
                dve.tensor_reduce(gs[:, 5, :], g(3), AX, ALU.add).then_inc(gated, 1)
                dve.wait_ge(gated, 8)
                dve.reciprocal(gs[:, 6, :], gs[:, 5, :]).then_inc(gated, 1)
                dve.wait_ge(gated, 9)
                dve.tensor_tensor(g(4), g(3), bcast(gs[:, 6, :], E, 2), ALU.mult).then_inc(gated, 1)
                dve.wait_ge(gated, 10)
                sq = lambda k: cmp[:, k, :, :].rearrange("p t (e f) -> p t e f", e=E)
                mine, other = bcast(g(4), E, 3), bcast(g(4), E, 2)
                dve.tensor_tensor(sq(0), other, mine, ALU.is_gt).then_inc(gated, 1)
                dve.tensor_tensor(sq(1), other, mine, ALU.is_equal).then_inc(gated, 1)
                dve.wait_ge(gated, 12)
                dve.tensor_tensor(sq(2), sq(1), bcast(lower[:, :, :], NT, 1), ALU.mult).then_inc(gated, 1)
                dve.wait_ge(gated, 13)
                dve.tensor_tensor(cmp[:, 3, :, :], cmp[:, 0, :, :], cmp[:, 2, :, :], ALU.add).then_inc(gated, 1)
                dve.wait_ge(gated, 14)
                dve.tensor_reduce(g(5), sq(3), AX, ALU.add).then_inc(gated, 1)
                dve.wait_ge(gated, 15)
                dve.tensor_scalar(g(6), g(5), TOP - 0.5, None, ALU.is_lt).then_inc(gated, 1)
                dve.wait_ge(gated, 16)
                dve.tensor_tensor(g(7), g(6), g(4), ALU.mult).then_inc(gated, 1)
                dve.wait_ge(gated, 17)
                dve.tensor_reduce(gs[:, 7, :], g(7), AX, ALU.add).then_inc(gated, 1)
                dve.wait_ge(gated, 18)
                dve.tensor_scalar(norm.tmp[:, 0, :], gs[:, 7, :], EPS, None, ALU.add).then_inc(gated, 1)
                dve.wait_ge(gated, 19)
                dve.reciprocal(norm.tmp[:, 1, :], norm.tmp[:, 0, :]).then_inc(gated, 1)
                dve.wait_ge(gated, 20)
                dve.tensor_tensor(weight[:, :, :], g(7), bcast(norm.tmp[:, 1, :], E, 2), ALU.mult).then_inc(gated, 1)
                dve.wait_ge(gated, 21)

                def hidden(i, e):
                    for c in range(C):
                        n = C * NE * i + C * e + c + 1
                        dve.wait_ge(silu_ready, n)
                        dve.wait_ge(up_mm, 2 * n)
                        dve.tensor_tensor(hT[:, (C * e + c) % 6, :], sg[:, c, :], ps_u[c][1][:, :], ALU.mult).then_inc(h_ready, 1)

                def add(i, e):
                    dve.wait_ge(down_mm, NE * i + e + 1)
                    dve.wait_ge(added, NE * i + e + 3)
                    if e == 0:
                        view = x[:, bass.ds(SUP * i, SUP), :]
                        dve.tensor_tensor(view, view, ps_y[0][:, :, :], ALU.add).then_inc(added, 1)
                    else:
                        for g in range(SUP):
                            t = SUP * i + g
                            op = dve.scalar_tensor_tensor(x[:, t, :], ps_y[e % 3][:, g, :], weight[:, t, e - 1 : e], x[:, t, :],
                                                          ALU.mult, ALU.add)
                        op.then_inc(added, 1)

                with dve.Fori(0, NSUP) as i:
                    for e in range(NE):
                        hidden(i, e)
                        if e:
                            add(i, e - 1)
                    add(i, NE - 1)
                dve.wait_ge(added, NE * NSUP + 3)


def norm_statistics(nc, x, norm):
    with nc.Block() as block:

        @block.scalar
        def _(act):
            norm.act(act)

        @block.vector
        def _(dve):
            norm.dve(dve, x)


INNER, STATE, TAPS, HEADS = 256, 64, 4, 4
HEADDIM = INNER // HEADS


def ssm_inputs(nc, x, ident, norm, m, backward, w, store):
    CH = 3
    NB = 2
    ZD = INNER + HEADS
    with ExitStack() as stack:
        k = Scope(nc, stack, m.prefix + "i")
        win = k.sb("win", [D, 2 * INNER + 2 * STATE + HEADS])
        wzd = k.sb("wzd", [D, ZD])
        cw = k.sb("conv_w", [P, CH, TAPS])
        cb = k.sb("conv_b", [P, CH])
        pick = k.sb("pick", [P, P])
        xn = k.sb("xn", [P, SUP, D])
        xnT = k.sb("xnT", [D, SUP * P])
        pad = k.sb("pad", [P, CH, NB, S + TAPS - 1])
        acc = k.sb("acc", [P, CH, NB, S])
        xs = k.sb("xs", [P, CH, NB, S])
        cs = k.sb("cs", [P, SUP * P])
        ps_a = [k.ps(f"ps_a{n}", [P, 512]) for n in range(4)]
        ps_b = [k.ps(f"ps_b{n}", [P, 512]) for n in range(4)]
        loaded, padded = k.sem("loaded"), k.sem("padded")
        xn_ready, xn_transposed, xnT_ready = k.sem("xn_ready"), k.sem("xn_transposed"), k.sem("xnT_ready")
        in_mm, in_ready = k.sem("in_mm"), k.sem("in_ready")
        z_mm, z_ready, dt_ready = k.sem("z_mm"), k.sem("z_ready"), k.sem("dt_ready")
        conv, xs_ready = k.sem("conv"), k.sem("xs_ready")
        c_mm, c_ready, c_kept = k.sem("c_mm"), k.sem("c_ready"), k.sem("c_kept")
        g_mm, g_ready = k.sem("g_mm"), k.sem("g_ready")
        turned, x_ready, b_ready = k.sem("turned"), k.sem("x_ready"), k.sem("b_ready")
        NLOAD = 5
        first = 0 if backward else TAPS - 1
        hole = S if backward else 0
        CONV = CH * TAPS

        def tiles(buf, i, g):
            return buf[:, B * (g % 2) + NB * i + g // 2, :]

        with nc.Block() as block:

            @block.sync
            def _(sp):
                for dst, src in ((win[:, :], w["in"]), (wzd[:, 0:INNER], w["in"][:, 0:INNER]),
                                 (cw[:, :, :], w["conv_w"]), (cb[:, :], w["conv_b"]), (pick[:, :], w["pick"])):
                    sp.dma_start(dst, src).then_inc(loaded, 16)

            @block.gpsimd
            def _(pool):
                pool.memset(pad[:, :, :, hole : hole + TAPS - 1], 0.0).then_inc(padded, 1)
                pool.wait_ge(loaded, 16 * NLOAD)
                pool.tensor_copy(wzd[:, INNER:ZD], win[:, 2 * INNER + 2 * STATE :]).then_inc(padded, 1)
                pool.sem_inc(c_kept, 1)
                with pool.Fori(0, NSUP) as i:
                    pool.wait_ge(c_ready, i + 1)
                    for g in range(SUP):
                        op = pool.tensor_copy(tiles(store["c"], i, g), cs[0:STATE, P * g : P * g + P])
                    op.then_inc(c_kept, 1)

            @block.tensor
            def _(pe):
                pe.wait_ge(loaded, 16 * NLOAD)
                pe.wait_ge(padded, 2)

                def turn_x(i):
                    pe.wait_ge(xn_ready, SUP * i + SUP)
                    for g in range(SUP):
                        mm = pe.transpose(ps_a[0][:, P * g : P * g + P], xn[:, g, :], ident[:, :])
                    mm.then_inc(xn_transposed, 1)

                def project(i):
                    pe.wait_ge(xnT_ready, i + 1)
                    pe.wait_ge(in_ready, CH * i + CH)
                    for c in range(CH):
                        if c == CH - 1:
                            pe.wait_ge(g_ready, i + 1)
                        mm = pe.matmul(ps_a[1 + c][:, :], win[:, INNER + P * c : INNER + P * c + P], xnT[:, :], start=True, stop=True)
                        mm.then_inc(in_mm, 1)
                    pe.wait_ge(x_ready, SUP * i + 1)
                    pe.wait_ge(b_ready, SUP * i + 1)
                    for g in range(SUP):
                        mm = pe.matmul(ps_b[g][:, 0:ZD], xnT[:, P * g : P * g + P], wzd[:, :], start=True, stop=True)
                        mm.then_inc(z_mm, 1)

                def finish(i, last):
                    pe.wait_ge(xs_ready, CH * i + CH)
                    if last:
                        pe.wait_ge(x_ready, SUP * i + SUP + 1)
                        pe.wait_ge(b_ready, SUP * i + SUP + 1)
                        pe.wait_ge(g_ready, i + 2)
                    pe.matmul(ps_a[0][:, :], pick[:, :], xs[:, 2, :, :], start=True, stop=True).then_inc(c_mm, 1)
                    for g in range(SUP):
                        held = SUP * i + g + (1 if last else SUP + 1)
                        pe.wait_ge(z_ready, held)
                        pe.wait_ge(dt_ready, held)
                        for c in range(CH):
                            mm = pe.transpose(ps_b[g][:, P * c : P * c + P], xs[:, c, g // 2, P * (g % 2) : P * (g % 2) + P], ident[:, :])
                        mm.then_inc(turned, 1)
                    pe.wait_ge(c_ready, i + 1)
                    if not last:
                        pe.wait_ge(in_ready, CH * i + 3 * CH)
                    for g in range(SUP):
                        mm = pe.matmul(ps_a[CH][:, P * g : P * g + P], xs[:, 2, g // 2, P * (g % 2) : P * (g % 2) + P],
                                       cs[:, P * g : P * g + P], start=True, stop=True)
                    mm.then_inc(g_mm, 1)

                pe.sem_inc(in_ready, CH)
                pe.sem_inc(g_ready, 2)
                pe.sem_inc(x_ready, SUP + 1)
                turn_x(0)
                project(0)
                turn_x(1)
                pe.wait_ge(dt_ready, SUP)
                with pe.Fori(0, NSUP - 2) as i:
                    project(i + 1)
                    finish(i, False)
                    turn_x(i + 2)
                project(NSUP - 1)
                finish(NSUP - 2, False)
                finish(NSUP - 1, True)

            @block.scalar
            def _(act):
                act.preload_act_table(ACT.Silu)
                act.wait_ge(padded, 1)

                def copy_x(i):
                    act.wait_ge(xn_transposed, i + 1)
                    act.activation(xnT[:, :], ps_a[0][:, :], ACT.Copy).then_inc(xnT_ready, 1)

                def copy_projections(i):
                    for c in range(CH):
                        act.wait_ge(in_mm, CH * i + c + 1)
                        act.activation(pad[:, c, :, first : first + S], ps_a[1 + c][:, :].rearrange("p (b s) -> p b s", b=NB),
                                       ACT.Copy).then_inc(in_ready, 1)
                    for g in range(SUP):
                        act.wait_ge(z_mm, SUP * i + g + 1)
                        act.activation(tiles(store["z"], i, g), ps_b[g][:, 0:INNER], ACT.Silu).then_inc(z_ready, 1)

                def convolved(i, first_time):
                    for c in range(CH):
                        act.wait_ge(conv, CONV * i + TAPS * (c + 1))
                        if c == CH - 1 and not first_time:
                            act.wait_ge(g_mm, i)
                        act.activation(xs[:, c, :, :], acc[:, c, :, :], ACT.Silu).then_inc(xs_ready, 1)

                def copy_finished(i):
                    act.wait_ge(c_mm, i + 1)
                    act.wait_ge(c_kept, i + 1)
                    act.activation(cs[:, :], ps_a[0][:, :], ACT.Copy).then_inc(c_ready, 1)
                    for g in range(SUP):
                        act.wait_ge(turned, SUP * i + g + 1)
                        act.activation(tiles(store["x"], i, g), ps_b[g][:, 0:INNER], ACT.Copy).then_inc(x_ready, 1)

                copy_x(0)
                copy_projections(0)
                copy_x(1)
                convolved(0, True)
                with act.Fori(0, NSUP - 2) as i:
                    copy_projections(i + 1)
                    copy_finished(i)
                    copy_x(i + 2)
                    convolved(i + 1, False)
                copy_projections(NSUP - 1)
                copy_finished(NSUP - 2)
                convolved(NSUP - 1, False)
                copy_finished(NSUP - 1)

            @block.vector
            def _(dve):
                dve.wait_ge(loaded, 16 * NLOAD)
                dve.sem_inc(b_ready, SUP + 1)

                def norm_x(i):
                    for g in range(SUP):
                        norm.tile(dve, xn[:, g, :], x, B * (g % 2) + NB * i + g // 2).then_inc(xn_ready, 1)

                def convolve(i, first_time):
                    for c in range(CH):
                        dve.wait_ge(in_ready, CH * i + c + CH + 1)
                        if not first_time:
                            dve.wait_ge(xs_ready, CH * i + c - CH + 1)
                        for n in range(TAPS):
                            at = TAPS - 1 - n if backward else n
                            src = pad[:, c, :, at : at + S]
                            if n == 0:
                                op = dve.tensor_scalar(acc[:, c, :, :], src, cw[:, c, 0:1], cb[:, c : c + 1], ALU.mult, ALU.add)
                            else:
                                dve.wait_ge(conv, CONV * i + TAPS * c + n)
                                op = dve.scalar_tensor_tensor(acc[:, c, :, :], src, cw[:, c, n : n + 1], acc[:, c, :, :],
                                                              ALU.mult, ALU.add)
                            op.then_inc(conv, 1)
                        if c == 0:
                            for g in range(SUP):
                                dve.wait_ge(z_mm, SUP * i + g + 1)
                                dve.wait_ge(z_ready, SUP * i + g + 1)
                                dve.tensor_copy(tiles(store["dt"], i, g), ps_b[g][:, INNER:ZD]).then_inc(dt_ready, 1)

                def finish(i):
                    for g in range(SUP):
                        dve.wait_ge(turned, SUP * i + g + 1)
                        dve.wait_ge(x_ready, SUP * i + SUP + g + 2)
                        dve.tensor_copy(tiles(store["b"], i, g), ps_b[g][:, INNER : INNER + STATE]).then_inc(b_ready, 1)
                    dve.wait_ge(g_mm, i + 1)
                    for g in range(SUP):
                        op = dve.tensor_tensor(tiles(store["g"], i, g), ps_a[CH][:, P * g : P * g + P], w["inc"][:, :], ALU.mult)
                    op.then_inc(g_ready, 1)

                norm_x(0)
                dve.wait_ge(xn_transposed, 1)
                norm_x(1)
                convolve(0, True)
                with dve.Fori(0, NSUP - 2) as i:
                    dve.wait_ge(xn_transposed, i + 2)
                    norm_x(i + 2)
                    convolve(i + 1, False)
                    finish(i)
                convolve(NSUP - 1, False)
                finish(NSUP - 2)
                finish(NSUP - 1)


def ssm_scan(nc, ident, m, backward, w, store, y_out, ssq):
    FAR = -120.0
    GX = HEADS * P
    with ExitStack() as stack:
        k = Scope(nc, stack, m.prefix + "s")
        small = k.sb("small", [P, 10, NT, HEADS])
        dtb = k.sb("dt_bias", [P, HEADS])
        alog = k.sb("a_log", [P, HEADS])
        aneg = k.sb("a_neg", [P, HEADS])
        dp = k.sb("dp", [P, HEADS])
        nw = k.sb("norm_w", [P, 2])
        ow_raw = k.sb("out_w_raw", [P, 2, D])
        ow = k.sb("out_w", [P, 2, D])
        strict = k.sb("strict", [P, P])
        an = k.sb("a_masked", [P, 2, HEADS, P])
        ex = k.sb("decay", [P, 2, HEADS, P])
        mt = k.sb("mt", [P, 2, HEADS, P])
        u = k.sb("u", [P, 2, HEADS, HEADDIM])
        ud = k.sb("u_decayed", [P, HEADS, HEADDIM])
        xd = k.sb("x_skip", [P, 2, HEADS, HEADDIM])
        bs = k.sb("b_staged", [P, STATE])
        cst = k.sb("c_staged", [STATE, P])
        st = k.sb("state", [STATE, INNER])
        eb = k.sb("edge_decay", [P, 2, HEADS])
        yi = k.sb("y_inter", [P, HEADS, HEADDIM])
        y1 = k.sb("y1", [P, 2, INNER])
        y2 = k.sb("y2", [P, 2, INNER])
        y3 = k.sb("y3", [P, 2, INNER])
        sq = k.sb("squares", [P, 2, INNER])
        yT = k.sb("yT", [P, 2, 2, P])
        ps_d = [k.ps(f"ps_d{n}", [P, HEADS, P]) for n in range(2)]
        ps_y = [k.ps(f"ps_y{n}", [P, 512]) for n in range(2)]
        ps_e = k.ps("ps_e", [P, 512])
        ps_s = k.ps("ps_s", [P, 512])
        ps_t = [k.ps(f"ps_t{n}", [P, 512]) for n in range(2)]
        loaded, prep, a_sem = k.sem("loaded"), k.sem("prep"), k.sem("act_prep")
        masked_ready, d_mm, ex_ready = k.sem("a_masked_ready"), k.sem("d_mm"), k.sem("ex_ready")
        staged, edge_mm, edge_ready = k.sem("staged"), k.sem("edge_mm"), k.sem("edge_ready")
        u_ready, mt_ready, ud_ready = k.sem("u_ready"), k.sem("mt_ready"), k.sem("ud_ready")
        state_mm, state_ready, inter_mm, inter_ready = k.sem("state_mm"), k.sem("state_ready"), k.sem("inter_mm"), k.sem("inter_ready")
        y_mm, y1_ready, y2_ready, y3_ready = k.sem("y_mm"), k.sem("y1_ready"), k.sem("y2_ready"), k.sem("y3_ready")
        sq_ready, turned, yT_ready, out_mm, out_ready = (k.sem("sq_ready"), k.sem("turned"), k.sem("yT_ready"),
                                                         k.sem("out_mm"), k.sem("out_ready"))
        xd_ready = k.sem("xd_ready")
        NLOAD = 6
        order = (1, 0) if backward else (0, 1)

        def tile(q, b):
            return B * order[q] + b

        dt, a = small[:, 8, :, :], small[:, 9, :, :]
        with nc.Block() as block:

            @block.sync
            def _(sp):
                for dst, src in ((dtb[:, :], w["dt_bias"]), (alog[:, :], w["a_log"]), (dp[:, :], w["dp"]),
                                 (nw[:, :], w["norm_w"]), (ow_raw[:, :, :], w["out_w"]), (strict[:, :], w["strict"])):
                    sp.dma_start(dst, src).then_inc(loaded, 16)

            @block.gpsimd
            def _(pool):
                pool.wait_ge(prep, 9)
                pool.sem_inc(staged, 2)
                with pool.Fori(0, B) as b:
                    for q in range(2):
                        pool.wait_ge(d_mm, 2 * b + q + 1)
                        pool.tensor_tensor(an[:, q, :, :], bcast(w["inc"][:, :], HEADS, 1), bcast(a[:, tile(q, b), :], P, 2),
                                           ALU.mult).then_inc(masked_ready, 1)
                    pool.wait_ge(state_mm, b + 1)
                    pool.tensor_copy(bs[:, :], store["b"][:, tile(0, b), :]).then_inc(staged, 1)
                    pool.wait_ge(inter_mm, b + 1)
                    pool.tensor_copy(cst[:, :], store["c"][:, tile(1, b), :]).then_inc(staged, 1)
                    for q in range(2):
                        pool.wait_ge(y1_ready, 2 * b + q + 1)
                        view = store["x"][:, tile(q, b), :].rearrange("p (h d) -> p h d", h=HEADS)
                        pool.tensor_tensor(xd[:, q, :, :], view, bcast(dp[:, :], HEADDIM, 2), ALU.mult).then_inc(xd_ready, 1)

            @block.tensor
            def _(pe):
                pe.wait_ge(prep, 9)
                pe.sem_inc(d_mm, 2)
                pe.sem_inc(state_mm, 1)
                pe.sem_inc(inter_mm, 1)

                def decays(b, q):
                    n = 2 * b + q
                    pe.wait_ge(masked_ready, n + 1)
                    pe.wait_ge(ex_ready, n + 1)
                    pe.matmul(ps_d[q][:, :, :], strict[:, :], an[:, q, :, :], start=True, stop=True).then_inc(d_mm, 1)
                    pe.wait_ge(edge_ready, n + 1)
                    lhs = strict if q == 0 else w["inc"]
                    pe.matmul(ps_e[:, 0:HEADS], lhs[:, :], a[:, tile(q, b), :], start=True, stop=True).then_inc(edge_mm, 1)

                def product(b, q):
                    n = 2 * b + q
                    pe.wait_ge(mt_ready, n + 1)
                    pe.wait_ge(u_ready, n + 1)
                    pe.wait_ge(y1_ready, n + 1)
                    for h in range(HEADS):
                        mm = pe.matmul(ps_y[q][:, HEADDIM * h : HEADDIM * h + HEADDIM], mt[:, q, h, :], u[:, q, h, :], start=True, stop=True)
                    mm.then_inc(y_mm, 1)

                def carry(b, q):
                    pe.wait_ge(staged, 2 * b + q + 3)
                    if q == 0:
                        pe.wait_ge(ud_ready, b + 1)
                        pe.matmul(ps_s[0:STATE, 0:INNER], bs[:, :], ud[:, :, :], start=True, stop=True).then_inc(state_mm, 1)
                    else:
                        pe.wait_ge(state_ready, b + 1)
                        pe.matmul(ps_s[:, 0:INNER], cst[:, :], st[:, :], start=True, stop=True).then_inc(inter_mm, 1)

                def turn(b, q):
                    n = 2 * b + q
                    pe.wait_ge(y3_ready, n + 1)
                    pe.wait_ge(out_ready, n + 1)
                    for c in range(2):
                        mm = pe.transpose(ps_t[q][:, P * c : P * c + P], y3[:, q, P * c : P * c + P], ident[:, :])
                    mm.then_inc(turned, 1)

                def out(b, q):
                    pe.wait_ge(yT_ready, 2 * b + q + 1)
                    for c in range(2):
                        mm = pe.matmul(ps_t[q][:, INNER : INNER + D], yT[:, q, c, :], ow[:, c, :], start=(c == 0), stop=(c == 1))
                    mm.then_inc(out_mm, 1)

                def batch(b, last):
                    carry(b, 0)
                    product(b, 0)
                    if not last:
                        decays(b + 1, 0)
                    carry(b, 1)
                    product(b, 1)
                    if not last:
                        decays(b + 1, 1)
                    turn(b, 0)
                    turn(b, 1)
                    out(b, 0)
                    out(b, 1)

                decays(0, 0)
                decays(0, 1)
                with pe.Fori(0, B - 1) as b:
                    batch(b, False)
                batch(B - 1, True)

            @block.scalar
            def _(act):
                act.wait_ge(loaded, 16 * NLOAD)
                act.activation(aneg[:, :], alog[:, :], ACT.Exp).then_inc(a_sem, 1)
                act.wait_ge(prep, 4)
                act.activation(small[:, 3, :, :], small[:, 2, :, :], ACT.Exp, scale=-1.0).then_inc(a_sem, 1)
                act.wait_ge(a_sem, 2)
                act.activation(small[:, 4, :, :], small[:, 3, :, :], ACT.Ln, bias=1.0).then_inc(a_sem, 1)
                act.wait_ge(a_sem, 3)
                act.preload_act_table(ACT.Exp)
                act.sem_inc(ex_ready, 2)
                act.sem_inc(edge_ready, 1)

                def decays(b, q):
                    n = 2 * b + q
                    act.wait_ge(d_mm, n + 3)
                    act.activation(ex[:, q, :, :], ps_d[q][:, :, :], ACT.Exp).then_inc(ex_ready, 1)
                    act.wait_ge(edge_mm, n + 1)
                    if q == 1:
                        act.wait_ge(inter_ready, 2 * b + 1)
                    act.activation(eb[:, q, :], ps_e[:, 0:HEADS], ACT.Exp).then_inc(edge_ready, 1)

                def copy_state(b):
                    act.wait_ge(state_mm, b + 2)
                    act.activation(st[:, :], ps_s[0:STATE, 0:INNER], ACT.Copy).then_inc(state_ready, 1)

                def square(b, q):
                    n = 2 * b + q
                    act.wait_ge(y3_ready, n + 1)
                    act.activation(sq[:, q, :], y3[:, q, :], ACT.Square, accum_out=ssq[:, bass.ds(tile(q, b), 1)]).then_inc(sq_ready, 1)
                    act.wait_ge(turned, n + 1)
                    act.activation(yT[:, q, :, :], ps_t[q][:, 0:INNER].rearrange("p (c j) -> p c j", c=2), ACT.Copy).then_inc(yT_ready, 1)

                def copy_out(b, q):
                    act.wait_ge(out_mm, 2 * b + q + 1)
                    act.activation(y_out[:, tile(q, b), :], ps_t[q][:, INNER : INNER + D], ACT.Copy).then_inc(out_ready, 1)

                def batch(b, last):
                    copy_state(b)
                    if not last:
                        decays(b + 1, 0)
                        decays(b + 1, 1)
                    square(b, 0)
                    square(b, 1)
                    copy_out(b, 0)
                    copy_out(b, 1)

                act.sem_inc(out_ready, 2)
                decays(0, 0)
                decays(0, 1)
                with act.Fori(0, B - 1) as b:
                    batch(b, False)
                batch(B - 1, True)
                act.wait_ge(out_ready, NT + 2)

            @block.vector
            def _(dve):
                dve.wait_ge(loaded, 16 * NLOAD)
                s = lambda n: small[:, n, :, :]
                dve.tensor_tensor(s(0), store["dt"][:, :, :], bcast(dtb[:, :], NT, 1), ALU.add).then_inc(prep, 1)
                dve.wait_ge(prep, 1)
                dve.tensor_scalar(s(1), s(0), -1.0, None, ALU.mult).then_inc(prep, 1)
                dve.tensor_scalar(s(5), s(0), 0.0, None, ALU.max).then_inc(prep, 1)
                dve.wait_ge(prep, 3)
                dve.tensor_tensor(s(2), s(0), s(1), ALU.max).then_inc(prep, 1)
                for c in range(2):
                    dve.tensor_scalar(ow[:, c, :], ow_raw[:, c, :], nw[:, c : c + 1], None, ALU.mult).then_inc(prep, 1)
                dve.wait_ge(a_sem, 3)
                dve.tensor_tensor(dt, s(4), s(5), ALU.add).then_inc(prep, 1)
                dve.wait_ge(prep, 7)
                dve.scalar_tensor_tensor(s(6), dt, -1.0, bcast(aneg[:, :], NT, 1), ALU.mult, ALU.mult).then_inc(prep, 1)
                dve.wait_ge(prep, 8)
                dve.tensor_scalar(a, s(6), FAR, None, ALU.max).then_inc(prep, 1)
                dve.wait_ge(prep, 9)
                dve.sem_inc(y1_ready, 2)
                dve.sem_inc(inter_ready, 2)

                def inputs(b, q):
                    t = tile(q, b)
                    view = store["x"][:, t, :].rearrange("p (h d) -> p h d", h=HEADS)
                    dve.tensor_tensor(u[:, q, :, :], view, bcast(dt[:, t, :], HEADDIM, 2), ALU.mult).then_inc(u_ready, 1)
                    if q == 0:
                        dve.wait_ge(edge_ready, 2 * b + 2)
                        dve.wait_ge(u_ready, 2 * b + 1)
                        dve.tensor_tensor(ud[:, :, :], u[:, 0, :, :], bcast(eb[:, 0, :], HEADDIM, 2), ALU.mult).then_inc(ud_ready, 1)
                    dve.wait_ge(ex_ready, 2 * b + q + 3)
                    dve.tensor_tensor(mt[:, q, :, :], ex[:, q, :, :], bcast(store["g"][:, t, :], HEADS, 1), ALU.mult).then_inc(mt_ready, 1)

                def gate(b, q):
                    n, t = 2 * b + q, tile(q, b)
                    flat = lambda ap: ap.rearrange("p h d -> p (h d)")
                    skip = flat(xd[:, q, :, :])
                    if q == 1:
                        dve.wait_ge(inter_mm, b + 2)
                        dve.wait_ge(edge_ready, 2 * b + 3)
                        dve.tensor_tensor(yi[:, :, :], ps_s[:, 0:INNER].rearrange("p (h d) -> p h d", h=HEADS),
                                          bcast(eb[:, 1, :], HEADDIM, 2), ALU.mult).then_inc(inter_ready, 1)
                        dve.wait_ge(inter_ready, 2 * b + 3)
                        dve.wait_ge(xd_ready, n + 1)
                        dve.tensor_tensor(y1[:, 0, :], flat(yi[:, :, :]), skip, ALU.add).then_inc(inter_ready, 1)
                        dve.wait_ge(inter_ready, 2 * b + 4)
                        skip = y1[:, 0, :]
                    dve.wait_ge(y_mm, n + 1)
                    dve.wait_ge(xd_ready, n + 1)
                    dve.tensor_tensor(y2[:, q, :], ps_y[q][:, 0:INNER], skip, ALU.add).then_inc(y1_ready, 1)
                    dve.wait_ge(y1_ready, n + 3)
                    dve.tensor_tensor(y3[:, q, :], y2[:, q, :], store["z"][:, t, :], ALU.mult).then_inc(y3_ready, 1)

                def batch(b, last):
                    gate(b, 0)
                    if not last:
                        inputs(b + 1, 0)
                    gate(b, 1)
                    if not last:
                        inputs(b + 1, 1)

                inputs(0, 0)
                inputs(0, 1)
                with dve.Fori(0, B - 1) as b:
                    batch(b, False)
                batch(B - 1, True)


def state_space(nc, x, ident, dirs):
    with ExitStack() as stack:
        m = Scope(nc, stack, "ss")
        norm = Norm(m)
        norm_statistics(nc, x, norm)
        y_out = [m.sb(f"y_out{n}", [P, NT, D]) for n in range(2)]
        ssq = [m.sb(f"ssq{n}", [P, NT]) for n in range(2)]
        inc = m.sb("inclusive", [P, P])
        store = {
            "z": m.sb("silu_z", [P, NT, INNER]), "x": m.sb("x_tok", [P, NT, INNER]), "b": m.sb("b_tok", [P, NT, STATE]),
            "c": m.sb("c_feat", [STATE, NT, P]), "g": m.sb("scores", [P, NT, P]), "dt": m.sb("dt_raw", [P, NT, HEADS]),
        }
        inc_loaded = m.sem("inc_loaded")
        for n, w in enumerate(dirs):
            with nc.Block() as block:

                @block.sync
                def _(sp):
                    sp.dma_start(inc[:, :], w["inclusive"]).then_inc(inc_loaded, 16)
                    sp.wait_ge(inc_loaded, 16 * n + 16)

            w = dict(w, inc=inc)
            k = Scope(nc, stack, f"ss{n}")
            ssm_inputs(nc, x, ident, norm, k, n == 1, w, store)
            ssm_scan(nc, ident, k, n == 1, w, store, y_out[n], ssq[n])

        mean = m.sb("mean_square", [P, 2, NT])
        root = m.sb("root", [P, 2, NT])
        r = m.sb("rms", [P, 2, NT])
        meant, rooted, inv, added = m.sem("meant"), m.sem("rooted"), m.sem("inverted"), m.sem("added")
        scaled = m.sem("scaled")
        with nc.Block() as block:

            @block.scalar
            def _(act):
                act.wait_ge(meant, 2)
                act.activation(root[:, :, :], mean[:, :, :], ACT.Sqrt).then_inc(rooted, 1)

            @block.vector
            def _(dve):
                for n in range(2):
                    dve.tensor_scalar(mean[:, n, :], ssq[n][:, :], 1.0 / INNER, EPS, ALU.mult, ALU.add).then_inc(meant, 1)
                dve.wait_ge(rooted, 1)
                dve.reciprocal(r[:, :, :], root[:, :, :]).then_inc(inv, 1)
                dve.wait_ge(inv, 1)
                dve.tensor_tensor(y_out[0][:, :, :], y_out[0][:, :, :], bcast(r[:, 0, :], D, 2), ALU.mult).then_inc(added, 1)
                dve.wait_ge(added, 1)
                dve.tensor_tensor(x[:, :, :], x[:, :, :], y_out[0][:, :, :], ALU.add).then_inc(added, 1)
                dve.wait_ge(added, 2)
                dve.wait_ge(scaled, 1)
                dve.tensor_tensor(x[:, :, :], x[:, :, :], y_out[1][:, :, :], ALU.add).then_inc(added, 1)
                dve.wait_ge(added, 3)

            @block.gpsimd
            def _(pool):
                pool.wait_ge(inv, 1)
                pool.tensor_tensor(y_out[1][:, :, :], y_out[1][:, :, :], bcast(r[:, 1, :], D, 2), ALU.mult).then_inc(scaled, 1)


def cross_attention(nc, x, ident, ctxT_dram, ctx2T_dram, mask_dram, wq_dram, wk_dram, wv_dram, wo_dram):
    H, HD, K = 16, 64, 64
    HP = H // 2
    SCALE = 1.0 / HD**0.5
    with ExitStack() as stack:
        m = Scope(nc, stack, "xa")
        norm = Norm(m)
        mask = m.sb("mask", [P, NT, K])
        wq = m.sb("wq", [D, H * HD])
        wo = m.sb("wo", [P, HP, D])
        keys = m.sb("keys", [P, HP, B, K])
        vals = m.sb("vals", [P, B, HP, HD])
        kblock = m.sb("kblock", [P, HP, 2, K])
        vblock = m.sb("vblock", [P, HP, 2, HD])
        load_done = m.sem("loaded")
        zeroed = m.sem("blocks_zeroed")
        with ExitStack() as inner:
            k = Scope(nc, inner, "xk")
            ctxT = k.sb("ctxT", [D, B * K])
            ctx2T = k.sb("ctx2T", [D, B, 2 * K])
            wk = k.sb("wk", [D, H * HD])
            wv = k.sb("wv", [D, H * HD])
            ps_k = [k.ps(f"ps_k{n}", [P, 8, K]) for n in range(4)]
            ps_v = [k.ps(f"ps_v{n}", [P, HP, 2, HD]) for n in range(2)]
            key_mm, key_ready = k.sem("key_mm"), k.sem("key_ready")
            val_mm, val_low, val_high = k.sem("val_mm"), k.sem("val_low"), k.sem("val_high")
            ctx_copied, raw_masked = k.sem("ctx_copied"), k.sem("masked")
            NLOAD = 7
            with nc.Block() as block:

                @block.sync
                def _(sp):
                    for dst, src in ((ctxT[:, :], ctxT_dram), (wk[:, :], wk_dram), (ctx2T[:, :, :], ctx2T_dram), (wv[:, :], wv_dram),
                                     (mask[:, :, :], mask_dram), (wq[:, :], wq_dram),
                                     (wo[:, :, :], wo_dram.rearrange("(c p) n -> p c n", p=P))):
                        sp.dma_start(dst, src).then_inc(load_done, 16)

                @block.gpsimd
                def _(pool):
                    pool.memset(kblock[:, :, :, :], 0.0).then_inc(zeroed, 1)
                    pool.memset(vblock[:, :, :, :], 0.0).then_inc(zeroed, 1)

                @block.tensor
                def _(pe):
                    pe.wait_ge(load_done, 16 * NLOAD)
                    for c in range(HP):
                        for n in range(2):
                            f = 2 * c + n
                            if f >= 4:
                                pe.wait_ge(key_ready, f - 3)
                            pe.matmul(ps_k[f % 4][:, :, :], wk[:, P * c : P * c + P], ctxT[:, 512 * n : 512 * n + 512],
                                      start=True, stop=True).then_inc(key_mm, 1)
                    for b in range(B):
                        if b >= 2:
                            pe.wait_ge(val_low, b - 1)
                            pe.wait_ge(val_high, b - 1)
                        for n in range(2):
                            mm = pe.matmul(ps_v[b % 2][:, 4 * n : 4 * n + 4, :, :], ctx2T[:, b, :], wv[:, 512 * n : 512 * n + 512],
                                           start=True, stop=True)
                        mm.then_inc(val_mm, 1)

                @block.scalar
                def _(act):
                    norm.act(act, ACT.Exp)
                    for f in range(2 * HP):
                        act.wait_ge(key_mm, f + 1)
                        act.activation(keys[:, f // 2, 8 * (f % 2) : 8 * (f % 2) + 8, :], ps_k[f % 4][:, :, :], ACT.Copy).then_inc(key_ready, 1)
                    for b in range(B):
                        act.wait_ge(val_mm, b + 1)
                        act.activation(vals[0:K, b, :, :], ps_v[b % 2][0:K, :, 0, :], ACT.Copy).then_inc(val_low, 1)

                @block.vector
                def _(dve):
                    norm.dve(dve, x)
                    dve.wait_ge(load_done, 16 * NLOAD)
                    dve.tensor_scalar(mask[:, :, :], mask[:, :, :], -1.0e9, None, ALU.mult).then_inc(raw_masked, 1)
                    for b in range(B):
                        dve.wait_ge(val_mm, b + 1)
                        dve.tensor_copy(vals[K:P, b, :, :], ps_v[b % 2][K:P, :, 1, :]).then_inc(val_high, 1)

        xn = m.sb("xn", [P, 2, D])
        xnT = m.sb("xnT", [D, 2 * P])
        qT = m.sb("qT", [P, HP, 2 * P])
        logits = m.sb("logits", [P, 2, H, K])
        rowmax = m.sb("rowmax", [P, 2, H])
        shifted = m.sb("shifted", [P, 2, H, K])
        probs = m.sb("probs", [P, 2, H, K])
        rowsum = m.sb("rowsum", [P, 2, H])
        rinv = m.sb("rinv", [P, 2, H])
        normed = m.sb("normed", [P, 2, H * K])
        probsT = m.sb("probsT", [P, HP, P])
        oT = m.sb("oT", [P, 2, HP, P])
        ps_m = [m.ps(f"ps_m{n}", [P, 512]) for n in range(2)]
        ps_s = [m.ps(f"ps_s{n}", [P, H, K]) for n in range(2)]
        ps_a = [m.ps(f"ps_a{n}", [P, HP // 2, P]) for n in range(2)]
        xn_ready, xn_transposed, xnT_ready = m.sem("xn_ready"), m.sem("xn_transposed"), m.sem("xnT_ready")
        q_mm, q_ready = m.sem("q_mm"), m.sem("q_ready")
        kblock_ready, vblock_ready = m.sem("kblock_ready"), m.sem("vblock_ready")
        scored, logits_ready, max_ready = m.sem("scored"), m.sem("logits_ready"), m.sem("max_ready")
        shifted_ready, exp_ready = m.sem("shifted_ready"), m.sem("exp_ready")
        sum_ready, rinv_ready, normed_ready = m.sem("sum_ready"), m.sem("rinv_ready"), m.sem("normed_ready")
        probs_transposed, probsT_ready = m.sem("probs_transposed"), m.sem("probsT_ready")
        attended, oT_ready, projected, x_out = m.sem("attended"), m.sem("oT_ready"), m.sem("projected"), m.sem("x_out")
        QF = HP // 2

        with nc.Block() as block:

            @block.gpsimd
            def _(pool):
                def stage(b):
                    for e in range(2):
                        rows = slice(K * e, K * e + K)
                        pool.tensor_copy(kblock[rows, :, e, :], keys[rows, :, b, :]).then_inc(kblock_ready, 1)

                def stage_values(b):
                    for e in range(2):
                        rows = slice(K * e, K * e + K)
                        pool.tensor_copy(vblock[rows, :, e, :], vals[rows, b, :, :]).then_inc(vblock_ready, 1)

                stage(0)
                stage_values(0)
                with pool.Fori(1, B) as b:
                    pool.wait_ge(scored, 2 * b)
                    stage(b)
                    pool.wait_ge(attended, 4 * b)
                    stage_values(b)

            @block.tensor
            def _(pe):
                def turn_x(b):
                    pe.wait_ge(xn_ready, 2 * b + 2)
                    for u in range(2):
                        mm = pe.transpose(ps_m[0][:, P * u : P * u + P], xn[:, u, :], ident[:, :])
                    mm.then_inc(xn_transposed, 1)

                def queries(b):
                    pe.wait_ge(xnT_ready, b + 1)
                    for f in range(QF):
                        if f >= 2:
                            pe.wait_ge(q_ready, QF * b + f - 1)
                        for c in range(2):
                            w = 2 * f + c
                            mm = pe.matmul(ps_m[(f + 1) % 2][:, 256 * c : 256 * c + 256], wq[:, P * w : P * w + P], xnT[:, :],
                                           start=True, stop=True)
                        mm.then_inc(q_mm, 1)

                def scores(b, u):
                    if u == 0:
                        pe.wait_ge(q_ready, QF * b + QF)
                        pe.wait_ge(kblock_ready, 2 * b + 2)
                    for c in range(HP):
                        mm = pe.matmul(ps_s[u][:, 2 * c : 2 * c + 2, :], qT[:, c, P * u : P * u + P], kblock[:, c, :, :],
                                       start=True, stop=True)
                    mm.then_inc(scored, 1)

                def turn_probs(b, u):
                    pe.wait_ge(normed_ready, 2 * b + u + 1)
                    for c in range(HP):
                        mm = pe.transpose(ps_a[c // 4][:, c % 4, :], normed[:, u, P * c : P * c + P], ident[:, :])
                        if c % 4 == 3:
                            mm.then_inc(probs_transposed, 1)

                def attend(b, u):
                    pe.wait_ge(vblock_ready, 2 * b + 2)
                    for n in range(2):
                        pe.wait_ge(probsT_ready, 2 * (2 * b + u) + n + 1)
                        for c in range(4 * n, 4 * n + 4):
                            mm = pe.matmul(ps_a[n][:, c % 4, :], vblock[:, c, :, :], probsT[:, c, :], start=True, stop=True)
                        mm.then_inc(attended, 1)

                def project(b, u):
                    pe.wait_ge(oT_ready, 2 * (2 * b + u) + 2)
                    for c in range(HP):
                        mm = pe.matmul(ps_m[(u + 1) % 2][:, 0:D], oT[:, u, c, :], wo[:, c, :], start=(c == 0), stop=(c == HP - 1))
                    mm.then_inc(projected, 1)

                turn_x(0)
                queries(0)
                scores(0, 0)
                scores(0, 1)
                with pe.Fori(1, B) as b:
                    turn_x(b)
                    queries(b)
                    turn_probs(b - 1, 0)
                    scores(b, 0)
                    attend(b - 1, 0)
                    pe.wait_ge(oT_ready, 4 * b - 2)
                    turn_probs(b - 1, 1)
                    project(b - 1, 0)
                    attend(b - 1, 1)
                    project(b - 1, 1)
                    scores(b, 1)
                    pe.wait_ge(oT_ready, 4 * b)
                    pe.wait_ge(x_out, 2 * b)
                turn_probs(B - 1, 0)
                attend(B - 1, 0)
                pe.wait_ge(oT_ready, 4 * B - 2)
                turn_probs(B - 1, 1)
                attend(B - 1, 1)
                project(B - 1, 0)
                project(B - 1, 1)

            @block.scalar
            def _(act):
                def copy_x(b):
                    act.wait_ge(xn_transposed, b + 1)
                    act.activation(xnT[:, :], ps_m[0][:, 0:256], ACT.Copy).then_inc(xnT_ready, 1)

                def copy_q(b, fills):
                    for f in fills:
                        act.wait_ge(q_mm, QF * b + f + 1)
                        act.activation(qT[:, 2 * f : 2 * f + 2, :], ps_m[(f + 1) % 2][:, :].rearrange("p (c j) -> p c j", c=2),
                                       ACT.Copy, scale=SCALE).then_inc(q_ready, 1)

                def exp(b, u):
                    act.wait_ge(shifted_ready, 2 * b + u + 1)
                    act.activation(probs[:, u, :, :], shifted[:, u, :, :], ACT.Exp).then_inc(exp_ready, 1)

                def copy_probs(b, u):
                    for n in range(2):
                        act.wait_ge(probs_transposed, 2 * (2 * b + u) + n + 1)
                        act.activation(probsT[:, 4 * n : 4 * n + 4, :], ps_a[n][:, :, :], ACT.Copy).then_inc(probsT_ready, 1)

                def copy_o(b, u):
                    for n in range(2):
                        act.wait_ge(attended, 2 * (2 * b + u) + n + 1)
                        act.activation(oT[:, u, 4 * n : 4 * n + 4, :], ps_a[n][:, :, :], ACT.Copy).then_inc(oT_ready, 1)

                copy_x(0)
                copy_q(0, range(QF))
                exp(0, 0)
                with act.Fori(1, B) as b:
                    copy_x(b)
                    copy_q(b, range(QF - 1))
                    exp(b - 1, 1)
                    copy_q(b, range(QF - 1, QF))
                    copy_probs(b - 1, 0)
                    copy_o(b - 1, 0)
                    copy_probs(b - 1, 1)
                    exp(b, 0)
                    copy_o(b - 1, 1)
                exp(B - 1, 1)
                copy_probs(B - 1, 0)
                copy_o(B - 1, 0)
                copy_probs(B - 1, 1)
                copy_o(B - 1, 1)

            @block.vector
            def _(dve):
                def norm_x(b):
                    for u in range(2):
                        norm.tile(dve, xn[:, u, :], x, B * u + b).then_inc(xn_ready, 1)

                def shift(b, u):
                    n = 2 * b + u + 1
                    dve.wait_ge(scored, n)
                    dve.tensor_tensor(logits[:, u, :, :], ps_s[u][:, :, :], bcast(mask[:, B * u + b, :], H, 1),
                                      ALU.add).then_inc(logits_ready, 1)
                    dve.wait_ge(logits_ready, n)
                    dve.tensor_reduce(rowmax[:, u, :], logits[:, u, :, :], AX, ALU.max).then_inc(max_ready, 1)
                    dve.wait_ge(max_ready, n)
                    dve.tensor_tensor(shifted[:, u, :, :], logits[:, u, :, :], bcast(rowmax[:, u, :], K, 2),
                                      ALU.subtract).then_inc(shifted_ready, 1)

                def divide(b, u):
                    n = 2 * b + u + 1
                    dve.wait_ge(exp_ready, n)
                    dve.tensor_reduce(rowsum[:, u, :], probs[:, u, :, :], AX, ALU.add).then_inc(sum_ready, 1)
                    dve.wait_ge(sum_ready, n)
                    dve.reciprocal(rinv[:, u, :], rowsum[:, u, :]).then_inc(rinv_ready, 1)
                    dve.wait_ge(rinv_ready, n)
                    dve.tensor_tensor(normed[:, u, :].rearrange("p (h k) -> p h k", h=H), probs[:, u, :, :],
                                      bcast(rinv[:, u, :], K, 2), ALU.mult).then_inc(normed_ready, 1)

                def add(b, u):
                    dve.wait_ge(projected, 2 * b + u + 1)
                    t = B * u + b
                    dve.tensor_tensor(x[:, t, :], x[:, t, :], ps_m[(u + 1) % 2][:, 0:D], ALU.add).then_inc(x_out, 1)

                def batch(b, last):
                    divide(b - 1, 1)
                    if not last:
                        dve.wait_ge(xn_transposed, b + 1)
                        norm_x(b + 1)
                    shift(b, 0)
                    add(b - 1, 0)
                    divide(b, 0)
                    add(b - 1, 1)
                    shift(b, 1)

                norm_x(0)
                dve.wait_ge(xn_transposed, 1)
                norm_x(1)
                shift(0, 0)
                divide(0, 0)
                shift(0, 1)
                with dve.Fori(1, B - 1) as b:
                    batch(b, False)
                batch(B - 1, True)
                divide(B - 1, 1)
                add(B - 1, 0)
                add(B - 1, 1)
                dve.wait_ge(x_out, 2 * B)


def threshold_experts(nc, x, ident, gw_dram, gb_dram, ew_dram, eb_dram):
    E, THRESHOLD = 8, 0.1
    with ExitStack() as stack:
        m = Scope(nc, stack, "te")
        gw = m.sb("gate_w", [D, E])
        gb = m.sb("gate_b", [P, E])
        ew = m.sb("expert_w", [D, E * D])
        eb = m.sb("expert_b", [E, D])
        norm = Norm(m)
        xn = m.sb("xn", [P, SUP, D])
        xnT = m.sb("xnT", [D, SUP * P])
        gt = m.sb("gate", [P, 8, SUP, E])
        gs = m.sb("gate_stats", [P, 6, SUP])
        weight = m.sb("weight", [P, SUP, E])
        wT = m.sb("weightT", [E, SUP * P])
        acc = m.sb("acc", [P, 2, SUP, D])
        both = m.sb("both", [P, SUP, D])
        ps_t = m.ps("ps_t", [P, 512])
        ps_l = m.ps("ps_l", [P, 512])
        ps_w = m.ps("ps_w", [P, 512])
        ps_b = m.ps("ps_b", [P, SUP, D])
        ps_e = [m.ps(f"ps_e{n}", [P, E, D]) for n in range(2)]
        loaded = m.sem("loaded")
        xn_ready, xn_transposed, xnT_ready = m.sem("xn_ready"), m.sem("xn_transposed"), m.sem("xnT_ready")
        logits_mm, gate_step, gate_exp, weighted = m.sem("logits_mm"), m.sem("gate_step"), m.sem("gate_exp"), m.sem("weighted")
        expert_mm, acc_step = m.sem("expert_mm"), m.sem("acc_step")
        turned, wT_ready, bias_mm, x_step = m.sem("turned"), m.sem("wT_ready"), m.sem("bias_mm"), m.sem("x_step")
        NLOAD, GSTEPS = 4, 11
        ACCS = E * SUP

        with nc.Block() as block:

            @block.sync
            def _(sp):
                for dst, src in ((gw, gw_dram), (gb, gb_dram), (ew, ew_dram), (eb, eb_dram)):
                    sp.dma_start(dst[:, :], src).then_inc(loaded, 16)

            @block.tensor
            def _(pe):
                pe.wait_ge(loaded, 16 * NLOAD)
                with pe.Fori(0, NSUP) as i:
                    pe.wait_ge(xn_ready, SUP * i + SUP)
                    for g in range(SUP):
                        mm = pe.transpose(ps_t[:, P * g : P * g + P], xn[:, g, :], ident[:, :])
                    mm.then_inc(xn_transposed, 1)
                    pe.wait_ge(xnT_ready, i + 1)
                    for g in range(SUP):
                        mm = pe.matmul(ps_l[:, E * g : E * g + E], xnT[:, P * g : P * g + P], gw[:, :], start=True, stop=True)
                    mm.then_inc(logits_mm, 1)
                    for g in range(SUP):
                        if g < 2:
                            pe.wait_ge(acc_step, ACCS * i + 1)
                        if g >= 2:
                            pe.wait_ge(acc_step, ACCS * i + E * (g - 1) + 1)
                        for n in range(2):
                            mm = pe.matmul(ps_e[g % 2][:, 4 * n : 4 * n + 4, :], xnT[:, P * g : P * g + P],
                                           ew[:, 512 * n : 512 * n + 512], start=True, stop=True)
                        mm.then_inc(expert_mm, 1)
                        if g == 1:
                            pe.wait_ge(weighted, i + 1)
                            for t in range(SUP):
                                mm = pe.transpose(ps_w[0:E, P * t : P * t + P], weight[:, t, :], ident[:, :])
                            mm.then_inc(turned, 1)
                    pe.wait_ge(wT_ready, i + 1)
                    for t in range(SUP):
                        mm = pe.matmul(ps_b[:, t, :], wT[:, P * t : P * t + P], eb[:, :], start=True, stop=True)
                    mm.then_inc(bias_mm, 1)

            @block.scalar
            def _(act):
                norm.act(act, ACT.Exp)
                with act.Fori(0, NSUP) as i:
                    act.wait_ge(xn_transposed, i + 1)
                    act.activation(xnT[:, :], ps_t[:, :], ACT.Copy).then_inc(xnT_ready, 1)
                    act.wait_ge(gate_step, GSTEPS * i + 4)
                    act.activation(gt[:, 2, :, :], gt[:, 1, :, :], ACT.Exp).then_inc(gate_exp, 1)
                    act.wait_ge(turned, i + 1)
                    act.activation(wT[:, :], ps_w[0:E, :], ACT.Copy).then_inc(wT_ready, 1)

            @block.vector
            def _(dve):
                norm.dve(dve, x)
                dve.wait_ge(loaded, 16 * NLOAD)
                dve.sem_inc(acc_step, 1)
                dve.sem_inc(x_step, 1)
                dve.sem_inc(gate_step, 1)
                with dve.Fori(0, NSUP) as i:
                    dve.wait_ge(x_step, 3 * i + 1)
                    for g in range(SUP):
                        norm.tile(dve, xn[:, g, :], x, SUP * i + g).then_inc(xn_ready, 1)

                    g_ = lambda n: gt[:, n, :, :]
                    done = lambda n: dve.wait_ge(gate_step, GSTEPS * i + n + 1)
                    dve.wait_ge(logits_mm, i + 1)
                    dve.tensor_tensor(g_(0), ps_l[:, 0 : SUP * E].rearrange("p (g e) -> p g e", e=E),
                                      bcast(gb[:, :], SUP, 1), ALU.add).then_inc(gate_step, 1)
                    done(1)
                    dve.tensor_reduce(gs[:, 0, :], g_(0), AX, ALU.max).then_inc(gate_step, 1)
                    done(2)
                    dve.tensor_tensor(g_(1), g_(0), bcast(gs[:, 0, :], E, 2), ALU.subtract).then_inc(gate_step, 1)
                    dve.wait_ge(gate_exp, i + 1)
                    dve.tensor_reduce(gs[:, 1, :], g_(2), AX, ALU.add).then_inc(gate_step, 1)
                    done(4)
                    dve.reciprocal(gs[:, 2, :], gs[:, 1, :]).then_inc(gate_step, 1)
                    done(5)
                    dve.tensor_tensor(g_(3), g_(2), bcast(gs[:, 2, :], E, 2), ALU.mult).then_inc(gate_step, 1)
                    done(6)
                    dve.scalar_tensor_tensor(g_(4), g_(3), THRESHOLD, g_(3), ALU.is_ge, ALU.mult).then_inc(gate_step, 1)
                    done(7)
                    dve.tensor_reduce(gs[:, 3, :], g_(4), AX, ALU.add).then_inc(gate_step, 1)
                    done(8)
                    dve.scalar_tensor_tensor(gs[:, 4, :], gs[:, 3, :], 0.0, gs[:, 3, :], ALU.is_equal, ALU.add).then_inc(gate_step, 1)
                    done(9)
                    dve.reciprocal(gs[:, 5, :], gs[:, 4, :]).then_inc(gate_step, 1)
                    done(10)
                    dve.tensor_tensor(weight[:, :, :], g_(4), bcast(gs[:, 5, :], E, 2), ALU.mult).then_inc(weighted, 1)
                    dve.wait_ge(weighted, i + 1)
                    dve.sem_inc(gate_step, 1)

                    for g in range(SUP):
                        dve.wait_ge(expert_mm, SUP * i + g + 1)
                        for e in range(E):
                            out, src = acc[:, e % 2, g, :], ps_e[g % 2][:, e, :]
                            if e < 2:
                                op = dve.tensor_scalar(out, src, weight[:, g, e : e + 1], None, ALU.mult)
                            else:
                                dve.wait_ge(acc_step, ACCS * i + E * g + e)
                                op = dve.scalar_tensor_tensor(out, src, weight[:, g, e : e + 1], out, ALU.mult, ALU.add)
                            op.then_inc(acc_step, 1)
                    dve.wait_ge(acc_step, ACCS * i + ACCS + 1)
                    dve.tensor_tensor(both[:, :, :], acc[:, 0, :, :], acc[:, 1, :, :], ALU.add).then_inc(x_step, 1)
                    dve.wait_ge(x_step, 3 * i + 2)
                    dve.wait_ge(bias_mm, i + 1)
                    dve.tensor_tensor(acc[:, 0, :, :], both[:, :, :], ps_b[:, :, :], ALU.add).then_inc(x_step, 1)
                    dve.wait_ge(x_step, 3 * i + 3)
                    view = x[:, bass.ds(SUP * i, SUP), :]
                    dve.tensor_tensor(view, view, acc[:, 0, :, :], ALU.add).then_inc(x_step, 1)
                dve.wait_ge(x_step, 3 * NSUP + 1)


def decoder(nc, a, x1_dram, out_dram):
    take = lambda *names: [a[n] for n in names]
    with ExitStack() as stack:
        bias = Scope(nc, stack, "gb").sb("bias", [P, NT, 64])
        self_attention(nc, *take("x", "ident", "sa_mask", "sa_wq", "sa_wkv", "sa_bq", "sa_bk", "sa_bv", "sa_wp", "sa_bp"),
                       x1_dram, *take("idx", "bins"), bias)
        m = Scope(nc, stack, "g")
        x = m.sb("x", [P, NT, D])
        ident = m.sb("ident", [P, P])
        load_x(nc, x, ident, x1_dram, a["ident"])
        gathered_attention(nc, x, bias, ident, *take("ctxT", "ga_downT", "ga_upT", "ga_qT", "ga_outT", "ga_hmask", "ga_pmask"))
        gated_experts(nc, x, ident, *take("ge_scale", "ge_bias", "ge_gateT", "ge_wg", "ge_wu", "ge_wd", "ge_lower"))
        dirs = [dict({n[2:]: v for n, v in a.items() if n[:2] == d + "_"}, pick=a["pick"]) for d in "fb"]
        state_space(nc, x, ident, dirs)
        cross_attention(nc, x, ident, *take("ctxT", "ctx2T", "xa_mask", "xa_wq", "xa_wk", "xa_wv", "xa_wo"))
        threshold_experts(nc, x, ident, *take("te_gw", "te_gb", "te_ew", "te_eb"))
        store_x(nc, x, out_dram)


def kernel(**inp):
    import numpy as np
    import concourse.bacc as bacc
    from concourse.bass_utils import run_bass_kernel_spmd as run

    c = np.ascontiguousarray
    rows = lambda v: c(np.broadcast_to(v[None], (P,) + v.shape))
    cols = lambda v: c(v.reshape(-1, P).T)
    K = 64
    k = np.arange(P)
    pick = np.zeros((P, P), np.float32)
    pick[64 + np.arange(64), np.arange(64)] = 1.0
    ctxT = c(inp["ctx_1024"].reshape(B * K, D).T)
    tiles = lambda v: c(v.reshape(B, 2, P, K).transpose(2, 1, 0, 3))
    arr = {
        "x": c(inp["x"].transpose(1, 0, 2).reshape(TOK, D)),
        "ident": np.eye(P, dtype=np.float32), "pick": pick,
        "sa_mask": np.where((k[:, None] // B) % 2 == np.arange(32)[None] // B, 0.0, -1e30).astype(np.float32),
        "sa_wq": inp["L0_attn_Wq"], "sa_wkv": inp["L0_attn_Wkv"], "sa_bq": cols(inp["L0_attn_bq"]),
        "sa_bk": cols(inp["L0_attn_bkv"][:1024]), "sa_bv": cols(inp["L0_attn_bkv"][1024:]),
        "sa_wp": inp["L0_attn_Wp"], "sa_bp": inp["L0_attn_bp"].reshape(1, D),
        "idx": tiles(inp["itok_BxSx64_0_2047"]).reshape(P, NT * K), "bins": rows(np.arange(K, dtype=np.float32)),
        "ctxT": ctxT, "ctx2T": c(np.broadcast_to(ctxT.reshape(D, B, 1, K), (D, B, 2, K)).reshape(D, B, 2 * K)),
        "ga_downT": c(inp["L0_xattn_W_kv_down"].T), "ga_upT": c(inp["L0_xattn_W_kv_up"].T),
        "ga_qT": c(inp["L0_xattn_W_q"].T), "ga_outT": c(inp["L0_xattn_W_out"].T),
        "ga_hmask": (k[:, None] // 8 == np.arange(16)[None]).astype(np.float32),
        "ga_pmask": (k[:, None] // 64 == np.arange(2)[None]).astype(np.float32),
        "ge_scale": c(inp["L0_ffn_ln_scale"].reshape(D, 1)), "ge_bias": c(inp["L0_ffn_ln_bias"].reshape(D, 1)),
        "ge_gateT": c(inp["L0_ffn_gate_w"].T),
        "ge_wg": c(np.concatenate([inp["L0_ffn_sWg"][None], inp["L0_ffn_Wg"]]).transpose(1, 0, 2)),
        "ge_wu": c(np.concatenate([inp["L0_ffn_sWu"][None], inp["L0_ffn_Wu"]]).transpose(1, 0, 2)),
        "ge_wd": c(np.concatenate([inp["L0_ffn_sWd"][None], inp["L0_ffn_Wd"]]).reshape(9, 2, P, D).transpose(2, 0, 1, 3)),
        "ge_lower": rows(np.tril(np.ones((8, 8), np.float32), -1)),
        "f_strict": (k[:, None] > k[None]).astype(np.float32), "b_strict": (k[:, None] < k[None]).astype(np.float32),
        "f_inclusive": (k[:, None] <= k[None]).astype(np.float32), "b_inclusive": (k[:, None] >= k[None]).astype(np.float32),
        "xa_mask": tiles(inp["mask_Bx1xSxS2_fk1"]).reshape(P, NT, K),
        "xa_wq": inp["L1_xattn_W_q"], "xa_wk": inp["L1_xattn_W_k"], "xa_wv": inp["L1_xattn_W_v"], "xa_wo": inp["L1_xattn_W_o"],
        "te_gw": inp["L1_ffn_gate_w"], "te_gb": rows(inp["L1_ffn_gate_b"]),
        "te_ew": c(inp["L1_ffn_expert_w"].transpose(1, 0, 2).reshape(D, 8 * D)), "te_eb": inp["L1_ffn_expert_b"],
    }
    for d in "fb":
        g = lambda n: inp[f"L1_attn_{d}_{n}"]
        arr.update({
            f"{d}_in": c(g("in_w").T), f"{d}_conv_w": c(g("conv_w").reshape(3, P, 4).transpose(1, 0, 2)),
            f"{d}_conv_b": cols(g("conv_b")), f"{d}_dt_bias": rows(g("dt_bias")), f"{d}_a_log": rows(g("A_log")),
            f"{d}_dp": rows(g("Dp")), f"{d}_norm_w": cols(g("norm_w")),
            f"{d}_out_w": c(g("out_w").T.reshape(2, P, D).transpose(1, 0, 2)),
        })
    nc = bacc.Bacc("TRN2", target_bir_lowering=False, num_devices=1)
    a = {n: nc.dram_tensor(f"in_{n}", v.shape, mybir.dt.from_np(v.dtype), kind="ExternalInput").ap() for n, v in arr.items()}
    x1 = nc.dram_tensor("x1", (TOK, D), F32, kind="Internal").ap()
    out = nc.dram_tensor("out", (B, S, D), F32, kind="ExternalOutput").ap()
    decoder(nc, a, x1, out)
    return run(nc, [{f"in_{n}": v for n, v in arr.items()}], core_ids=[0]).results[0]["out"]
```

```python
from contextlib import ExitStack

import concourse.bass as bass
from concourse import mybir

F32 = mybir.dt.float32
F32R = mybir.dt.float32r
I32 = mybir.dt.int32
BF16 = mybir.dt.bfloat16
ALU = mybir.AluOpType
ACT = mybir.ActivationFunctionType
AX = mybir.AxisListType.X

P = 128
B, S, D = 16, 256, 128
TOK = B * S
NT = TOK // P
SUP = 4
NSUP = NT // SUP
EPS = 1e-5


class Scope:

    def __init__(self, nc, stack, prefix):
        self.nc, self.stack, self.prefix = nc, stack, prefix
        self.sems = []
        stack.callback(self.wipe)

    def sb(self, name, shape, dt=F32):
        return self.stack.enter_context(self.nc.sbuf_tensor(f"{self.prefix}_{name}", shape, dt))

    def ps(self, name, shape, dt=F32):
        return self.stack.enter_context(self.nc.psum_tensor(f"{self.prefix}_{name}", shape, dt))

    def sem(self, name):
        self.sems.append(self.nc.alloc_semaphore(f"{self.prefix}_{name}"))
        return self.sems[-1]

    def wipe(self):
        if self.sems:
            self.nc.clear_and_free_semaphores(self.sems)
            self.nc.all_engine_barrier()


def bcast(ap, n, where):
    return ap.unsqueeze(where).to_broadcast(list(ap.shape[:where]) + [n] + list(ap.shape[where:]))


def product(pe, out, lhsT, rhs):
    for n, (a, b) in enumerate(((0, 1), (1, 0), (0, 0))):
        mm = pe.matmul(out, lhsT(a), rhs(b), start=(n == 0), stop=(n == 2))
    return mm


class Norm:

    def __init__(self, m, stats=None):
        self.given = stats is not None
        self.stats = stats if self.given else m.sb("stats", [P, NT, 6])
        self.tmp = m.sb("tmp", [P, 8, NT])
        self.mean = m.sb("mean", [P, NT])
        self.rstd = m.sb("rstd", [P, NT])
        self.counted = m.sem("stats_counted")
        self.var_ready = m.sem("var_ready")
        self.std_ready = m.sem("std_ready")
        self.done = m.sem("norm_done")

    def dve(self, dve, x):
        st, tmp = self.stats, self.tmp
        if self.given:
            dve.sem_inc(self.counted, NT)
        else:
            with dve.Fori(0, NT // 8) as i:
                for g in range(8):
                    t = 8 * i + g
                    dve.bn_stats(st[:, t, :], x[:, t, :]).then_inc(self.counted, 1)
            dve.wait_ge(self.counted, NT)
        me, mo, ve, vo = st[:, :, 1], st[:, :, 4], st[:, :, 2], st[:, :, 5]
        dve.tensor_tensor(tmp[:, 0, :], me, mo, ALU.add).then_inc(self.counted, 1)
        dve.tensor_tensor(tmp[:, 1, :], me, mo, ALU.subtract).then_inc(self.counted, 1)
        dve.tensor_tensor(tmp[:, 2, :], ve, vo, ALU.add).then_inc(self.counted, 1)
        dve.wait_ge(self.counted, NT + 3)
        dve.tensor_scalar(self.mean[:, :], tmp[:, 0, :], 0.5, None, ALU.mult).then_inc(self.counted, 1)
        dve.tensor_scalar(tmp[:, 3, :], tmp[:, 1, :], 0.5, None, ALU.mult).then_inc(self.counted, 1)
        dve.tensor_scalar(tmp[:, 4, :], tmp[:, 2, :], 1.0 / D, EPS, ALU.mult, ALU.add).then_inc(self.counted, 1)
        dve.wait_ge(self.counted, NT + 6)
        dve.tensor_tensor(tmp[:, 5, :], tmp[:, 3, :], tmp[:, 3, :], ALU.mult).then_inc(self.counted, 1)
        dve.wait_ge(self.counted, NT + 7)
        dve.tensor_tensor(tmp[:, 6, :], tmp[:, 5, :], tmp[:, 4, :], ALU.add).then_inc(self.var_ready, 1)
        dve.wait_ge(self.std_ready, 1)
        dve.reciprocal(self.rstd[:, :], tmp[:, 7, :]).then_inc(self.done, 1)
        dve.wait_ge(self.done, 1)

    def act(self, act, then=None):
        act.preload_act_table(ACT.Sqrt)
        act.wait_ge(self.var_ready, 1)
        act.activation(self.tmp[:, 7, :], self.tmp[:, 6, :], ACT.Sqrt).then_inc(self.std_ready, 1)
        if then is not None:
            act.preload_act_table(then)

    def tile(self, eng, out, x, t):
        return eng.tensor_scalar(out, x[:, t, :], self.mean[:, bass.ds(t, 1)], self.rstd[:, bass.ds(t, 1)],
                                 ALU.subtract, ALU.mult)


def load_x(nc, x, ident, x_dram, ident_dram):
    with ExitStack() as stack:
        m = Scope(nc, stack, "lx")
        loaded = m.sem("loaded")
        with nc.Block() as block:

            @block.sync
            def _(sp):
                for u in range(2):
                    sp.dma_start(x[:, B * u : B * u + B, :],
                                 x_dram[P * B * u : P * B * (u + 1), :].rearrange("(p b) d -> p b d", b=B)).then_inc(loaded, 16)
                sp.dma_start(ident[:, :], ident_dram).then_inc(loaded, 16)
                sp.wait_ge(loaded, 48)


def store_x(nc, x, out_dram):
    with ExitStack() as stack:
        m = Scope(nc, stack, "st")
        stored = m.sem("stored")
        with nc.Block() as block:

            @block.sync
            def _(sp):
                for u in range(2):
                    sp.dma_start(out_dram.rearrange("b (u p) d -> u p b d", u=2)[u], x[:, B * u : B * u + B, :]).then_inc(stored, 16)
                sp.wait_ge(stored, 32)


def self_attention(nc, x, ident, x_dram, ident_dram, mask_dram, wq_dram, wkv_dram, bq_dram, bk_dram, bv_dram, wp_dram, bp_dram, out_dram,
                   idx_dram, bins_dram, bias):
    H, HD = 16, 64
    HP = H // 2
    SCALE = 1.0 / HD**0.5
    Q = 32
    NB = P // Q
    NQKV = 2 * HP + 2 * SUP
    NLOAD = 11
    K = 64
    BINS = K // NSUP
    STEPS = 5
    NEVER = -1e30
    with ExitStack() as stack:
        m = Scope(nc, stack, "sa")
        mask = m.sb("mask", [P, Q])
        wqs = m.sb("wq_halves", [P, 2, H * HD], F32R)
        wkvs = m.sb("wkv_halves", [P, 2, 2 * H * HD], F32R)
        bq = m.sb("bq", [P, HP])
        bk = m.sb("bk", [P, HP])
        bv = m.sb("bv", [P, HP])
        wp = m.sb("wp", [P, HP, D])
        bp = m.sb("bp", [1, D])
        one = m.sb("one", [1, P])
        crow = m.sb("crow", [1, D])
        raw = m.sb("raw", [P, NT * K], I32)
        bins = m.sb("bins", [P, K])
        val = m.sb("val", [P, 2, NT * K])
        wkv, wq = val[:, 0, :], val[:, 1, 0 : H * HD]
        idx = m.sb("idx", [P, NT * K], BF16)
        same = m.sb("same", [P, 2, NT, K], BF16)
        part = m.sb("part", [P, 2, NT, K], BF16)
        norm = Norm(m)
        xn = m.sb("xn", [P, SUP, D])
        xnT = m.sb("xnT", [P, 2, SUP * P], F32R)
        qT = m.sb("qT", [P, HP, SUP * P])
        kT = m.sb("kT", [P, HP, SUP * P])
        v = m.sb("v", [P, SUP, H * HD])
        logits = m.sb("logits", [P, 2, H, Q])
        shifted = m.sb("shifted", [P, 2, H, Q])
        probs = m.sb("probs", [P, 2, H, Q])
        normed = m.sb("normed", [P, 2, H, Q])
        rowmax = m.sb("rowmax", [P, 2, H])
        rowsum = m.sb("rowsum", [P, 2, H])
        rinv = m.sb("rinv", [P, 2, H])
        turned = m.sb("turned", [P, 2, H, Q])
        probsT = m.sb("probsT", [P, 2, H, P])
        oT = m.sb("oT", [P, 2, HP, P])

        ps_s = [[m.ps(f"ps_s{n}{o}", [P, HP, 2 * Q]) for o in range(2)] for n in range(2)]
        ps_q = [m.ps(f"ps_q{n}", [P, 512]) for n in range(4)]
        ps_o = [ps_q[2 + n][:, :].rearrange("p (c q) -> p c q", q=P) for n in range(2)]

        x_loaded = m.sem("x_loaded")
        w_loaded = m.sem("w_loaded")
        ones_ready = m.sem("ones_ready")
        zeroed = m.sem("probsT_zeroed")
        const_mm = m.sem("const_mm")
        const_ready = m.sem("const_ready")
        xn_ready = m.sem("xn_ready")
        xn_transposed = m.sem("xn_transposed")
        xnT_ready = m.sem("xnT_ready")
        qkv_mm = m.sem("qkv_mm")
        qkv_ready = m.sem("qkv_ready")
        scores_begun = m.sem("scores_begun")
        scored = m.sem("scored")
        logits_ready = m.sem("logits_ready")
        max_ready = m.sem("max_ready")
        shifted_ready = m.sem("shifted_ready")
        exp_ready = m.sem("exp_ready")
        sum_ready = m.sem("sum_ready")
        rinv_ready = m.sem("rinv_ready")
        normed_ready = m.sem("probs_normed")
        turned_ready = m.sem("turned_ready")
        probsT_ready = m.sem("probsT_ready")
        attended = m.sem("attended")
        oT_ready = m.sem("oT_ready")
        projected = m.sem("projected")
        x_out = m.sem("x_out")
        stored = m.sem("stored")
        high_ready, low_ready, xnT_low = m.sem("high_ready"), m.sem("low_ready"), m.sem("xnT_low")
        prep = m.sem("index_prep")
        summed = m.sem("summed")
        logged = m.sem("logged")

        with nc.Block() as block:

            @block.sync
            def _(sp):
                rows = x_dram.rearrange("(t p) d -> p t d", p=P)
                sp.dma_start(x[:, :, :], rows).then_inc(x_loaded, 16)
                for dst, src in ((ident[:, :], ident_dram), (mask[:, :], mask_dram), (wq, wq_dram),
                                 (wkv, wkv_dram), (bq[:, :], bq_dram), (bk[:, :], bk_dram),
                                 (bv[:, :], bv_dram), (wp[:, :, :], wp_dram.rearrange("(c p) n -> p c n", p=P)),
                                 (bp[:, :], bp_dram), (raw[:, :], idx_dram), (bins[:, :], bins_dram)):
                    sp.dma_start(dst, src).then_inc(w_loaded, 16)
                out_rows = out_dram.rearrange("(t p) d -> p t d", p=P)
                with sp.Fori(0, NSUP) as i:
                    sp.wait_ge(x_out, SUP * i + SUP + 2)
                    sp.dma_start(out_rows[:, bass.ds(SUP * i, SUP), :], x[:, bass.ds(SUP * i, SUP), :]).then_inc(stored, 16)
                sp.wait_ge(stored, 16 * NSUP)

            @block.gpsimd
            def _(pool):
                pool.memset(one[:, :], 1.0).then_inc(ones_ready, 1)
                pool.memset(probsT[:, :, :, :], 0.0).then_inc(zeroed, 1)
                pool.wait_ge(high_ready, 2)
                pool.tensor_tensor(wqs[:, 1, :], wq, wqs[:, 0, :], ALU.subtract).then_inc(low_ready, 1)
                pool.tensor_tensor(wkvs[:, 1, :], wkv, wkvs[:, 0, :], ALU.subtract).then_inc(low_ready, 1)

            @block.tensor
            def _(pe):
                pe.wait_ge(w_loaded, 16 * NLOAD)
                pe.wait_ge(ones_ready, 1)
                for c in range(HP):
                    pe.matmul(ps_q[0][0:1, 0:D], bv[:, c : c + 1], wp[:, c, :], start=(c == 0), stop=False)
                pe.matmul(ps_q[0][0:1, 0:D], one[:, 0:1], bp[:, :], start=False, stop=True).then_inc(const_mm, 1)
                pe.sem_inc(qkv_ready, 4)
                pe.sem_inc(xn_transposed, 1)
                pe.sem_inc(logits_ready, 4)
                pe.wait_ge(const_ready, 1)

                def scores(i, g):
                    pe.wait_ge(logits_ready, 2 * (SUP * i + g) + 2)
                    pe.sem_inc(scores_begun, 1)
                    for h in range(H):
                        r, c = HD * (h % 2), h // 2
                        for j in range(NB):
                            cols = slice(P * g + Q * j, P * g + Q * j + Q)
                            mm = pe.matmul(ps_s[g % 2][h % 2][Q * j : Q * j + Q, c, 0:Q], qT[r : r + HD, c, cols],
                                           kT[r : r + HD, c, cols], start=True, stop=True, skip_group_check=True)
                    mm.then_inc(scored, 1)

                def attend(i, g):
                    pe.wait_ge(probsT_ready, SUP * i + g + 1)
                    pe.wait_ge(oT_ready, 2 * (SUP * i + g) + 1)
                    for h in range(H):
                        r, c = HD * (h % 2), h // 2
                        mm = pe.matmul(ps_o[c // (HP // 2)][r : r + HD, c % (HP // 2), :], v[:, g, h * HD : (h + 1) * HD],
                                       probsT[:, g % 2, HP * (h % 2) + c, :], start=True, stop=True, skip_group_check=True)
                        if h % (H // 2) == H // 2 - 1:
                            mm.then_inc(attended, 1)

                def project(i, g):
                    if g >= 2:
                        pe.wait_ge(x_out, SUP * i + g + 1)
                    y = ps_q[g % 2][:, 0:D]
                    pe.matmul(y, one[:, :], crow[:, :], start=True, stop=False)
                    for c in range(HP):
                        if c % (HP // 2) == 0:
                            pe.wait_ge(oT_ready, 2 * (SUP * i + g) + 2 + c // (HP // 2))
                        mm = pe.matmul(y, oT[:, g % 2, c, :], wp[:, c, :], start=False, stop=(c == HP - 1))
                    mm.then_inc(projected, 1)

                def turn_x(i):
                    pe.wait_ge(xn_ready, SUP * i + SUP)
                    for g in range(SUP):
                        mm = pe.transpose(ps_s[0][0][:, :, :].rearrange("p c k -> p (c k)")[:, P * g : P * g + P], xn[:, g, :], ident[:, :])
                    mm.then_inc(xn_transposed, 1)

                def fill(i, n):
                    pe.wait_ge(qkv_ready, NQKV * i + n + 1)
                    bank = ps_q[n % 4][:, :]
                    if n < 2 * HP:
                        w, c = (wqs, n) if n < HP else (wkvs, n - HP)
                        mm = product(pe, bank, lambda half: w[:, half, P * c : P * c + P], lambda half: xnT[:, half, :])
                    else:
                        g, at = (n - 2 * HP) // 2, H * HD + 512 * (n % 2)
                        mm = product(pe, bank, lambda half: xnT[:, half, P * g : P * g + P],
                                     lambda half: wkvs[:, half, at : at + 512])
                    mm.then_inc(qkv_mm, 1)

                def super_tile(i, last):
                    pe.wait_ge(xnT_low, i + 1)
                    pe.wait_ge(oT_ready, 2 * SUP * i + 1)
                    for n in range(2 * HP):
                        if n < 2:
                            pe.wait_ge(x_out, SUP * i + n + 1)
                        fill(i, n)
                    for g in range(SUP):
                        fill(i, 2 * HP + 2 * g)
                        fill(i, 2 * HP + 2 * g + 1)
                        if g == 0:
                            pe.wait_ge(qkv_ready, NQKV * i + 2 * HP + 4)
                        scores(i, g)
                    pe.wait_ge(qkv_ready, NQKV * i + NQKV + 4)
                    attend(i, 0)
                    project(i, 0)
                    attend(i, 1)
                    if not last:
                        pe.wait_ge(logits_ready, 2 * (SUP * i + SUP) + 4)
                        turn_x(i + 1)
                    project(i, 1)
                    attend(i, 2)
                    project(i, 2)
                    attend(i, 3)
                    project(i, 3)

                turn_x(0)
                pe.wait_ge(low_ready, 2)
                with pe.Fori(0, NSUP - 1) as i:
                    super_tile(i, False)
                super_tile(NSUP - 1, True)

            @block.scalar
            def _(act):
                act.wait_ge(w_loaded, 16 * NLOAD)
                act.activation(wqs[:, 0, :], wq, ACT.Copy).then_inc(high_ready, 1)
                act.activation(wkvs[:, 0, :], wkv, ACT.Copy).then_inc(high_ready, 1)
                act.wait_ge(const_mm, 1)
                act.activation(crow[:, :], ps_q[0][0:1, 0:D], ACT.Copy).then_inc(const_ready, 1)
                norm.act(act, ACT.Exp)
                act.sem_inc(oT_ready, 1)

                def exp(i, g):
                    act.wait_ge(shifted_ready, SUP * i + g + 1)
                    act.activation(probs[:, g % 2, :, :], shifted[:, g % 2, :, :], ACT.Exp).then_inc(exp_ready, 1)

                def out(i, g):
                    for half in range(2):
                        act.wait_ge(attended, 2 * (SUP * i + g) + half + 1)
                        act.activation(oT[:, g % 2, half * (HP // 2) : (half + 1) * (HP // 2), :], ps_o[half],
                                       ACT.Copy).then_inc(oT_ready, 1)

                def copy_x(i):
                    act.wait_ge(xn_transposed, i + 2)
                    act.activation(xnT[:, 0, :], ps_s[0][0][:, :, :].rearrange("p c k -> p (c k)"), ACT.Copy).then_inc(xnT_ready, 1)

                def copy_fill(i, n):
                    act.wait_ge(qkv_mm, NQKV * i + n + 1)
                    bank = ps_q[n % 4][:, :]
                    if n < 2 * HP:
                        dst, b, c = (qT, bq, n) if n < HP else (kT, bk, n - HP)
                        op = act.activation(dst[:, c, :], bank, ACT.Identity, bias=b[:, c : c + 1])
                    else:
                        g, half = (n - 2 * HP) // 2, n % 2
                        op = act.activation(v[:, g, 512 * half : 512 * half + 512], bank, ACT.Copy)
                    op.then_inc(qkv_ready, 1)

                def spread(i, g):
                    act.wait_ge(turned_ready, SUP * i + g + 1)
                    if g >= 2:
                        act.wait_ge(attended, 2 * (SUP * i + g - 1))
                    for j in range(NB):
                        rows = slice(Q * j, Q * j + Q)
                        op = act.activation(probsT[rows, g % 2, :, rows], turned[rows, g % 2, :, :], ACT.Copy)
                    op.then_inc(probsT_ready, 1)

                def super_tile(i, last):
                    for n in range(2 * HP + 4):
                        copy_fill(i, n)
                    exp(i, 0)
                    copy_fill(i, 2 * HP + 4)
                    copy_fill(i, 2 * HP + 5)
                    exp(i, 1)
                    copy_fill(i, 2 * HP + 6)
                    copy_fill(i, 2 * HP + 7)
                    spread(i, 0)
                    exp(i, 2)
                    spread(i, 1)
                    exp(i, 3)
                    out(i, 0)
                    spread(i, 2)
                    out(i, 1)
                    if not last:
                        copy_x(i + 1)
                    spread(i, 3)
                    out(i, 2)
                    out(i, 3)

                copy_x(0)
                with act.Fori(0, NSUP - 1) as i:
                    super_tile(i, False)
                super_tile(NSUP - 1, True)
                act.wait_ge(prep, 5)
                act.activation(val[:, 1, :], val[:, 0, :], ACT.Ln).then_inc(logged, 1)

            @block.vector
            def _(dve):
                dve.wait_ge(x_loaded, 16)
                norm.dve(dve, x)
                dve.wait_ge(xn_transposed, 1)
                for g in range(SUP):
                    norm.tile(dve, xn[:, g, :], x, g).then_inc(xn_ready, 1)
                dve.wait_ge(w_loaded, 16 * NLOAD)
                dve.wait_ge(zeroed, 1)
                dve.sem_inc(x_out, 2)

                def shift(i, g):
                    n = SUP * i + g + 1
                    u = g % 2
                    dve.wait_ge(scored, n)
                    for o in range(2):
                        dve.scalar_tensor_tensor(logits[:, u, HP * o : HP * o + HP, :], ps_s[u][o][:, :, 0:Q], SCALE,
                                                 bcast(mask[:, :], HP, 1), ALU.mult, ALU.add).then_inc(logits_ready, 1)
                    dve.wait_ge(logits_ready, 2 * n + 4)
                    dve.tensor_reduce(rowmax[:, u, :], logits[:, u, :, :], AX, ALU.max).then_inc(max_ready, 1)
                    dve.wait_ge(max_ready, n)
                    dve.tensor_tensor(shifted[:, u, :, :], logits[:, u, :, :], bcast(rowmax[:, u, :], Q, 2),
                                      ALU.subtract).then_inc(shifted_ready, 1)

                def normalise(i, g):
                    n = SUP * i + g + 1
                    u = g % 2
                    dve.wait_ge(exp_ready, n)
                    dve.tensor_reduce(rowsum[:, u, :], probs[:, u, :, :], AX, ALU.add).then_inc(sum_ready, 1)
                    dve.wait_ge(sum_ready, n)
                    dve.reciprocal(rinv[:, u, :], rowsum[:, u, :]).then_inc(rinv_ready, 1)
                    dve.wait_ge(rinv_ready, n)
                    dve.tensor_tensor(normed[:, u, :, :], probs[:, u, :, :], bcast(rinv[:, u, :], Q, 2),
                                      ALU.mult).then_inc(normed_ready, 1)
                    dve.wait_ge(normed_ready, n)
                    if g >= 2:
                        dve.wait_ge(probsT_ready, SUP * i + g - 1)
                    dve.transpose(turned[:, u, :, :], normed[:, u, :, :]).then_inc(turned_ready, 1)

                def low_x(i):
                    dve.wait_ge(xnT_ready, i + 1)
                    dve.tensor_tensor(xnT[:, 1, :], ps_s[0][0][:, :, :].rearrange("p c k -> p (c k)"), xnT[:, 0, :],
                                      ALU.subtract).then_inc(xnT_low, 1)

                def add(i, g):
                    dve.wait_ge(projected, SUP * i + g + 1)
                    dve.tensor_tensor(x[:, SUP * i + g, :], x[:, SUP * i + g, :], ps_q[g % 2][:, 0:D], ALU.add).then_inc(x_out, 1)

                def norm_x(i):
                    dve.wait_ge(xn_transposed, i + 1)
                    for g in range(SUP):
                        norm.tile(dve, xn[:, g, :], x, SUP * i + g).then_inc(xn_ready, 1)

                def count(i, first, n):
                    for j in range(first, first + n, 2):
                        at = BINS * i + j
                        base = STEPS * at
                        for u in range(2):
                            dve.wait_ge(summed, base + 1)
                            dve.tensor_scalar(same[:, u, :, :].rearrange("p t k -> p (t k)"), idx[:, :],
                                              bins[:, bass.ds(at + u, 1)], None, ALU.is_equal).then_inc(summed, 1)
                        n_slots, off = K // 2, 0
                        src = [same[:, u, :, :] for u in range(2)]
                        for level in range(3):
                            for u in range(2):
                                dve.wait_ge(summed, base + 2 * level + u + 2)
                                dst = part[:, u, :, off : off + n_slots]
                                dve.tensor_tensor(dst, src[u][:, :, 0:n_slots], src[u][:, :, n_slots : 2 * n_slots],
                                                  ALU.add).then_inc(summed, 1)
                                src[u] = dst
                            off, n_slots = off + n_slots, n_slots // 2
                        for u in range(2):
                            dve.wait_ge(summed, base + 8 + u)
                            dve.tensor_reduce(bias[:, :, bass.ds(at + u, 1)], src[u], AX, ALU.add).then_inc(summed, 1)

                low_x(0)
                dve.wait_ge(low_ready, 2)
                dve.tensor_copy(val[:, 0, :], raw[:, :]).then_inc(prep, 1)
                dve.wait_ge(prep, 1)
                dve.tensor_scalar(val[:, 1, :], val[:, 0, :], 0.0, float(K), ALU.is_lt, ALU.mult).then_inc(prep, 1)
                dve.wait_ge(prep, 2)
                dve.tensor_tensor(val[:, 0, :], val[:, 0, :], val[:, 1, :], ALU.add).then_inc(prep, 1)
                dve.wait_ge(prep, 3)
                dve.tensor_scalar(idx[:, :], val[:, 0, :], 0.0, float(K - 1), ALU.max, ALU.min).then_inc(prep, 1)
                dve.wait_ge(prep, 4)
                dve.sem_inc(summed, 1)

                def super_tile(i, last):
                    if not last:
                        norm_x(i + 1)
                    count(i, 0, 4)
                    shift(i, 0)
                    shift(i, 1)
                    normalise(i, 0)
                    shift(i, 2)
                    normalise(i, 1)
                    shift(i, 3)
                    normalise(i, 2)
                    count(i, 4, 2)
                    add(i, 0)
                    normalise(i, 3)
                    add(i, 1)
                    if not last:
                        low_x(i + 1)
                    count(i, 6, 2)
                    add(i, 2)
                    add(i, 3)

                with dve.Fori(0, NSUP - 1) as i:
                    super_tile(i, False)
                super_tile(NSUP - 1, True)
                bflat = bias[:, :, :].rearrange("p t k -> p (t k)")
                dve.wait_ge(summed, STEPS * K + 1)
                dve.tensor_scalar(val[:, 0, :], bflat, 1.0, None, ALU.max).then_inc(prep, 1)
                dve.tensor_scalar(bflat, bflat, 0.0, NEVER, ALU.is_equal, ALU.mult).then_inc(prep, 1)
                dve.wait_ge(logged, 1)
                dve.wait_ge(prep, 6)
                dve.tensor_tensor(bflat, bflat, val[:, 1, :], ALU.add).then_inc(prep, 1)
                dve.wait_ge(prep, 7)
def gathered_attention(nc, x, bias, ident, ctxT_dram, downT_dram, upT_dram, qT_dram, outT_dram, hmask_dram, pmask_dram):
    H, HD, K = 16, 8, 64
    HP, VW = H // 2, 2 * (HD + 1)
    SCALE = 1.0 / HD**0.5
    HK = H * K
    with ExitStack() as stack:
        m = Scope(nc, stack, "ga")
        ctxT = m.sb("ctxT", [D, B * K])
        downT = m.sb("downT", [D, D])
        upT = m.sb("upT", [D, 2 * D])
        qW = m.sb("qW", [D, D])
        oW = m.sb("oW", [D, D])
        hmask = m.sb("hmask", [P, H])
        pmask = m.sb("pmask", [P, 2])
        cT = m.sb("cT", [P, B, 2, K])
        kT = m.sb("kT", [P, B, K])
        keys = m.sb("keys", [P, B, H, K])
        vals = m.sb("vals", [P, B, HP, VW])
        norm = Norm(m)
        xn = m.sb("xn", [P, 2, D])
        xnT = m.sb("xnT", [P, 2 * P])
        qT = m.sb("qT", [P, 2 * P])
        logits = m.sb("logits", [P, 2, H, K])
        rowmax = m.sb("rowmax", [P, 2, H])
        shifted = m.sb("shifted", [P, 2, H, K])
        probs = m.sb("probs", [P, 2, HK])
        probsT = m.sb("probsT", [P, 2, HP, P])
        rinv = m.sb("rinv", [P, 2, HP, 2])
        o = m.sb("o", [P, 2, D])
        oT = m.sb("oT", [P, 2, P])
        ps_s = [m.ps(f"ps_s{u}", [P, H, K]) for u in range(2)]
        ps_p = m.ps("ps_p", [P, HP, P])
        ps_m = m.ps("ps_m", [P, 512])
        ps_o = m.ps("ps_o", [P, 512])

        loaded = m.sem("loaded")
        ctx_mm, ctx_ready = m.sem("ctx_mm"), m.sem("ctx_ready")
        key_mm, key_ready = m.sem("key_mm"), m.sem("key_ready")
        val_mm, val_ready = m.sem("val_mm"), m.sem("val_ready")
        keys_ready = m.sem("keys_ready")
        ones_ready = m.sem("ones_ready")
        xn_ready, xn_transposed, xnT_ready = m.sem("xn_ready"), m.sem("xn_transposed"), m.sem("xnT_ready")
        q_mm, qT_ready = m.sem("q_mm"), m.sem("qT_ready")
        scored, logits_ready, max_ready = m.sem("scored"), m.sem("logits_ready"), m.sem("max_ready")
        shifted_ready, exp_ready = m.sem("shifted_ready"), m.sem("exp_ready")
        probs_transposed, probsT_ready = m.sem("probs_transposed"), m.sem("probsT_ready")
        attended, rinv_ready, o_ready = m.sem("attended"), m.sem("rinv_ready"), m.sem("o_ready")
        o_transposed, oT_ready = m.sem("o_transposed"), m.sem("oT_ready")
        projected, x_out = m.sem("projected"), m.sem("x_out")
        NLOAD = 7

        with nc.Block() as block:

            @block.sync
            def _(sp):
                for dst, src in ((ctxT, ctxT_dram), (downT, downT_dram), (upT, upT_dram), (qW, qT_dram),
                                 (oW, outT_dram), (hmask, hmask_dram), (pmask, pmask_dram)):
                    sp.dma_start(dst[:, :], src).then_inc(loaded, 16)

            @block.gpsimd
            def _(pool):
                pool.wait_ge(loaded, 16 * NLOAD)
                for h2 in range(2):
                    col = vals[:, :, :, h2 * (HD + 1) + HD].rearrange("p b c -> p (b c)")
                    pool.tensor_copy(col, bcast(pmask[:, h2], B * HP, 1)).then_inc(ones_ready, 1)
                pool.wait_ge(key_ready, 2)
                with pool.Fori(0, B) as b:
                    pool.tensor_tensor(keys[:, b, :, :], bcast(kT[:, b, :], H, 1), bcast(hmask[:, :], K, 2),
                                       ALU.mult).then_inc(keys_ready, 1)

            @block.tensor
            def _(pe):
                pe.wait_ge(loaded, 16 * NLOAD)
                for n in range(2):
                    pe.matmul(ps_s[0][:, 8 * n : 8 * n + 8, :], downT[:, :], ctxT[:, 512 * n : 512 * n + 512],
                              start=True, stop=True).then_inc(ctx_mm, 1)
                pe.wait_ge(ctx_ready, 4)
                for n in range(2):
                    pe.matmul(ps_s[1][:, 8 * n : 8 * n + 8, :], upT[:, 0:D], cT[:, 8 * n : 8 * n + 8, 0, :],
                              start=True, stop=True).then_inc(key_mm, 1)
                banks = [ps_p[:, 0:4, :], ps_p[:, 4:8, :]]
                for b in range(B):
                    if b in (8, 12):
                        pe.wait_ge(val_ready, (b - 4) // 4)
                    mm = pe.matmul(banks[(b // 4) % 2][:, b % 4, :], cT[:, b, :, :].rearrange("p e k -> p (e k)"), upT[:, D : 2 * D],
                                   start=True, stop=True)
                    if b % 4 == 3:
                        mm.then_inc(val_mm, 1)
                pe.wait_ge(val_ready, B // 4)
                pe.wait_ge(ones_ready, 2)
                pe.wait_ge(key_ready, 2)

                def turn_x(b):
                    pe.wait_ge(xn_ready, 2 * b + 2)
                    for u in range(2):
                        mm = pe.transpose(ps_m[:, P * u : P * u + P], xn[:, u, :], ident[:, :])
                    mm.then_inc(xn_transposed, 1)

                def queries(b):
                    pe.wait_ge(xnT_ready, b + 1)
                    pe.matmul(ps_m[:, 256:512], qW[:, :], xnT[:, :], start=True, stop=True).then_inc(q_mm, 1)

                def scores(b, u, first=False):
                    if not first:
                        pe.wait_ge(logits_ready, 2 * b + u - 1)
                    if u == 0:
                        pe.wait_ge(qT_ready, b + 1)
                        pe.wait_ge(keys_ready, b + 1)
                    for n in range(2):
                        mm = pe.matmul(ps_s[u][:, 8 * n : 8 * n + 8, :], qT[:, P * u : P * u + P],
                                       keys[:, b, 8 * n : 8 * n + 8, :], start=True, stop=True)
                    mm.then_inc(scored, 1)

                def turn_probs(b, u):
                    pe.wait_ge(exp_ready, 2 * b + u + 1)
                    for c in range(HP):
                        mm = pe.transpose(ps_p[:, c, :], probs[:, u, P * c : P * c + P], ident[:, :])
                        if c % 4 == 3:
                            mm.then_inc(probs_transposed, 1)

                def attend(b, u, first=False):
                    if not first:
                        pe.wait_ge(o_ready, 2 * b + u)
                    pe.wait_ge(probsT_ready, 2 * (2 * b + u) + 2)
                    for c in range(HP):
                        mm = pe.matmul(ps_o[:, VW * c : VW * c + VW], probsT[:, u, c, :], vals[:, b, c, :],
                                       start=True, stop=True)
                    mm.then_inc(attended, 1)

                def turn_o(b):
                    pe.wait_ge(o_ready, 2 * b + 2)
                    for u in range(2):
                        mm = pe.transpose(ps_m[:, P * u : P * u + P], o[:, u, :], ident[:, :])
                    mm.then_inc(o_transposed, 1)

                def project(b):
                    pe.wait_ge(oT_ready, b + 1)
                    for u in range(2):
                        mm = pe.matmul(ps_m[:, 256 + P * u : 256 + P * u + P], oT[:, u, :], oW[:, :], start=True, stop=True)
                    mm.then_inc(projected, 1)

                def batch(b, first, last):
                    if not first:
                        turn_probs(b - 1, 1)
                        pe.wait_ge(x_out, b)
                    if not last:
                        turn_x(b + 1)
                    scores(b, 1, first)
                    if not last:
                        queries(b + 1)
                    if not first:
                        attend(b - 1, 1)
                    turn_probs(b, 0)
                    if not last:
                        scores(b + 1, 0)
                    if not first:
                        turn_o(b - 1)
                    attend(b, 0, first)
                    if not first:
                        project(b - 1)

                turn_x(0)
                queries(0)
                scores(0, 0, True)
                batch(0, True, False)
                with pe.Fori(1, B - 1) as b:
                    batch(b, False, False)
                batch(B - 1, False, True)
                turn_probs(B - 1, 1)
                attend(B - 1, 1)
                pe.wait_ge(x_out, B)
                turn_o(B - 1)
                project(B - 1)

            @block.scalar
            def _(act):
                for n in range(2):
                    act.wait_ge(ctx_mm, n + 1)
                    for e in range(2):
                        act.activation(cT[:, 8 * n : 8 * n + 8, e, :], ps_s[0][:, 8 * n : 8 * n + 8, :], ACT.Copy).then_inc(ctx_ready, 1)
                for n in range(2):
                    act.wait_ge(key_mm, n + 1)
                    act.activation(kT[:, 8 * n : 8 * n + 8, :], ps_s[1][:, 8 * n : 8 * n + 8, :], ACT.Copy).then_inc(key_ready, 1)
                norm.act(act, ACT.Exp)

                def copy_x(b):
                    act.wait_ge(xn_transposed, b + 1)
                    act.activation(xnT[:, :], ps_m[:, 0:256], ACT.Copy).then_inc(xnT_ready, 1)

                def copy_q(b):
                    act.wait_ge(q_mm, b + 1)
                    act.activation(qT[:, :], ps_m[:, 256:512], ACT.Copy, scale=SCALE).then_inc(qT_ready, 1)

                def exp(b, u):
                    act.wait_ge(shifted_ready, 2 * b + u + 1)
                    act.activation(probs[:, u, :], shifted[:, u, :, :].rearrange("p h k -> p (h k)"), ACT.Exp).then_inc(exp_ready, 1)

                def copy_probs(b, u):
                    for n in range(2):
                        act.wait_ge(probs_transposed, 2 * (2 * b + u) + n + 1)
                        act.activation(probsT[:, u, 4 * n : 4 * n + 4, :], ps_p[:, 4 * n : 4 * n + 4, :], ACT.Copy).then_inc(probsT_ready, 1)

                def copy_o(b):
                    act.wait_ge(o_transposed, b + 1)
                    act.activation(oT[:, :, :], ps_m[:, 0:256].rearrange("p (u q) -> p u q", u=2), ACT.Copy).then_inc(oT_ready, 1)

                def batch(b, first, last):
                    if not first:
                        exp(b - 1, 1)
                        copy_probs(b - 1, 1)
                    if not last:
                        copy_x(b + 1)
                        copy_q(b + 1)
                    exp(b, 0)
                    copy_probs(b, 0)
                    if not first:
                        copy_o(b - 1)

                copy_x(0)
                copy_q(0)
                batch(0, True, False)
                with act.Fori(1, B - 1) as b:
                    batch(b, False, False)
                batch(B - 1, False, True)
                exp(B - 1, 1)
                copy_probs(B - 1, 1)
                copy_o(B - 1)

            @block.vector
            def _(dve):
                norm.dve(dve, x)
                dve.wait_ge(loaded, 16 * NLOAD)
                banks = [ps_p[:, 0:4, :], ps_p[:, 4:8, :]]
                for n in range(B // 4):
                    dve.wait_ge(val_mm, n + 1)
                    dst = vals[:, 4 * n : 4 * n + 4, :, :].rearrange("p b c (e w) -> p (b c) e w", e=2)[:, :, :, 0:HD]
                    src = banks[n % 2].rearrange("p b (c e d) -> p (b c) e d", e=2, d=HD)
                    dve.tensor_tensor(dst, src, bcast(bcast(pmask[:, :], HD, 2), 4 * HP, 1), ALU.mult).then_inc(val_ready, 1)

                def norm_x(b):
                    for u in range(2):
                        norm.tile(dve, xn[:, u, :], x, B * u + b).then_inc(xn_ready, 1)

                def bias_scores(b, u, first):
                    dve.wait_ge(scored, 2 * b + u + 1)
                    if not first:
                        dve.wait_ge(shifted_ready, 2 * b + u - 1)
                    dve.tensor_tensor(logits[:, u, :, :], ps_s[u][:, :, :], bcast(bias[:, B * u + b, :], H, 1),
                                      ALU.add).then_inc(logits_ready, 1)

                def shift(b, u):
                    n = 2 * b + u + 1
                    dve.wait_ge(logits_ready, n)
                    dve.tensor_reduce(rowmax[:, u, :], logits[:, u, :, :], AX, ALU.max).then_inc(max_ready, 1)
                    dve.wait_ge(max_ready, n)
                    dve.tensor_tensor(shifted[:, u, :, :], logits[:, u, :, :], bcast(rowmax[:, u, :], K, 2),
                                      ALU.subtract).then_inc(shifted_ready, 1)

                def divide(b, u):
                    n = 2 * b + u + 1
                    dve.wait_ge(attended, n)
                    out = ps_o[:, 0 : HP * VW].rearrange("p (c e w) -> p c e w", c=HP, e=2)
                    dve.reciprocal(rinv[:, u, :, :], out[:, :, :, HD]).then_inc(rinv_ready, 1)
                    dve.wait_ge(rinv_ready, n)
                    dve.tensor_tensor(o[:, u, :].rearrange("p (c e d) -> p c e d", c=HP, e=2), out[:, :, :, 0:HD],
                                      bcast(rinv[:, u, :, :], HD, 3), ALU.mult).then_inc(o_ready, 1)

                def add(b):
                    dve.wait_ge(projected, b + 1)
                    view = x[:, :, :].rearrange("p (u b) d -> p u b d", u=2)[:, :, b, :]
                    dve.tensor_tensor(view, view, ps_m[:, 256:512].rearrange("p (u d) -> p u d", u=2), ALU.add).then_inc(x_out, 1)

                def batch(b, nth, norms):
                    for u in range(2):
                        bias_scores(b, u, nth == 0)
                        if nth > 0:
                            divide(b - 1, u)
                        if nth > 1 and u == 0:
                            add(b - 2)
                        shift(b, u)
                    if norms:
                        dve.wait_ge(xn_transposed, b + 2)
                        norm_x(b + 2)

                dve.sem_inc(x_out, 1)
                norm_x(0)
                dve.wait_ge(xn_transposed, 1)
                norm_x(1)
                batch(0, 0, True)
                batch(1, 1, True)
                with dve.Fori(2, B - 2) as b:
                    batch(b, 2, True)
                batch(B - 2, 2, False)
                batch(B - 1, 2, False)
                divide(B - 1, 0)
                add(B - 2)
                divide(B - 1, 1)
                add(B - 1)
                dve.wait_ge(x_out, B + 1)


def gated_experts(nc, x, ident, scale_dram, bias_dram, gateT_dram, wg_dram, wu_dram, wd_dram, order_dram, stats=None):
    E, F, TOP = 8, 256, 2
    C = F // P
    NE = E + 1
    with ExitStack() as stack:
        m = Scope(nc, stack, "ge")
        lns = m.sb("ln_scale", [D, 1])
        lnb = m.sb("ln_bias", [D, 1])
        lnbB = m.sb("ln_bias_rows", [D, P])
        gateT = m.sb("gateT", [D, E])
        gateS = m.sb("gateS", [D, E])
        order = m.sb("order", [P, E])
        wg = m.sb("wg", [D, NE, F])
        wu = m.sb("wu", [D, NE, F])
        wd = m.sb("wd", [P, NE, C, D])
        wgs = m.sb("wg_halves", [D, 2, NE, F], F32R)
        wus = m.sb("wu_halves", [D, 2, NE, F], F32R)
        norm = Norm(m)
        xn = m.sb("xn", [P, 2, SUP, D])
        xnT = m.sb("xnT", [D, 2, SUP * P])
        xT = m.sb("xT", [D, 2, TOK], F32R)
        gbias = m.sb("gbias", [P, E])
        raw = m.sb("raw_logits", [P, NT, E])
        gt = m.sb("gate", [P, 16, NT, E])
        gs = m.sb("gate_stats", [P, 12, NT])
        weight = m.sb("weight", [P, NT, E])
        sg = m.sb("silu_g", [P, 2, SUP * P])
        hT = m.sb("hT", [P, 6, SUP * P])
        ps_u = [[m.ps(f"ps_{k}{n}", [P, SUP * P]) for k in "gu"] for n in range(2)]
        ps_y = [m.ps(f"ps_y{n}", [P, SUP, D]) for n in range(3)]
        ps_m = m.ps("ps_m", [P, 512])

        ps_l = [ps_m, ps_y[0][:, :, :].rearrange("p g d -> p (g d)")]
        loaded = m.sem("loaded")
        gate_prep = m.sem("gate_prep")
        gbias_mm = m.sem("gbias_mm")
        gbias_ready = m.sem("gbias_ready")
        xn_ready, xn_transposed, xnT_ready = m.sem("xn_ready"), m.sem("xn_transposed"), m.sem("xnT_ready")
        xT_ready, logits_mm, raw_ready = m.sem("xT_ready"), m.sem("logits_mm"), m.sem("raw_ready")
        gated = m.sem("gated")
        gate_sqrt, gate_exp = m.sem("gate_sqrt"), m.sem("gate_exp")
        high_ready, low_ready, xTh_ready = m.sem("high_ready"), m.sem("low_ready"), m.sem("xTh_ready")
        up_mm, silu_ready, h_ready = m.sem("up_mm"), m.sem("silu_ready"), m.sem("h_ready")
        down_mm, added, counted = m.sem("down_mm"), m.sem("added"), m.sem("counted")
        NLOAD = 7

        with nc.Block() as block:

            @block.sync
            def _(sp):
                for dst, src in ((lns[:, :], scale_dram), (lnb[:, :], bias_dram), (gateT[:, :], gateT_dram),
                                 (order[:, :], order_dram), (wg[:, :, :], wg_dram), (wu[:, :, :], wu_dram),
                                 (wd[:, :, :, :], wd_dram)):
                    sp.dma_start(dst, src).then_inc(loaded, 16)

            @block.gpsimd
            def _(pool):
                for w, halves in ((wg, wgs), (wu, wus)):
                    pool.wait_ge(high_ready, 1 if w is wg else 2)
                    pool.tensor_tensor(halves[:, 1, :, :], w[:, :, :], halves[:, 0, :, :], ALU.subtract).then_inc(low_ready, 1)
                pool.sem_inc(xT_ready, 2)
                with pool.Fori(0, NSUP // 2) as j:
                    for s in range(2):
                        i = 2 * j + s
                        pool.wait_ge(xTh_ready, i + 1)
                        at = bass.ds(SUP * P * i, SUP * P)
                        pool.tensor_tensor(xT[:, 1, at], xnT[:, s, :], xT[:, 0, at], ALU.subtract).then_inc(xT_ready, 1)

            @block.tensor
            def _(pe):
                pe.wait_ge(gate_prep, 2)
                pe.matmul(ps_m[:, 0:E], lnbB[:, :], gateT[:, :], start=True, stop=True).then_inc(gbias_mm, 1)
                pe.wait_ge(gbias_ready, 1)

                def turn_x(i, s, first):
                    pe.wait_ge(xn_ready, SUP * i + SUP)
                    if not first:
                        pe.wait_ge(xTh_ready, i - 1)
                    for g in range(SUP):
                        mm = pe.transpose(ps_u[s][0][:, P * g : P * g + P], xn[:, s, g, :], ident[:, :])
                    mm.then_inc(xn_transposed, 1)

                def logits(i, s):
                    pe.wait_ge(xnT_ready, i + 1)
                    pe.wait_ge(raw_ready, i + 1)
                    for g in range(SUP):
                        mm = pe.matmul(ps_l[s][:, E * g : E * g + E], xnT[:, s, P * g : P * g + P], gateS[:, :], start=True, stop=True)
                    mm.then_inc(logits_mm, 1)

                turn_x(0, 0, True)
                turn_x(1, 1, True)
                with pe.Fori(0, NSUP // 2 - 1) as j:
                    for s in range(2):
                        logits(2 * j + s, s)
                        turn_x(2 * j + s + 2, s, False)
                logits(NSUP - 2, 0)
                logits(NSUP - 1, 1)
                pe.wait_ge(xT_ready, NSUP + 2)
                pe.wait_ge(low_ready, 2)
                pe.sem_inc(h_ready, 2)
                pe.sem_inc(added, 3)

                def up(i, e, c):
                    pe.wait_ge(h_ready, C * NE * i + C * e + c + 1)
                    for w, bank in zip((wgs, wus), ps_u[c]):
                        product(pe, bank[:, :], lambda half: w[:, half, e, P * c : P * c + P],
                                lambda half: xT[:, half, bass.ds(SUP * P * i, SUP * P)]).then_inc(up_mm, 1)

                def down(i, e):
                    pe.wait_ge(h_ready, C * NE * i + C * e + C + 2)
                    pe.wait_ge(added, NE * i + e + 1)
                    for g in range(SUP):
                        for c in range(C):
                            mm = pe.matmul(ps_y[e % 3][:, g, :], hT[:, (C * e + c) % 6, P * g : P * g + P], wd[:, e, c, :],
                                           start=(c == 0), stop=(c == C - 1))
                    mm.then_inc(down_mm, 1)

                with pe.Fori(0, NSUP) as i:
                    for e in range(NE):
                        for c in range(C):
                            up(i, e, c)
                        if e:
                            down(i, e - 1)
                    down(i, NE - 1)

            @block.scalar
            def _(act):
                act.wait_ge(loaded, 16 * NLOAD)
                for w, halves in ((wg, wgs), (wu, wus)):
                    act.activation(halves[:, 0, :, :], w[:, :, :], ACT.Copy).then_inc(high_ready, 1)
                norm.act(act)
                with act.Fori(0, NSUP // 2) as j:
                    for s in range(2):
                        act.wait_ge(xn_transposed, 2 * j + s + 1)
                        act.wait_ge(xT_ready, 2 * j + s + 1)
                        act.activation(xnT[:, s, :], ps_u[s][0][:, :], ACT.Copy).then_inc(xnT_ready, 1)
                        act.activation(xT[:, 0, bass.ds(SUP * P * (2 * j + s), SUP * P)], ps_u[s][0][:, :], ACT.Copy).then_inc(xTh_ready, 1)
                act.wait_ge(gated, 2)
                act.activation(gs[:, 2, :], gs[:, 1, :], ACT.Sqrt).then_inc(gate_sqrt, 1)
                act.wait_ge(gated, 7)
                act.activation(gt[:, 3, :, :], gt[:, 2, :, :], ACT.Exp).then_inc(gate_exp, 1)
                act.preload_act_table(ACT.Silu)
                with act.Fori(0, NSUP) as i:
                    for n in range(C * NE):
                        act.wait_ge(up_mm, 2 * (C * NE * i + n) + 1)
                        act.activation(sg[:, n % 2, :], ps_u[n % 2][0][:, :], ACT.Silu).then_inc(silu_ready, 1)

            @block.vector
            def _(dve):
                norm.dve(dve, x)
                dve.wait_ge(loaded, 16 * NLOAD)
                dve.tensor_copy(lnbB[:, :], bcast(lnb[:, 0], P, 1)).then_inc(gate_prep, 1)
                dve.tensor_scalar(gateS[:, :], gateT[:, :], lns[:, 0:1], None, ALU.mult).then_inc(gate_prep, 1)
                dve.wait_ge(gbias_mm, 1)
                dve.tensor_copy(gbias[:, :], ps_m[:, 0:E]).then_inc(gbias_ready, 1)
                dve.sem_inc(raw_ready, 2)

                def norm_x(i, s):
                    for g in range(SUP):
                        norm.tile(dve, xn[:, s, g, :], x, SUP * i + g).then_inc(xn_ready, 1)

                def copy_logits(i, s):
                    dve.wait_ge(logits_mm, i + 1)
                    dve.tensor_copy(raw[:, bass.ds(SUP * i, SUP), :],
                                    ps_l[s][:, 0 : SUP * E].rearrange("p (g e) -> p g e", e=E)).then_inc(raw_ready, 1)

                norm_x(0, 0)
                norm_x(1, 1)
                with dve.Fori(0, NSUP // 2 - 1) as j:
                    for s in range(2):
                        dve.wait_ge(xn_transposed, 2 * j + s + 1)
                        norm_x(2 * j + s + 2, s)
                        copy_logits(2 * j + s, s)
                copy_logits(NSUP - 2, 0)
                copy_logits(NSUP - 1, 1)
                dve.wait_ge(raw_ready, NSUP + 2)

                g = lambda k: gt[:, k, :, :]
                dve.tensor_tensor(gs[:, 0, :], norm.rstd[:, :], norm.rstd[:, :], ALU.mult).then_inc(gated, 1)
                dve.wait_ge(gated, 1)
                dve.tensor_scalar(gs[:, 1, :], gs[:, 0, :], -EPS, 1.0 + EPS, ALU.mult, ALU.add).then_inc(gated, 1)
                dve.wait_ge(gate_sqrt, 1)
                dve.reciprocal(gs[:, 3, :], gs[:, 2, :]).then_inc(gated, 1)
                dve.wait_ge(gated, 3)
                dve.tensor_tensor(g(0), raw[:, :, :], bcast(gs[:, 3, :], E, 2), ALU.mult).then_inc(gated, 1)
                dve.wait_ge(gated, 4)
                dve.tensor_tensor(g(1), g(0), bcast(gbias[:, :], NT, 1), ALU.add).then_inc(gated, 1)
                dve.wait_ge(gated, 5)
                dve.tensor_reduce(gs[:, 4, :], g(1), AX, ALU.max).then_inc(gated, 1)
                dve.wait_ge(gated, 6)
                dve.tensor_tensor(g(2), g(1), bcast(gs[:, 4, :], E, 2), ALU.subtract).then_inc(gated, 1)
                dve.wait_ge(gate_exp, 1)
                dve.tensor_reduce(gs[:, 5, :], g(3), AX, ALU.add).then_inc(gated, 1)
                dve.wait_ge(gated, 8)
                dve.reciprocal(gs[:, 6, :], gs[:, 5, :]).then_inc(gated, 1)
                dve.wait_ge(gated, 9)
                dve.tensor_tensor(g(4), g(3), bcast(gs[:, 6, :], E, 2), ALU.mult).then_inc(gated, 1)
                dve.wait_ge(gated, 10)
                left, chosen = g(4), []
                step = 10
                for n in range(TOP):
                    top, even, mark, first, pick, rest = gs[:, 7 + n, :], g(5 + 4 * n), g(6 + 4 * n), norm.tmp[:, n, :], g(7 + 4 * n), g(8)
                    dve.tensor_reduce(top, left, AX, ALU.max).then_inc(gated, 1)
                    dve.wait_ge(gated, step + 1)
                    dve.tensor_tensor(even, left, bcast(top, E, 2), ALU.is_equal).then_inc(gated, 1)
                    dve.wait_ge(gated, step + 2)
                    dve.tensor_tensor(mark, even, bcast(order[:, :], NT, 1), ALU.mult).then_inc(gated, 1)
                    dve.wait_ge(gated, step + 3)
                    dve.tensor_reduce(first, mark, AX, ALU.max).then_inc(gated, 1)
                    dve.wait_ge(gated, step + 4)
                    dve.tensor_tensor(pick, mark, bcast(first, E, 2), ALU.is_equal).then_inc(gated, 1)
                    dve.wait_ge(gated, step + 5)
                    chosen.append(pick)
                    if n == 0:
                        dve.scalar_tensor_tensor(rest, pick, -2.0, left, ALU.mult, ALU.add).then_inc(gated, 1)
                        dve.wait_ge(gated, step + 6)
                        left, step = rest, step + 6
                dve.tensor_tensor(g(12), chosen[0], chosen[1], ALU.add).then_inc(gated, 1)
                dve.wait_ge(gated, 22)
                dve.tensor_tensor(g(13), g(12), g(4), ALU.mult).then_inc(gated, 1)
                dve.wait_ge(gated, 23)
                dve.tensor_reduce(gs[:, 9, :], g(13), AX, ALU.add).then_inc(gated, 1)
                dve.wait_ge(gated, 24)
                dve.tensor_scalar(gs[:, 10, :], gs[:, 9, :], EPS, None, ALU.add).then_inc(gated, 1)
                dve.wait_ge(gated, 25)
                dve.reciprocal(gs[:, 11, :], gs[:, 10, :]).then_inc(gated, 1)
                dve.wait_ge(gated, 26)
                dve.tensor_tensor(weight[:, :, :], g(13), bcast(gs[:, 11, :], E, 2), ALU.mult).then_inc(gated, 1)
                dve.wait_ge(gated, 27)

                def hidden(i, e):
                    for c in range(C):
                        n = C * NE * i + C * e + c + 1
                        dve.wait_ge(silu_ready, n)
                        dve.wait_ge(up_mm, 2 * n)
                        dve.tensor_tensor(hT[:, (C * e + c) % 6, :], sg[:, c, :], ps_u[c][1][:, :], ALU.mult).then_inc(h_ready, 1)

                def add(i, e):
                    dve.wait_ge(down_mm, NE * i + e + 1)
                    dve.wait_ge(added, NE * i + e + 3)
                    if e == 0:
                        view = x[:, bass.ds(SUP * i, SUP), :]
                        dve.tensor_tensor(view, view, ps_y[0][:, :, :], ALU.add).then_inc(added, 1)
                    else:
                        for g in range(SUP):
                            t = SUP * i + g
                            op = dve.scalar_tensor_tensor(x[:, t, :], ps_y[e % 3][:, g, :], weight[:, t, e - 1 : e], x[:, t, :],
                                                          ALU.mult, ALU.add)
                        op.then_inc(added, 1)

                with dve.Fori(0, NSUP) as i:
                    for e in range(NE):
                        hidden(i, e)
                        if e:
                            add(i, e - 1)
                    add(i, NE - 1)
                    if stats is not None:
                        dve.wait_ge(added, NE * i + NE + 3)
                        for g in range(SUP):
                            t = SUP * i + g
                            dve.bn_stats(stats[:, t, :], x[:, t, :]).then_inc(counted, 1)
                dve.wait_ge(added, NE * NSUP + 3)
                if stats is not None:
                    dve.wait_ge(counted, NT)


INNER, STATE, TAPS, HEADS = 256, 64, 4, 4
HEADDIM = INNER // HEADS
ZD = INNER + HEADS


def load_weights(nc, x, norm, m, dirs):
    shapes = {
        "in": [D, 2 * INNER + 2 * STATE + HEADS], "zd": [D, ZD], "conv_w": [P, 3, TAPS], "conv_b": [P, 3],
        "dt_bias": [P, HEADS], "a_log": [P, HEADS], "dp": [P, HEADS], "norm_w": [P, 2], "out_w": [P, 2, D],
        "strict": [P, P], "inclusive": [P, P],
    }
    loaded = m.sem("loaded")
    pick = m.sb("pick", [P, P])
    weights = [{n: m.sb(f"{n}{k}", shape) for n, shape in shapes.items()} for k in range(len(dirs))]
    with nc.Block() as block:

        @block.sync
        def _(sp):
            sp.dma_start(pick[:, :], dirs[0]["pick"]).then_inc(loaded, 16)
            count = 1
            for w, dram in zip(weights, dirs):
                for n in shapes:
                    every = tuple(slice(None) for _ in shapes[n])
                    if n == "zd":
                        sp.dma_start(w[n][:, 0:INNER], dram["in"][:, 0:INNER]).then_inc(loaded, 16)
                        sp.dma_start(w[n][:, INNER:ZD], dram["in"][:, 2 * INNER + 2 * STATE :]).then_inc(loaded, 16)
                        count += 2
                    else:
                        sp.dma_start(w[n][every], dram[n]).then_inc(loaded, 16)
                        count += 1
            sp.wait_ge(loaded, 16 * count)

        @block.scalar
        def _(act):
            norm.act(act)

        @block.vector
        def _(dve):
            norm.dve(dve, x)

    return [dict(w, pick=pick) for w in weights]


def ssm_inputs(nc, x, ident, norm, m, backward, w, store):
    CH = 3
    NB = 2
    with ExitStack() as stack:
        k = Scope(nc, stack, m.prefix + "i")
        win, wzd, cw, cb, pick = w["in"], w["zd"], w["conv_w"], w["conv_b"], w["pick"]
        centred = k.sb("centred", [P, SUP, D])
        xn = k.sb("xn", [P, SUP, D])
        xnT = k.sb("xnT", [D, SUP * P])
        pad = k.sb("pad", [P, CH, NB, S + TAPS - 1])
        acc = k.sb("acc", [P, CH, NB, S])
        xs = k.sb("xs", [P, CH, NB, S])
        cs = k.sb("cs", [P, SUP * P])
        ps_a = [k.ps(f"ps_a{n}", [P, 512]) for n in range(4)]
        ps_b = [k.ps(f"ps_b{n}", [P, 512]) for n in range(4)]
        padded, centred_ready = k.sem("padded"), k.sem("centred_ready")
        xn_ready, xn_transposed, xnT_ready = k.sem("xn_ready"), k.sem("xn_transposed"), k.sem("xnT_ready")
        in_mm, in_ready = k.sem("in_mm"), k.sem("in_ready")
        z_mm, z_ready, dt_ready = k.sem("z_mm"), k.sem("z_ready"), k.sem("dt_ready")
        conv, xs_ready = k.sem("conv"), k.sem("xs_ready")
        c_mm, c_ready, c_kept = k.sem("c_mm"), k.sem("c_ready"), k.sem("c_kept")
        g_mm, g_ready = k.sem("g_mm"), k.sem("g_ready")
        turned, xb_ready = k.sem("turned"), k.sem("xb_ready")
        first = 0 if backward else TAPS - 1
        hole = S if backward else 0
        CONV = CH * TAPS

        def tiles(buf, i, g):
            return buf[:, B * (g % 2) + NB * i + g // 2, :]

        with nc.Block() as block:

            @block.gpsimd
            def _(pool):
                pool.memset(pad[:, :, :, hole : hole + TAPS - 1], 0.0).then_inc(padded, 1)
                pool.sem_inc(c_kept, 1)

                def norm_x(i):
                    of = lambda buf: buf.rearrange("p (u b) d -> p b u d", u=2)[:, bass.ds(NB * i, NB), :, :]
                    stat = lambda buf: bcast(buf.rearrange("p (u b) -> p b u", u=2)[:, bass.ds(NB * i, NB), :], D, 3)
                    grid = lambda buf: buf[:, :, :].rearrange("p (b u) d -> p b u d", u=2)
                    pool.tensor_tensor(grid(centred), of(x[:, :, :]), stat(norm.mean[:, :]), ALU.subtract).then_inc(centred_ready, 1)
                    pool.wait_ge(centred_ready, i + 1)
                    pool.tensor_tensor(grid(xn), grid(centred), stat(norm.rstd[:, :]), ALU.mult).then_inc(xn_ready, 1)

                def keep(i):
                    pool.wait_ge(c_ready, i + 1)
                    for g in range(SUP):
                        op = pool.tensor_copy(tiles(store["c"], i, g), cs[0:STATE, P * g : P * g + P])
                    op.then_inc(c_kept, 1)

                norm_x(0)
                pool.wait_ge(xn_transposed, 1)
                norm_x(1)
                with pool.Fori(0, NSUP - 2) as i:
                    pool.wait_ge(xn_transposed, i + 2)
                    norm_x(i + 2)
                    keep(i)
                keep(NSUP - 2)
                keep(NSUP - 1)

            @block.tensor
            def _(pe):
                def turn_x(i):
                    pe.wait_ge(xn_ready, i + 1)
                    for g in range(SUP):
                        mm = pe.transpose(ps_a[0][:, P * g : P * g + P], xn[:, g, :], ident[:, :])
                    mm.then_inc(xn_transposed, 1)

                def project(i):
                    pe.wait_ge(xnT_ready, i + 1)
                    pe.wait_ge(in_ready, CH * i + CH)
                    for c in range(CH):
                        if c == CH - 1:
                            pe.wait_ge(g_ready, i + 1)
                        mm = pe.matmul(ps_a[1 + c][:, :], win[:, INNER + P * c : INNER + P * c + P], xnT[:, :], start=True, stop=True)
                        mm.then_inc(in_mm, 1)
                    pe.wait_ge(xb_ready, SUP * i + 1)
                    for g in range(SUP):
                        mm = pe.matmul(ps_b[g][:, 0:ZD], xnT[:, P * g : P * g + P], wzd[:, :], start=True, stop=True)
                        mm.then_inc(z_mm, 1)

                def finish(i, last):
                    pe.wait_ge(xs_ready, CH * i + CH)
                    if last:
                        pe.wait_ge(xb_ready, SUP * i + SUP + 1)
                        pe.wait_ge(g_ready, i + 2)
                    pe.matmul(ps_a[0][:, :], pick[:, :], xs[:, 2, :, :], start=True, stop=True).then_inc(c_mm, 1)
                    for g in range(SUP):
                        held = SUP * i + g + (1 if last else SUP + 1)
                        pe.wait_ge(z_ready, held)
                        pe.wait_ge(dt_ready, held)
                        for c in range(CH):
                            mm = pe.transpose(ps_b[g][:, P * c : P * c + P], xs[:, c, g // 2, P * (g % 2) : P * (g % 2) + P], ident[:, :])
                        mm.then_inc(turned, 1)
                    pe.wait_ge(c_ready, i + 1)
                    if not last:
                        pe.wait_ge(in_ready, CH * i + 3 * CH)
                    for g in range(SUP):
                        mm = pe.matmul(ps_a[CH][:, P * g : P * g + P], xs[:, 2, g // 2, P * (g % 2) : P * (g % 2) + P],
                                       cs[:, P * g : P * g + P], start=True, stop=True)
                    mm.then_inc(g_mm, 1)

                pe.sem_inc(in_ready, CH)
                pe.sem_inc(g_ready, 2)
                pe.sem_inc(xb_ready, SUP + 1)
                turn_x(0)
                project(0)
                turn_x(1)
                pe.wait_ge(dt_ready, SUP)
                with pe.Fori(0, NSUP - 2) as i:
                    project(i + 1)
                    finish(i, False)
                    turn_x(i + 2)
                project(NSUP - 1)
                finish(NSUP - 2, False)
                finish(NSUP - 1, True)

            @block.scalar
            def _(act):
                act.preload_act_table(ACT.Silu)
                act.wait_ge(padded, 1)

                def copy_x(i):
                    act.wait_ge(xn_transposed, i + 1)
                    act.activation(xnT[:, :], ps_a[0][:, :], ACT.Copy).then_inc(xnT_ready, 1)

                def copy_projections(i):
                    for c in range(CH):
                        act.wait_ge(in_mm, CH * i + c + 1)
                        act.activation(pad[:, c, :, first : first + S], ps_a[1 + c][:, :].rearrange("p (b s) -> p b s", b=NB),
                                       ACT.Copy).then_inc(in_ready, 1)
                    for g in range(SUP):
                        act.wait_ge(z_mm, SUP * i + g + 1)
                        act.activation(tiles(store["z"], i, g), ps_b[g][:, 0:INNER], ACT.Silu).then_inc(z_ready, 1)

                def convolved(i, first_time):
                    for c in range(CH):
                        act.wait_ge(conv, CONV * i + TAPS * (c + 1))
                        if c == CH - 1 and not first_time:
                            act.wait_ge(g_mm, i)
                        act.activation(xs[:, c, :, :], acc[:, c, :, :], ACT.Silu).then_inc(xs_ready, 1)

                def copy_finished(i):
                    act.wait_ge(c_mm, i + 1)
                    act.wait_ge(c_kept, i + 1)
                    act.activation(cs[:, :], ps_a[0][:, :], ACT.Copy).then_inc(c_ready, 1)
                    for g in range(SUP):
                        act.wait_ge(turned, SUP * i + g + 1)
                        act.activation(tiles(store["xb"], i, g), ps_b[g][:, 0 : INNER + STATE], ACT.Copy).then_inc(xb_ready, 1)

                copy_x(0)
                copy_projections(0)
                copy_x(1)
                convolved(0, True)
                with act.Fori(0, NSUP - 2) as i:
                    copy_projections(i + 1)
                    copy_finished(i)
                    copy_x(i + 2)
                    convolved(i + 1, False)
                copy_projections(NSUP - 1)
                copy_finished(NSUP - 2)
                convolved(NSUP - 1, False)
                copy_finished(NSUP - 1)

            @block.vector
            def _(dve):

                def convolve(i, first_time):
                    for c in range(CH):
                        dve.wait_ge(in_ready, CH * i + c + CH + 1)
                        if not first_time:
                            dve.wait_ge(xs_ready, CH * i + c - CH + 1)
                        for n in range(TAPS):
                            at = TAPS - 1 - n if backward else n
                            src = pad[:, c, :, at : at + S]
                            if n == 0:
                                op = dve.tensor_scalar(acc[:, c, :, :], src, cw[:, c, 0:1], cb[:, c : c + 1], ALU.mult, ALU.add)
                            else:
                                dve.wait_ge(conv, CONV * i + TAPS * c + n)
                                op = dve.scalar_tensor_tensor(acc[:, c, :, :], src, cw[:, c, n : n + 1], acc[:, c, :, :],
                                                              ALU.mult, ALU.add)
                            op.then_inc(conv, 1)
                        if c == 0:
                            for g in range(SUP):
                                dve.wait_ge(z_mm, SUP * i + g + 1)
                                dve.wait_ge(z_ready, SUP * i + g + 1)
                                dve.tensor_copy(tiles(store["dt"], i, g), ps_b[g][:, INNER:ZD]).then_inc(dt_ready, 1)

                def finish(i):
                    dve.wait_ge(g_mm, i + 1)
                    for g in range(SUP):
                        op = dve.tensor_tensor(tiles(store["g"], i, g), ps_a[CH][:, P * g : P * g + P], w["inclusive"][:, :], ALU.mult)
                    op.then_inc(g_ready, 1)

                convolve(0, True)
                with dve.Fori(0, NSUP - 2) as i:
                    convolve(i + 1, False)
                    finish(i)
                convolve(NSUP - 1, False)
                finish(NSUP - 2)
                finish(NSUP - 1)


def ssm_scan(nc, ident, m, backward, w, store, y_out, ssq):
    FAR = -120.0
    GX = HEADS * P
    with ExitStack() as stack:
        k = Scope(nc, stack, m.prefix + "s")
        small = k.sb("small", [P, 10, NT, HEADS])
        dtb, alog, dp, nw, ow_raw, strict = (w[n] for n in ("dt_bias", "a_log", "dp", "norm_w", "out_w", "strict"))
        aneg = k.sb("a_neg", [P, HEADS])
        ow = k.sb("out_w", [P, 2, D])
        an = k.sb("a_masked", [P, 2, HEADS, P])
        ex = k.sb("decay", [P, 2, HEADS, P])
        mt = k.sb("mt", [P, 2, HEADS, P])
        u = k.sb("u", [P, 2, HEADS, HEADDIM])
        ud = k.sb("u_decayed", [P, HEADS, HEADDIM])
        xd = k.sb("x_skip", [P, 2, HEADS, HEADDIM])
        bs = k.sb("b_staged", [P, STATE])
        cst = k.sb("c_staged", [STATE, P])
        st = k.sb("state", [STATE, INNER])
        eb = k.sb("edge_decay", [P, 2, HEADS])
        yi = k.sb("y_inter", [P, HEADS, HEADDIM])
        y1 = k.sb("y1", [P, 2, INNER])
        y2 = k.sb("y2", [P, 2, INNER])
        y3 = k.sb("y3", [P, 2, INNER])
        sq = k.sb("squares", [P, 2, INNER])
        yT = k.sb("yT", [P, 2, 2, P])
        ps_d = [k.ps(f"ps_d{n}", [P, HEADS, P]) for n in range(2)]
        ps_y = [k.ps(f"ps_y{n}", [P, 512]) for n in range(2)]
        ps_e = k.ps("ps_e", [P, 512])
        ps_s = k.ps("ps_s", [P, 512])
        ps_t = [k.ps(f"ps_t{n}", [P, 512]) for n in range(2)]
        prep, a_sem = k.sem("prep"), k.sem("act_prep")
        masked_ready, d_mm, ex_ready = k.sem("a_masked_ready"), k.sem("d_mm"), k.sem("ex_ready")
        staged, edge_mm, edge_ready = k.sem("staged"), k.sem("edge_mm"), k.sem("edge_ready")
        u_ready, mt_ready, ud_ready = k.sem("u_ready"), k.sem("mt_ready"), k.sem("ud_ready")
        state_mm, state_ready, inter_mm, inter_ready = k.sem("state_mm"), k.sem("state_ready"), k.sem("inter_mm"), k.sem("inter_ready")
        y_mm, y1_ready, y2_ready, y3_ready = k.sem("y_mm"), k.sem("y1_ready"), k.sem("y2_ready"), k.sem("y3_ready")
        sq_ready, turned, yT_ready, out_mm, out_ready = (k.sem("sq_ready"), k.sem("turned"), k.sem("yT_ready"),
                                                         k.sem("out_mm"), k.sem("out_ready"))
        xd_ready = k.sem("xd_ready")
        order = (1, 0) if backward else (0, 1)

        def tile(q, b):
            return B * order[q] + b

        dt, a = small[:, 8, :, :], small[:, 9, :, :]
        with nc.Block() as block:

            @block.gpsimd
            def _(pool):
                pool.wait_ge(prep, 9)
                pool.sem_inc(staged, 2)
                with pool.Fori(0, B) as b:
                    for q in range(2):
                        pool.wait_ge(d_mm, 2 * b + q + 1)
                        pool.tensor_tensor(an[:, q, :, :], bcast(w["inclusive"][:, :], HEADS, 1), bcast(a[:, tile(q, b), :], P, 2),
                                           ALU.mult).then_inc(masked_ready, 1)
                    pool.wait_ge(state_mm, b + 1)
                    pool.tensor_copy(bs[:, :], store["xb"][:, tile(0, b), INNER:]).then_inc(staged, 1)
                    pool.wait_ge(inter_mm, b + 1)
                    pool.tensor_copy(cst[:, :], store["c"][:, tile(1, b), :]).then_inc(staged, 1)
                    for q in range(2):
                        pool.wait_ge(y1_ready, 2 * b + q + 1)
                        view = store["xb"][:, tile(q, b), 0:INNER].rearrange("p (h d) -> p h d", h=HEADS)
                        pool.tensor_tensor(xd[:, q, :, :], view, bcast(dp[:, :], HEADDIM, 2), ALU.mult).then_inc(xd_ready, 1)

            @block.tensor
            def _(pe):
                pe.wait_ge(prep, 9)
                pe.sem_inc(d_mm, 2)
                pe.sem_inc(state_mm, 1)
                pe.sem_inc(inter_mm, 1)

                def decays(b, q):
                    n = 2 * b + q
                    pe.wait_ge(masked_ready, n + 1)
                    pe.wait_ge(ex_ready, n + 1)
                    pe.matmul(ps_d[q][:, :, :], strict[:, :], an[:, q, :, :], start=True, stop=True).then_inc(d_mm, 1)
                    pe.wait_ge(edge_ready, n + 1)
                    lhs = strict if q == 0 else w["inclusive"]
                    pe.matmul(ps_e[:, 0:HEADS], lhs[:, :], a[:, tile(q, b), :], start=True, stop=True).then_inc(edge_mm, 1)

                def product(b, q):
                    n = 2 * b + q
                    pe.wait_ge(mt_ready, n + 1)
                    pe.wait_ge(u_ready, n + 1)
                    pe.wait_ge(y1_ready, n + 1)
                    for h in range(HEADS):
                        mm = pe.matmul(ps_y[q][:, HEADDIM * h : HEADDIM * h + HEADDIM], mt[:, q, h, :], u[:, q, h, :], start=True, stop=True)
                    mm.then_inc(y_mm, 1)

                def carry(b, q):
                    pe.wait_ge(staged, 2 * b + q + 3)
                    if q == 0:
                        pe.wait_ge(inter_ready, 2 * b + 1)
                        pe.wait_ge(ud_ready, b + 1)
                        pe.matmul(ps_s[0:STATE, 0:INNER], bs[:, :], ud[:, :, :], start=True, stop=True).then_inc(state_mm, 1)
                    else:
                        pe.wait_ge(state_ready, b + 1)
                        pe.matmul(ps_s[:, 0:INNER], cst[:, :], st[:, :], start=True, stop=True).then_inc(inter_mm, 1)

                def turn(b, q):
                    n = 2 * b + q
                    pe.wait_ge(y3_ready, n + 1)
                    pe.wait_ge(out_ready, n + 1)
                    for c in range(2):
                        mm = pe.transpose(ps_t[q][:, P * c : P * c + P], y3[:, q, P * c : P * c + P], ident[:, :])
                    mm.then_inc(turned, 1)

                def out(b, q):
                    pe.wait_ge(yT_ready, 2 * b + q + 1)
                    for c in range(2):
                        mm = pe.matmul(ps_t[q][:, INNER : INNER + D], yT[:, q, c, :], ow[:, c, :], start=(c == 0), stop=(c == 1))
                    mm.then_inc(out_mm, 1)

                def batch(b, first, last):
                    carry(b, 0)
                    product(b, 0)
                    if not first:
                        turn(b - 1, 1)
                    if not last:
                        decays(b + 1, 0)
                    carry(b, 1)
                    if not first:
                        out(b - 1, 1)
                    product(b, 1)
                    turn(b, 0)
                    if not last:
                        decays(b + 1, 1)
                    out(b, 0)

                decays(0, 0)
                decays(0, 1)
                batch(0, True, False)
                with pe.Fori(1, B - 1) as b:
                    batch(b, False, False)
                batch(B - 1, False, True)
                turn(B - 1, 1)
                out(B - 1, 1)

            @block.scalar
            def _(act):
                act.activation(aneg[:, :], alog[:, :], ACT.Exp).then_inc(a_sem, 1)
                act.wait_ge(prep, 4)
                act.activation(small[:, 3, :, :], small[:, 2, :, :], ACT.Exp, scale=-1.0).then_inc(a_sem, 1)
                act.wait_ge(a_sem, 2)
                act.activation(small[:, 4, :, :], small[:, 3, :, :], ACT.Ln, bias=1.0).then_inc(a_sem, 1)
                act.wait_ge(a_sem, 3)
                act.preload_act_table(ACT.Exp)
                act.sem_inc(ex_ready, 2)
                act.sem_inc(edge_ready, 1)

                def decays(b, q):
                    n = 2 * b + q
                    act.wait_ge(d_mm, n + 3)
                    act.activation(ex[:, q, :, :], ps_d[q][:, :, :], ACT.Exp).then_inc(ex_ready, 1)
                    act.wait_ge(edge_mm, n + 1)
                    if q == 1:
                        act.wait_ge(inter_ready, 2 * b + 1)
                    act.activation(eb[:, q, :], ps_e[:, 0:HEADS], ACT.Exp).then_inc(edge_ready, 1)

                def copy_state(b):
                    act.wait_ge(state_mm, b + 2)
                    act.activation(st[:, :], ps_s[0:STATE, 0:INNER], ACT.Copy).then_inc(state_ready, 1)

                def square(b, q):
                    n = 2 * b + q
                    act.wait_ge(y3_ready, n + 1)
                    act.activation(sq[:, q, :], y3[:, q, :], ACT.Square, accum_out=ssq[:, bass.ds(tile(q, b), 1)]).then_inc(sq_ready, 1)
                    act.wait_ge(turned, n + 1)
                    act.activation(yT[:, q, :, :], ps_t[q][:, 0:INNER].rearrange("p (c j) -> p c j", c=2), ACT.Copy).then_inc(yT_ready, 1)

                def copy_out(b, q):
                    act.wait_ge(out_mm, 2 * b + q + 1)
                    act.activation(y_out[:, tile(q, b), :], ps_t[q][:, INNER : INNER + D], ACT.Copy).then_inc(out_ready, 1)

                def batch(b, first, last):
                    copy_state(b)
                    if not first:
                        square(b - 1, 1)
                    if not last:
                        decays(b + 1, 0)
                    if not first:
                        copy_out(b - 1, 1)
                    square(b, 0)
                    if not last:
                        decays(b + 1, 1)
                    copy_out(b, 0)

                act.sem_inc(out_ready, 2)
                decays(0, 0)
                decays(0, 1)
                batch(0, True, False)
                with act.Fori(1, B - 1) as b:
                    batch(b, False, False)
                batch(B - 1, False, True)
                square(B - 1, 1)
                copy_out(B - 1, 1)
                act.wait_ge(out_ready, NT + 2)

            @block.vector
            def _(dve):
                s = lambda n: small[:, n, :, :]
                dve.tensor_tensor(s(0), store["dt"][:, :, :], bcast(dtb[:, :], NT, 1), ALU.add).then_inc(prep, 1)
                dve.wait_ge(prep, 1)
                dve.tensor_scalar(s(1), s(0), -1.0, None, ALU.mult).then_inc(prep, 1)
                dve.tensor_scalar(s(5), s(0), 0.0, None, ALU.max).then_inc(prep, 1)
                dve.wait_ge(prep, 3)
                dve.tensor_tensor(s(2), s(0), s(1), ALU.max).then_inc(prep, 1)
                for c in range(2):
                    dve.tensor_scalar(ow[:, c, :], ow_raw[:, c, :], nw[:, c : c + 1], None, ALU.mult).then_inc(prep, 1)
                dve.wait_ge(a_sem, 3)
                dve.tensor_tensor(dt, s(4), s(5), ALU.add).then_inc(prep, 1)
                dve.wait_ge(prep, 7)
                dve.scalar_tensor_tensor(s(6), dt, -1.0, bcast(aneg[:, :], NT, 1), ALU.mult, ALU.mult).then_inc(prep, 1)
                dve.wait_ge(prep, 8)
                dve.tensor_scalar(a, s(6), FAR, None, ALU.max).then_inc(prep, 1)
                dve.wait_ge(prep, 9)
                dve.sem_inc(y1_ready, 2)
                dve.sem_inc(inter_ready, 2)

                def inputs(b, q):
                    t = tile(q, b)
                    view = store["xb"][:, t, 0:INNER].rearrange("p (h d) -> p h d", h=HEADS)
                    dve.tensor_tensor(u[:, q, :, :], view, bcast(dt[:, t, :], HEADDIM, 2), ALU.mult).then_inc(u_ready, 1)
                    if q == 0:
                        dve.wait_ge(edge_ready, 2 * b + 2)
                        dve.wait_ge(u_ready, 2 * b + 1)
                        dve.tensor_tensor(ud[:, :, :], u[:, 0, :, :], bcast(eb[:, 0, :], HEADDIM, 2), ALU.mult).then_inc(ud_ready, 1)
                    dve.wait_ge(ex_ready, 2 * b + q + 3)
                    dve.tensor_tensor(mt[:, q, :, :], ex[:, q, :, :], bcast(store["g"][:, t, :], HEADS, 1), ALU.mult).then_inc(mt_ready, 1)

                def gate(b, q):
                    n, t = 2 * b + q, tile(q, b)
                    flat = lambda ap: ap.rearrange("p h d -> p (h d)")
                    skip = flat(xd[:, q, :, :])
                    if q == 1:
                        dve.wait_ge(inter_mm, b + 2)
                        dve.wait_ge(edge_ready, 2 * b + 3)
                        dve.tensor_tensor(yi[:, :, :], ps_s[:, 0:INNER].rearrange("p (h d) -> p h d", h=HEADS),
                                          bcast(eb[:, 1, :], HEADDIM, 2), ALU.mult).then_inc(inter_ready, 1)
                        dve.wait_ge(inter_ready, 2 * b + 3)
                        dve.wait_ge(xd_ready, n + 1)
                        dve.tensor_tensor(y1[:, 0, :], flat(yi[:, :, :]), skip, ALU.add).then_inc(inter_ready, 1)
                        dve.wait_ge(inter_ready, 2 * b + 4)
                        skip = y1[:, 0, :]
                    dve.wait_ge(y_mm, n + 1)
                    dve.wait_ge(xd_ready, n + 1)
                    dve.tensor_tensor(y2[:, q, :], ps_y[q][:, 0:INNER], skip, ALU.add).then_inc(y1_ready, 1)
                    dve.wait_ge(y1_ready, n + 3)
                    dve.tensor_tensor(y3[:, q, :], y2[:, q, :], store["z"][:, t, :], ALU.mult).then_inc(y3_ready, 1)

                def batch(b, last):
                    gate(b, 0)
                    if not last:
                        inputs(b + 1, 0)
                    gate(b, 1)
                    if not last:
                        inputs(b + 1, 1)

                inputs(0, 0)
                inputs(0, 1)
                with dve.Fori(0, B - 1) as b:
                    batch(b, False)
                batch(B - 1, True)


def state_space(nc, x, ident, dirs, stats=None):
    with ExitStack() as stack:
        m = Scope(nc, stack, "ss")
        norm = Norm(m, stats)
        weights = load_weights(nc, x, norm, m, dirs)
        y_out = [m.sb(f"y_out{n}", [P, NT, D]) for n in range(2)]
        ssq = [m.sb(f"ssq{n}", [P, NT]) for n in range(2)]
        store = {
            "z": m.sb("silu_z", [P, NT, INNER]), "xb": m.sb("x_and_b", [P, NT, INNER + STATE]),
            "c": m.sb("c_feat", [STATE, NT, P]), "g": m.sb("scores", [P, NT, P]), "dt": m.sb("dt_raw", [P, NT, HEADS]),
        }
        for n, w in enumerate(weights):
            k = Scope(nc, stack, f"ss{n}")
            ssm_inputs(nc, x, ident, norm, k, n == 1, w, store)
            ssm_scan(nc, ident, k, n == 1, w, store, y_out[n], ssq[n])

        mean = m.sb("mean_square", [P, 2, NT])
        root = m.sb("root", [P, 2, NT])
        r = m.sb("rms", [P, 2, NT])
        meant, rooted, inv, added = m.sem("meant"), m.sem("rooted"), m.sem("inverted"), m.sem("added")
        scaled = m.sem("scaled")
        with nc.Block() as block:

            @block.scalar
            def _(act):
                act.wait_ge(meant, 2)
                act.activation(root[:, :, :], mean[:, :, :], ACT.Sqrt).then_inc(rooted, 1)

            @block.vector
            def _(dve):
                for n in range(2):
                    dve.tensor_scalar(mean[:, n, :], ssq[n][:, :], 1.0 / INNER, EPS, ALU.mult, ALU.add).then_inc(meant, 1)
                dve.wait_ge(rooted, 1)
                dve.reciprocal(r[:, :, :], root[:, :, :]).then_inc(inv, 1)
                dve.wait_ge(inv, 1)
                dve.tensor_tensor(y_out[0][:, :, :], y_out[0][:, :, :], bcast(r[:, 0, :], D, 2), ALU.mult).then_inc(added, 1)
                dve.wait_ge(added, 1)
                dve.tensor_tensor(x[:, :, :], x[:, :, :], y_out[0][:, :, :], ALU.add).then_inc(added, 1)
                dve.wait_ge(added, 2)
                dve.wait_ge(scaled, 1)
                dve.tensor_tensor(x[:, :, :], x[:, :, :], y_out[1][:, :, :], ALU.add).then_inc(added, 1)
                dve.wait_ge(added, 3)

            @block.gpsimd
            def _(pool):
                pool.wait_ge(inv, 1)
                pool.tensor_tensor(y_out[1][:, :, :], y_out[1][:, :, :], bcast(r[:, 1, :], D, 2), ALU.mult).then_inc(scaled, 1)


def cross_attention(nc, x, ident, ctxT_dram, ctx2T_dram, mask_dram, wq_dram, wk_dram, wv_dram, wo_dram, stats=None):
    H, HD, K = 16, 64, 64
    HP = H // 2
    SCALE = 1.0 / HD**0.5
    with ExitStack() as stack:
        m = Scope(nc, stack, "xa")
        norm = Norm(m)
        mask = m.sb("mask", [P, NT, K])
        wq = m.sb("wq", [D, H * HD])
        wo = m.sb("wo", [P, HP, D])
        keys = m.sb("keys", [P, HP, B, K])
        vals = m.sb("vals", [P, B, HP, HD])
        kblock = m.sb("kblock", [P, HP, 2, K])
        vblock = m.sb("vblock", [P, HP, 2, HD])
        wqs = m.sb("wq_halves", [D, 2, H * HD], F32R)
        wq_high, wq_low = m.sem("wq_high"), m.sem("wq_low")
        load_done = m.sem("loaded")
        zeroed = m.sem("blocks_zeroed")
        with ExitStack() as inner:
            k = Scope(nc, inner, "xk")
            ctxT = k.sb("ctxT", [D, B * K])
            ctx2T = k.sb("ctx2T", [D, B, 2 * K])
            wk = k.sb("wk", [D, H * HD])
            wv = k.sb("wv", [D, H * HD])
            ps_k = [k.ps(f"ps_k{n}", [P, 8, K]) for n in range(4)]
            ps_v = [k.ps(f"ps_v{n}", [P, HP, 2, HD]) for n in range(2)]
            key_mm, key_ready = k.sem("key_mm"), k.sem("key_ready")
            val_mm, val_low, val_high = k.sem("val_mm"), k.sem("val_low"), k.sem("val_high")
            ctx_copied, raw_masked = k.sem("ctx_copied"), k.sem("masked")
            NLOAD = 5
            key_loaded = k.sem("key_loaded")
            with nc.Block() as block:

                @block.sync
                def _(sp):
                    for dst, src in ((ctxT[:, :], ctxT_dram), (wk[:, :], wk_dram)):
                        sp.dma_start(dst, src).then_inc(key_loaded, 16)
                    for dst, src in ((ctx2T[:, :, :], ctx2T_dram), (wv[:, :], wv_dram),
                                     (mask[:, :, :], mask_dram), (wq[:, :], wq_dram),
                                     (wo[:, :, :], wo_dram.rearrange("(c p) n -> p c n", p=P))):
                        sp.dma_start(dst, src).then_inc(load_done, 16)

                @block.gpsimd
                def _(pool):
                    pool.memset(kblock[:, :, :, :], 0.0).then_inc(zeroed, 1)
                    pool.memset(vblock[:, :, :, :], 0.0).then_inc(zeroed, 1)
                    pool.wait_ge(wq_high, 1)
                    pool.tensor_tensor(wqs[:, 1, :], wq[:, :], wqs[:, 0, :], ALU.subtract).then_inc(wq_low, 1)

                @block.tensor
                def _(pe):
                    pe.wait_ge(key_loaded, 32)
                    for c in range(HP):
                        for n in range(2):
                            f = 2 * c + n
                            if f >= 4:
                                pe.wait_ge(key_ready, f - 3)
                            pe.matmul(ps_k[f % 4][:, :, :], wk[:, P * c : P * c + P], ctxT[:, 512 * n : 512 * n + 512],
                                      start=True, stop=True).then_inc(key_mm, 1)
                    pe.wait_ge(load_done, 16 * NLOAD)
                    for b in range(B):
                        if b >= 2:
                            pe.wait_ge(val_low, b - 1)
                            pe.wait_ge(val_high, b - 1)
                        for n in range(2):
                            mm = pe.matmul(ps_v[b % 2][:, 4 * n : 4 * n + 4, :, :], ctx2T[:, b, :], wv[:, 512 * n : 512 * n + 512],
                                           start=True, stop=True)
                        mm.then_inc(val_mm, 1)

                @block.scalar
                def _(act):
                    norm.act(act, ACT.Exp)
                    for f in range(2 * HP):
                        act.wait_ge(key_mm, f + 1)
                        act.activation(keys[:, f // 2, 8 * (f % 2) : 8 * (f % 2) + 8, :], ps_k[f % 4][:, :, :], ACT.Copy).then_inc(key_ready, 1)
                    act.wait_ge(load_done, 16 * NLOAD)
                    act.activation(wqs[:, 0, :], wq[:, :], ACT.Copy).then_inc(wq_high, 1)
                    for b in range(B):
                        act.wait_ge(val_mm, b + 1)
                        act.activation(vals[0:K, b, :, :], ps_v[b % 2][0:K, :, 0, :], ACT.Copy).then_inc(val_low, 1)

                @block.vector
                def _(dve):
                    norm.dve(dve, x)
                    dve.wait_ge(load_done, 16 * NLOAD)
                    dve.tensor_scalar(mask[:, :, :], mask[:, :, :], -1.0e9, None, ALU.mult).then_inc(raw_masked, 1)
                    for b in range(B):
                        dve.wait_ge(val_mm, b + 1)
                        dve.tensor_copy(vals[K:P, b, :, :], ps_v[b % 2][K:P, :, 1, :]).then_inc(val_high, 1)

        xn = m.sb("xn", [P, 2, D])
        xnT = m.sb("xnT", [D, 2, 2 * P], F32R)
        qT = m.sb("qT", [P, HP, 2 * P])
        logits = m.sb("logits", [P, 2, H, K])
        rowmax = m.sb("rowmax", [P, 2, H])
        shifted = m.sb("shifted", [P, 2, H, K])
        probs = m.sb("probs", [P, 2, H, K])
        rowsum = m.sb("rowsum", [P, 2, H])
        rinv = m.sb("rinv", [P, 2, H])
        normed = m.sb("normed", [P, 2, H * K])
        probsT = m.sb("probsT", [P, HP, P])
        oT = m.sb("oT", [P, 2, HP, P])
        ps_m = [m.ps(f"ps_m{n}", [P, 512]) for n in range(2)]
        ps_s = [m.ps(f"ps_s{n}", [P, H, K]) for n in range(2)]
        ps_a = [m.ps(f"ps_a{n}", [P, HP // 2, P]) for n in range(2)]
        xnT_low, counted = m.sem("xnT_low"), m.sem("counted")
        xn_ready, xn_transposed, xnT_ready = m.sem("xn_ready"), m.sem("xn_transposed"), m.sem("xnT_ready")
        q_mm, q_ready = m.sem("q_mm"), m.sem("q_ready")
        kblock_ready, vblock_ready = m.sem("kblock_ready"), m.sem("vblock_ready")
        scored, logits_ready, max_ready = m.sem("scored"), m.sem("logits_ready"), m.sem("max_ready")
        shifted_ready, exp_ready = m.sem("shifted_ready"), m.sem("exp_ready")
        sum_ready, rinv_ready, normed_ready = m.sem("sum_ready"), m.sem("rinv_ready"), m.sem("normed_ready")
        probs_transposed, probsT_ready = m.sem("probs_transposed"), m.sem("probsT_ready")
        attended, oT_ready, projected, x_out = m.sem("attended"), m.sem("oT_ready"), m.sem("projected"), m.sem("x_out")
        QF = HP // 2

        with nc.Block() as block:

            @block.gpsimd
            def _(pool):
                def stage(b):
                    for e in range(2):
                        rows = slice(K * e, K * e + K)
                        pool.tensor_copy(kblock[rows, :, e, :], keys[rows, :, b, :]).then_inc(kblock_ready, 1)

                def stage_values(b):
                    for e in range(2):
                        rows = slice(K * e, K * e + K)
                        pool.tensor_copy(vblock[rows, :, e, :], vals[rows, b, :, :]).then_inc(vblock_ready, 1)

                stage(0)
                stage_values(0)
                with pool.Fori(1, B) as b:
                    pool.wait_ge(scored, 2 * b)
                    stage(b)
                    pool.wait_ge(attended, 4 * b)
                    stage_values(b)

            @block.tensor
            def _(pe):
                def turn_x(b):
                    pe.wait_ge(xn_ready, 2 * b + 2)
                    for u in range(2):
                        mm = pe.transpose(ps_m[0][:, P * u : P * u + P], xn[:, u, :], ident[:, :])
                    mm.then_inc(xn_transposed, 1)

                def queries(b):
                    pe.wait_ge(xnT_low, b + 1)
                    for f in range(QF):
                        if f >= 2:
                            pe.wait_ge(q_ready, QF * b + f - 1)
                        for c in range(2):
                            w = 2 * f + c
                            mm = product(pe, ps_m[(f + 1) % 2][:, 256 * c : 256 * c + 256],
                                         lambda half: wqs[:, half, P * w : P * w + P], lambda half: xnT[:, half, :])
                        mm.then_inc(q_mm, 1)

                def scores(b, u, part):
                    if u == 0 and part == 0:
                        pe.wait_ge(q_ready, QF * b + QF)
                        pe.wait_ge(kblock_ready, 2 * b + 2)
                    for c in range(part * HP // 2, (part + 1) * HP // 2):
                        mm = pe.matmul(ps_s[u][:, 2 * c : 2 * c + 2, :], qT[:, c, P * u : P * u + P], kblock[:, c, :, :],
                                       start=True, stop=True)
                    if part == 1:
                        mm.then_inc(scored, 1)

                def turn_probs(b, u):
                    pe.wait_ge(normed_ready, 2 * b + u + 1)
                    for c in range(HP):
                        mm = pe.transpose(ps_a[c // 4][:, c % 4, :], normed[:, u, P * c : P * c + P], ident[:, :])
                        if c % 4 == 3:
                            mm.then_inc(probs_transposed, 1)

                def attend(b, u):
                    pe.wait_ge(vblock_ready, 2 * b + 2)
                    for n in range(2):
                        pe.wait_ge(probsT_ready, 2 * (2 * b + u) + n + 1)
                        for c in range(4 * n, 4 * n + 4):
                            mm = pe.matmul(ps_a[n][:, c % 4, :], vblock[:, c, :, :], probsT[:, c, :], start=True, stop=True)
                        mm.then_inc(attended, 1)

                def project(b, u):
                    pe.wait_ge(oT_ready, 2 * (2 * b + u) + 2)
                    for c in range(HP):
                        mm = pe.matmul(ps_m[u][:, 0:D], oT[:, u, c, :], wo[:, c, :], start=(c == 0), stop=(c == HP - 1))
                    mm.then_inc(projected, 1)

                turn_x(0)
                queries(0)
                scores(0, 0, 0)
                scores(0, 0, 1)
                turn_x(1)
                scores(0, 1, 0)
                scores(0, 1, 1)

                def batch(b, last):
                    queries(b)
                    turn_probs(b - 1, 0)
                    scores(b, 0, 0)
                    attend(b - 1, 0)
                    scores(b, 0, 1)
                    pe.wait_ge(oT_ready, 4 * b - 2)
                    turn_probs(b - 1, 1)
                    project(b - 1, 0)
                    attend(b - 1, 1)
                    if not last:
                        pe.wait_ge(x_out, 2 * b - 1)
                        turn_x(b + 1)
                    scores(b, 1, 0)
                    project(b - 1, 1)
                    scores(b, 1, 1)
                    pe.wait_ge(oT_ready, 4 * b)
                    pe.wait_ge(x_out, 2 * b)

                with pe.Fori(1, B - 1) as b:
                    batch(b, False)
                batch(B - 1, True)
                turn_probs(B - 1, 0)
                attend(B - 1, 0)
                pe.wait_ge(oT_ready, 4 * B - 2)
                turn_probs(B - 1, 1)
                attend(B - 1, 1)
                project(B - 1, 0)
                project(B - 1, 1)

            @block.scalar
            def _(act):
                def copy_x(b):
                    act.wait_ge(xn_transposed, b + 1)
                    act.activation(xnT[:, 0, :], ps_m[0][:, 0:256], ACT.Copy).then_inc(xnT_ready, 1)

                def copy_q(b, fills):
                    for f in fills:
                        act.wait_ge(q_mm, QF * b + f + 1)
                        act.activation(qT[:, 2 * f : 2 * f + 2, :], ps_m[(f + 1) % 2][:, :].rearrange("p (c j) -> p c j", c=2),
                                       ACT.Copy, scale=SCALE).then_inc(q_ready, 1)

                def exp(b, u):
                    act.wait_ge(shifted_ready, 2 * b + u + 1)
                    act.activation(probs[:, u, :, :], shifted[:, u, :, :], ACT.Exp).then_inc(exp_ready, 1)

                def copy_probs(b, u):
                    for n in range(2):
                        act.wait_ge(probs_transposed, 2 * (2 * b + u) + n + 1)
                        act.activation(probsT[:, 4 * n : 4 * n + 4, :], ps_a[n][:, :, :], ACT.Copy).then_inc(probsT_ready, 1)

                def copy_o(b, u):
                    for n in range(2):
                        act.wait_ge(attended, 2 * (2 * b + u) + n + 1)
                        act.activation(oT[:, u, 4 * n : 4 * n + 4, :], ps_a[n][:, :, :], ACT.Copy).then_inc(oT_ready, 1)

                copy_x(0)
                copy_q(0, range(QF))
                exp(0, 0)
                copy_x(1)

                def batch(b, last):
                    copy_q(b, range(QF))
                    exp(b - 1, 1)
                    copy_probs(b - 1, 0)
                    copy_o(b - 1, 0)
                    copy_probs(b - 1, 1)
                    exp(b, 0)
                    copy_o(b - 1, 1)
                    if not last:
                        copy_x(b + 1)

                with act.Fori(1, B - 1) as b:
                    batch(b, False)
                batch(B - 1, True)
                exp(B - 1, 1)
                copy_probs(B - 1, 0)
                copy_o(B - 1, 0)
                copy_probs(B - 1, 1)
                copy_o(B - 1, 1)

            @block.vector
            def _(dve):
                def norm_x(b):
                    for u in range(2):
                        norm.tile(dve, xn[:, u, :], x, B * u + b).then_inc(xn_ready, 1)

                def shift(b, u):
                    n = 2 * b + u + 1
                    dve.wait_ge(scored, n)
                    dve.tensor_tensor(logits[:, u, :, :], ps_s[u][:, :, :], bcast(mask[:, B * u + b, :], H, 1),
                                      ALU.add).then_inc(logits_ready, 1)
                    dve.wait_ge(logits_ready, n)
                    dve.tensor_reduce(rowmax[:, u, :], logits[:, u, :, :], AX, ALU.max).then_inc(max_ready, 1)
                    dve.wait_ge(max_ready, n)
                    dve.tensor_tensor(shifted[:, u, :, :], logits[:, u, :, :], bcast(rowmax[:, u, :], K, 2),
                                      ALU.subtract).then_inc(shifted_ready, 1)

                def divide(b, u):
                    n = 2 * b + u + 1
                    dve.wait_ge(exp_ready, n)
                    dve.tensor_reduce(rowsum[:, u, :], probs[:, u, :, :], AX, ALU.add).then_inc(sum_ready, 1)
                    dve.wait_ge(sum_ready, n)
                    dve.reciprocal(rinv[:, u, :], rowsum[:, u, :]).then_inc(rinv_ready, 1)
                    dve.wait_ge(rinv_ready, n)
                    dve.tensor_tensor(normed[:, u, :].rearrange("p (h k) -> p h k", h=H), probs[:, u, :, :],
                                      bcast(rinv[:, u, :], K, 2), ALU.mult).then_inc(normed_ready, 1)

                def low_x(b):
                    dve.wait_ge(xnT_ready, b + 1)
                    dve.tensor_tensor(xnT[:, 1, :], ps_m[0][:, 0:256], xnT[:, 0, :], ALU.subtract).then_inc(xnT_low, 1)

                def count(b, u):
                    if stats is not None:
                        dve.wait_ge(x_out, 2 * b + u + 1)
                        dve.bn_stats(stats[:, B * u + b, :], x[:, B * u + b, :]).then_inc(counted, 1)

                def add(b, u):
                    dve.wait_ge(projected, 2 * b + u + 1)
                    t = B * u + b
                    dve.tensor_tensor(x[:, t, :], x[:, t, :], ps_m[u][:, 0:D], ALU.add).then_inc(x_out, 1)

                def batch(b, last):
                    divide(b - 1, 1)
                    if not last:
                        dve.wait_ge(xn_transposed, b + 1)
                        norm_x(b + 1)
                    shift(b, 0)
                    add(b - 1, 0)
                    divide(b, 0)
                    count(b - 1, 0)
                    add(b - 1, 1)
                    if not last:
                        low_x(b + 1)
                    count(b - 1, 1)
                    shift(b, 1)

                norm_x(0)
                low_x(0)
                norm_x(1)
                shift(0, 0)
                low_x(1)
                divide(0, 0)
                shift(0, 1)
                with dve.Fori(1, B - 1) as b:
                    batch(b, False)
                batch(B - 1, True)
                divide(B - 1, 1)
                add(B - 1, 0)
                add(B - 1, 1)
                count(B - 1, 0)
                count(B - 1, 1)
                if stats is not None:
                    dve.wait_ge(counted, NT)
                dve.wait_ge(x_out, 2 * B)


def threshold_experts(nc, x, ident, gw_dram, gb_dram, ew_dram, eb_dram, out_dram, stats=None):
    E, THRESHOLD = 8, 0.1
    with ExitStack() as stack:
        m = Scope(nc, stack, "te")
        gw = m.sb("gate_w", [D, E])
        gb = m.sb("gate_b", [P, E])
        ew = m.sb("expert_w", [D, E * D])
        eb = m.sb("expert_b", [E, D])
        norm = Norm(m, stats)
        xn = m.sb("xn", [P, SUP, D])
        xnT = m.sb("xnT", [D, 2, SUP * P])
        gt = m.sb("gate", [P, 8, SUP, E])
        gs = m.sb("gate_stats", [P, 6, SUP])
        weight = m.sb("weight", [P, 2, SUP, E])
        wT = m.sb("weightT", [E, SUP * P])
        acc = m.sb("acc", [P, 2, SUP, D])
        both = m.sb("both", [P, SUP, D])
        ps_t = m.ps("ps_t", [P, 512])
        ps_l = m.ps("ps_l", [P, 512])
        ps_w = m.ps("ps_w", [P, 512])
        ps_b = m.ps("ps_b", [P, SUP, D])
        ps_e = [m.ps(f"ps_e{n}", [P, E, D]) for n in range(2)]
        loaded, stored = m.sem("loaded"), m.sem("stored")
        xn_ready, xn_transposed, xnT_ready = m.sem("xn_ready"), m.sem("xn_transposed"), m.sem("xnT_ready")
        logits_mm, gate_step, gate_exp, weighted = m.sem("logits_mm"), m.sem("gate_step"), m.sem("gate_exp"), m.sem("weighted")
        expert_mm, acc_step = m.sem("expert_mm"), m.sem("acc_step")
        turned, wT_ready, bias_mm, x_step = m.sem("turned"), m.sem("wT_ready"), m.sem("bias_mm"), m.sem("x_step")
        NLOAD, GSTEPS = 4, 11
        ACCS = E * SUP

        def loop(eng, super_tile):
            with eng.Fori(0, NSUP // 2 - 1) as j:
                for s in range(2):
                    super_tile(2 * j + s, s, False)
            super_tile(NSUP - 2, 0, False)
            super_tile(NSUP - 1, 1, True)

        with nc.Block() as block:

            @block.sync
            def _(sp):
                for dst, src in ((gw, gw_dram), (gb, gb_dram), (ew, ew_dram), (eb, eb_dram)):
                    sp.dma_start(dst[:, :], src).then_inc(loaded, 16)
                out_rows = out_dram.rearrange("b (u p) d -> u p b d", u=2)
                with sp.Fori(0, NSUP // 2) as k:
                    sp.wait_ge(x_step, 3 * k + 4)
                    sp.dma_start(out_rows[0][:, bass.ds(SUP * k, SUP), :], x[:, bass.ds(SUP * k, SUP), :]).then_inc(stored, 16)
                with sp.Fori(0, NSUP // 2) as k:
                    sp.wait_ge(x_step, 3 * k + 3 * (NSUP // 2) + 4)
                    sp.dma_start(out_rows[1][:, bass.ds(SUP * k, SUP), :],
                                 x[:, bass.ds(SUP * k + B, SUP), :]).then_inc(stored, 16)
                sp.wait_ge(stored, 16 * NSUP)

            @block.tensor
            def _(pe):
                pe.wait_ge(loaded, 16 * NLOAD)

                def gate(i, s):
                    pe.wait_ge(xn_ready, SUP * i + SUP)
                    for g in range(SUP):
                        mm = pe.transpose(ps_t[:, P * g : P * g + P], xn[:, g, :], ident[:, :])
                    mm.then_inc(xn_transposed, 1)
                    pe.wait_ge(xnT_ready, i + 1)
                    for g in range(SUP):
                        mm = pe.matmul(ps_l[:, E * g : E * g + E], xnT[:, s, P * g : P * g + P], gw[:, :], start=True, stop=True)
                    mm.then_inc(logits_mm, 1)

                def experts(i, s, g):
                    pe.wait_ge(acc_step, ACCS * i + E * g + 1)
                    for n in range(2):
                        mm = pe.matmul(ps_e[g % 2][:, 4 * n : 4 * n + 4, :], xnT[:, s, P * g : P * g + P],
                                       ew[:, 512 * n : 512 * n + 512], start=True, stop=True)
                    mm.then_inc(expert_mm, 1)

                def super_tile(i, s, last):
                    experts(i, s, 0)
                    experts(i, s, 1)
                    pe.wait_ge(weighted, i + 1)
                    for t in range(SUP):
                        mm = pe.transpose(ps_w[0:E, P * t : P * t + P], weight[:, s, t, :], ident[:, :])
                    mm.then_inc(turned, 1)
                    if not last:
                        gate(i + 1, 1 - s)
                    experts(i, s, 2)
                    pe.wait_ge(wT_ready, i + 1)
                    pe.wait_ge(x_step, 3 * i + 1)
                    for t in range(SUP):
                        mm = pe.matmul(ps_b[:, t, :], wT[:, P * t : P * t + P], eb[:, :], start=True, stop=True)
                    mm.then_inc(bias_mm, 1)
                    experts(i, s, 3)

                gate(0, 0)
                loop(pe, super_tile)

            @block.scalar
            def _(act):
                norm.act(act, ACT.Exp)

                def copy_x(i, s):
                    act.wait_ge(xn_transposed, i + 1)
                    act.activation(xnT[:, s, :], ps_t[:, :], ACT.Copy).then_inc(xnT_ready, 1)

                def exp(i):
                    act.wait_ge(gate_step, GSTEPS * i + 4)
                    act.activation(gt[:, 2, :, :], gt[:, 1, :, :], ACT.Exp).then_inc(gate_exp, 1)

                def super_tile(i, s, last):
                    act.wait_ge(turned, i + 1)
                    act.activation(wT[:, :], ps_w[0:E, :], ACT.Copy).then_inc(wT_ready, 1)
                    if not last:
                        copy_x(i + 1, 1 - s)
                        exp(i + 1)

                copy_x(0, 0)
                exp(0)
                loop(act, super_tile)

            @block.vector
            def _(dve):
                norm.dve(dve, x)
                dve.wait_ge(loaded, 16 * NLOAD)
                dve.sem_inc(acc_step, E + 1)
                dve.sem_inc(x_step, 1)
                dve.sem_inc(gate_step, 1)

                def norm_x(i):
                    for g in range(SUP):
                        norm.tile(dve, xn[:, g, :], x, SUP * i + g).then_inc(xn_ready, 1)

                def gate(i, s):
                    g_ = lambda n: gt[:, n, :, :]
                    done = lambda n: dve.wait_ge(gate_step, GSTEPS * i + n + 1)
                    dve.wait_ge(logits_mm, i + 1)
                    dve.tensor_tensor(g_(0), ps_l[:, 0 : SUP * E].rearrange("p (g e) -> p g e", e=E),
                                      bcast(gb[:, :], SUP, 1), ALU.add).then_inc(gate_step, 1)
                    done(1)
                    dve.tensor_reduce(gs[:, 0, :], g_(0), AX, ALU.max).then_inc(gate_step, 1)
                    done(2)
                    dve.tensor_tensor(g_(1), g_(0), bcast(gs[:, 0, :], E, 2), ALU.subtract).then_inc(gate_step, 1)
                    dve.wait_ge(gate_exp, i + 1)
                    dve.tensor_reduce(gs[:, 1, :], g_(2), AX, ALU.add).then_inc(gate_step, 1)
                    done(4)
                    dve.reciprocal(gs[:, 2, :], gs[:, 1, :]).then_inc(gate_step, 1)
                    done(5)
                    dve.tensor_tensor(g_(3), g_(2), bcast(gs[:, 2, :], E, 2), ALU.mult).then_inc(gate_step, 1)
                    done(6)
                    dve.scalar_tensor_tensor(g_(4), g_(3), THRESHOLD, g_(3), ALU.is_ge, ALU.mult).then_inc(gate_step, 1)
                    done(7)
                    dve.tensor_reduce(gs[:, 3, :], g_(4), AX, ALU.add).then_inc(gate_step, 1)
                    done(8)
                    dve.scalar_tensor_tensor(gs[:, 4, :], gs[:, 3, :], 0.0, gs[:, 3, :], ALU.is_equal, ALU.add).then_inc(gate_step, 1)
                    done(9)
                    dve.reciprocal(gs[:, 5, :], gs[:, 4, :]).then_inc(gate_step, 1)
                    done(10)
                    dve.tensor_tensor(weight[:, s, :, :], g_(4), bcast(gs[:, 5, :], E, 2), ALU.mult).then_inc(weighted, 1)
                    dve.wait_ge(weighted, i + 1)
                    dve.sem_inc(gate_step, 1)

                def accumulate(i, s, g):
                    dve.wait_ge(expert_mm, SUP * i + g + 1)
                    for e in range(E):
                        out, src = acc[:, e % 2, g, :], ps_e[g % 2][:, e, :]
                        if e < 2:
                            op = dve.tensor_scalar(out, src, weight[:, s, g, e : e + 1], None, ALU.mult)
                        else:
                            dve.wait_ge(acc_step, ACCS * i + E * g + e + E)
                            op = dve.scalar_tensor_tensor(out, src, weight[:, s, g, e : e + 1], out, ALU.mult, ALU.add)
                        op.then_inc(acc_step, 1)

                def super_tile(i, s, last):
                    if not last:
                        dve.wait_ge(xn_transposed, i + 1)
                        norm_x(i + 1)
                    dve.wait_ge(x_step, 3 * i + 1)
                    accumulate(i, s, 0)
                    accumulate(i, s, 1)
                    if not last:
                        gate(i + 1, 1 - s)
                    accumulate(i, s, 2)
                    accumulate(i, s, 3)
                    dve.wait_ge(acc_step, ACCS * i + ACCS + E + 1)
                    dve.tensor_tensor(both[:, :, :], acc[:, 0, :, :], acc[:, 1, :, :], ALU.add).then_inc(x_step, 1)
                    dve.wait_ge(x_step, 3 * i + 2)
                    dve.wait_ge(bias_mm, i + 1)
                    dve.tensor_tensor(acc[:, 0, :, :], both[:, :, :], ps_b[:, :, :], ALU.add).then_inc(x_step, 1)
                    dve.wait_ge(x_step, 3 * i + 3)
                    view = x[:, bass.ds(SUP * i, SUP), :]
                    dve.tensor_tensor(view, view, acc[:, 0, :, :], ALU.add).then_inc(x_step, 1)

                norm_x(0)
                gate(0, 0)
                loop(dve, super_tile)
                dve.wait_ge(x_step, 3 * NSUP + 1)


def decoder(nc, a, x1_dram, out_dram):
    take = lambda *names: [a[n] for n in names]
    with ExitStack() as stack:
        m = Scope(nc, stack, "g")
        x = m.sb("x", [P, NT, D])
        ident = m.sb("ident", [P, P])
        stats = m.sb("stats", [P, NT, 6])
        with ExitStack() as inner:
            bias = Scope(nc, inner, "gb").sb("bias", [P, NT, 64])
            self_attention(nc, x, ident, *take("x", "ident", "sa_mask", "sa_wq", "sa_wkv", "sa_bq", "sa_bk", "sa_bv", "sa_wp", "sa_bp"),
                           x1_dram, *take("idx", "bins"), bias)
            load_x(nc, x, ident, x1_dram, a["ident"])
            gathered_attention(nc, x, bias, ident, *take("ctxT", "ga_downT", "ga_upT", "ga_qT", "ga_outT", "ga_hmask", "ga_pmask"))
        gated_experts(nc, x, ident, *take("ge_scale", "ge_bias", "ge_gateT", "ge_wg", "ge_wu", "ge_wd", "ge_order"), stats)
        dirs = [dict({n[2:]: v for n, v in a.items() if n[:2] == d + "_"}, pick=a["pick"]) for d in "fb"]
        state_space(nc, x, ident, dirs, stats)
        cross_attention(nc, x, ident, *take("ctxT", "ctx2T", "xa_mask", "xa_wq", "xa_wk", "xa_wv", "xa_wo"), stats)
        threshold_experts(nc, x, ident, *take("te_gw", "te_gb", "te_ew", "te_eb"), out_dram, stats)


def kernel(**inp):
    import numpy as np
    import concourse.bacc as bacc
    from concourse.bass_utils import run_bass_kernel_spmd as run

    c = np.ascontiguousarray
    rows = lambda v: c(np.broadcast_to(v[None], (P,) + v.shape))
    cols = lambda v: c(v.reshape(-1, P).T)
    K = 64
    k = np.arange(P)
    pick = np.zeros((P, P), np.float32)
    pick[64 + np.arange(64), np.arange(64)] = 1.0
    ctxT = c(inp["ctx_1024"].reshape(B * K, D).T)
    tiles = lambda v: c(v.reshape(B, 2, P, K).transpose(2, 1, 0, 3))
    arr = {
        "x": c(inp["x"].transpose(1, 0, 2).reshape(TOK, D)),
        "ident": np.eye(P, dtype=np.float32), "pick": pick,
        "sa_mask": np.where((k[:, None] // B) % 2 == np.arange(32)[None] // B, 0.0, -1e30).astype(np.float32),
        "sa_wq": inp["L0_attn_Wq"], "sa_wkv": inp["L0_attn_Wkv"], "sa_bq": cols(inp["L0_attn_bq"]),
        "sa_bk": cols(inp["L0_attn_bkv"][:1024]), "sa_bv": cols(inp["L0_attn_bkv"][1024:]),
        "sa_wp": inp["L0_attn_Wp"], "sa_bp": inp["L0_attn_bp"].reshape(1, D),
        "idx": tiles(inp["itok_BxSx64_0_2047"]).reshape(P, NT * K), "bins": rows(np.arange(K, dtype=np.float32)),
        "ctxT": ctxT, "ctx2T": c(np.broadcast_to(ctxT.reshape(D, B, 1, K), (D, B, 2, K)).reshape(D, B, 2 * K)),
        "ga_downT": c(inp["L0_xattn_W_kv_down"].T), "ga_upT": c(inp["L0_xattn_W_kv_up"].T),
        "ga_qT": c(inp["L0_xattn_W_q"].T), "ga_outT": c(inp["L0_xattn_W_out"].T),
        "ga_hmask": (k[:, None] // 8 == np.arange(16)[None]).astype(np.float32),
        "ga_pmask": (k[:, None] // 64 == np.arange(2)[None]).astype(np.float32),
        "ge_scale": c(inp["L0_ffn_ln_scale"].reshape(D, 1)), "ge_bias": c(inp["L0_ffn_ln_bias"].reshape(D, 1)),
        "ge_gateT": c(inp["L0_ffn_gate_w"].T),
        "ge_wg": c(np.concatenate([inp["L0_ffn_sWg"][None], inp["L0_ffn_Wg"]]).transpose(1, 0, 2)),
        "ge_wu": c(np.concatenate([inp["L0_ffn_sWu"][None], inp["L0_ffn_Wu"]]).transpose(1, 0, 2)),
        "ge_wd": c(np.concatenate([inp["L0_ffn_sWd"][None], inp["L0_ffn_Wd"]]).reshape(9, 2, P, D).transpose(2, 0, 1, 3)),
        "ge_order": rows(np.arange(8, 0, -1, dtype=np.float32)),
        "f_strict": (k[:, None] > k[None]).astype(np.float32), "b_strict": (k[:, None] < k[None]).astype(np.float32),
        "f_inclusive": (k[:, None] <= k[None]).astype(np.float32), "b_inclusive": (k[:, None] >= k[None]).astype(np.float32),
        "xa_mask": tiles(inp["mask_Bx1xSxS2_fk1"]).reshape(P, NT, K),
        "xa_wq": inp["L1_xattn_W_q"], "xa_wk": inp["L1_xattn_W_k"], "xa_wv": inp["L1_xattn_W_v"], "xa_wo": inp["L1_xattn_W_o"],
        "te_gw": inp["L1_ffn_gate_w"], "te_gb": rows(inp["L1_ffn_gate_b"]),
        "te_ew": c(inp["L1_ffn_expert_w"].transpose(1, 0, 2).reshape(D, 8 * D)), "te_eb": inp["L1_ffn_expert_b"],
    }
    for d in "fb":
        g = lambda n: inp[f"L1_attn_{d}_{n}"]
        arr.update({
            f"{d}_in": c(g("in_w").T), f"{d}_conv_w": c(g("conv_w").reshape(3, P, 4).transpose(1, 0, 2)),
            f"{d}_conv_b": cols(g("conv_b")), f"{d}_dt_bias": rows(g("dt_bias")), f"{d}_a_log": rows(g("A_log")),
            f"{d}_dp": rows(g("Dp")), f"{d}_norm_w": cols(g("norm_w")),
            f"{d}_out_w": c(g("out_w").T.reshape(2, P, D).transpose(1, 0, 2)),
        })
    nc = bacc.Bacc("TRN2", target_bir_lowering=False, num_devices=1)
    a = {n: nc.dram_tensor(f"in_{n}", v.shape, mybir.dt.from_np(v.dtype), kind="ExternalInput").ap() for n, v in arr.items()}
    x1 = nc.dram_tensor("x1", (TOK, D), F32, kind="Internal").ap()
    out = nc.dram_tensor("out", (B, S, D), F32, kind="ExternalOutput").ap()
    decoder(nc, a, x1, out)
    return run(nc, [{f"in_{n}": v for n, v in arr.items()}], core_ids=[0]).results[0]["out"]
```
